# Optimizing a Trainium2 kernel written in Bass

```python
import numpy as np
import jax
import jax.numpy as jnp

def _softmax(x, axis=-1):
    return jax.nn.softmax(x, axis=axis)

def _gelu(x):
    return jax.nn.gelu(x, approximate=True)

def _silu(x):
    return jax.nn.silu(x)

def _sigmoid(x):
    return jax.nn.sigmoid(x)

def _layernorm(x, axis=-1, eps=1e-05):
    m = jnp.mean(x, axis=axis, keepdims=True)
    v = jnp.var(x, axis=axis, keepdims=True)
    return (x - m) / jnp.sqrt(v + eps)

def _scatter_add(tgt, idx, src, axis=0):
    return tgt.at[idx].add(src)

def _segment_sum(src, seg, n):
    return jax.ops.segment_sum(src, seg, n)
kernel_name = 'mk_decoder_preln_d4_seqx_r8_377e0e'

def setup_inputs(seed: int=0):
    np.random.seed(seed)
    _w = jnp.asarray

    def _rec_inputs():
        import jax
        import jax.numpy as jnp
        _rk = jax.random.key(seed)
        x = 7.22e-05 + 1 * jax.random.normal(jax.random.fold_in(_rk, 1), (2, 512, 128), jnp.float32)
        _lenS = 512 - jax.random.randint(jax.random.fold_in(_rk, 7), (2,), 0, max(1, 512 // 4) + 1, jnp.int32)
        _lenS2 = 77 - jax.random.randint(jax.random.fold_in(_rk, 8), (2,), 0, max(1, 77 // 4) + 1, jnp.int32)
        _ctx_1024P = jax.random.normal(jax.random.fold_in(_rk, 11), (2, 16, 128), jnp.float32)
        _ctx_1024c = jax.random.dirichlet(jax.random.fold_in(_rk, 511), 0.3 * jnp.ones((16,), jnp.float32), (2, 77))
        _ctx_1024t = jnp.einsum('bsk,bkd->bsd', _ctx_1024c, _ctx_1024P)
        _ctx_1024t = _ctx_1024t * jax.lax.rsqrt(jnp.mean(jnp.square(_ctx_1024t)) + 1e-12) * 0.953939
        ctx_1024 = 4.13588e-05 + 0.999923 * (_ctx_1024t + 0.3 * jax.random.normal(jax.random.fold_in(_rk, 611), (2, 77, 128), jnp.float32))
        _validS = jnp.arange(512)[None, :] < _lenS[:, None]
        _validS2 = jnp.arange(77)[None, :] < _lenS2[:, None]
        _causal = jnp.tril(jnp.ones((512, 512), dtype=bool))
        mask_BxSxS2_ik1 = jnp.where(jnp.broadcast_to(_validS2[:, None, :], (2, 512, 77)), 1, 0).astype(jnp.int32)
        mask_Bx1xSxS2_ik1 = jnp.where(jnp.broadcast_to(_validS2[:, None, None, :], (2, 1, 512, 77)), 1, 0).astype(jnp.int32)
        mask_BxS_bf1 = jnp.ones((2, 512), dtype=bool)
        return (x, ctx_1024, mask_BxSxS2_ik1, mask_Bx1xSxS2_ik1, mask_BxS_bf1)
    x, ctx_1024, mask_BxSxS2_ik1, mask_Bx1xSxS2_ik1, mask_BxS_bf1 = _rec_inputs()

    def _L0_attn_setup():
        import jax, jax.numpy as jnp
        import numpy as np
        import math
        N_EMBD = 128
        N_HEAD = 16
        N_LAYER = 12
        key = jax.random.key(seed)
        kx, kw, kb = jax.random.split(key, 3)
        B, T, C = (4, 256, N_EMBD)
        x = jax.random.normal(kx, (B, T, C), dtype=jnp.float32)
        bound = 1.0 / math.sqrt(C)
        W = jax.random.uniform(kw, (3 * C, C), minval=-bound, maxval=bound, dtype=jnp.float32)
        W = W * (1.0 / math.sqrt(N_LAYER * 2))
        b = jax.random.uniform(kb, (3 * C,), minval=-bound, maxval=bound, dtype=jnp.float32)
        return {'x': x, 'W': W, 'b': b}
    _L0_attn_all = _L0_attn_setup()
    _L0_attn_in = {k: v for k, v in _L0_attn_all.items() if k in ('W', 'b')}
    del _L0_attn_all

    def _L0_xattn_setup():
        import jax, jax.numpy as jnp
        import numpy as np
        NEG = -9000000000000000.0
        EPS = 1e-05
        key = jax.random.key(seed)
        k1, k2, k3, k4 = jax.random.split(key, 4)
        B, S, D = (4, 256, 128)
        q = jax.random.normal(k1, (B, S, D), dtype=jnp.float32)
        k = jax.random.normal(k2, (B, S, D), dtype=jnp.float32)
        v = jax.random.normal(k3, (B, S, D), dtype=jnp.float32)
        mask = jax.random.randint(k4, (B, S, S), 0, 2, dtype=jnp.int32)
        gamma = jnp.ones((D,), dtype=jnp.float32)
        beta = jnp.zeros((D,), dtype=jnp.float32)
        return {'q': q, 'k': k, 'v': v, 'mask': mask, 'gamma': gamma, 'beta': beta}
    _L0_xattn_all = _L0_xattn_setup()
    _L0_xattn_in = {k: v for k, v in _L0_xattn_all.items() if k in ('gamma', 'beta')}
    del _L0_xattn_all

    def _L0_ffn_setup():
        import jax, jax.numpy as jnp
        import numpy as np
        B, T, C = (4, 1024, 128)
        E, I, IS, K = (8, 128, 32, 6)
        key = jax.random.key(seed)
        ks = jax.random.split(key, 8)
        s = 0.02
        return {'x': jax.random.normal(ks[0], (B, T, C), dtype=jnp.float32), 'w1': jax.random.normal(ks[1], (E, C, I), dtype=jnp.float32) * s, 'w2': jax.random.normal(ks[2], (E, C, I), dtype=jnp.float32) * s, 'w3': jax.random.normal(ks[3], (E, I, C), dtype=jnp.float32) * s, 'ws1': jax.random.normal(ks[4], (C, IS), dtype=jnp.float32) * s, 'ws2': jax.random.normal(ks[5], (C, IS), dtype=jnp.float32) * s, 'ws3': jax.random.normal(ks[6], (IS, C), dtype=jnp.float32) * s, 'wr': jax.random.normal(ks[7], (C, E), dtype=jnp.float32) * s}
    _L0_ffn_all = _L0_ffn_setup()
    _L0_ffn_in = {k: v for k, v in _L0_ffn_all.items() if k in ('w1', 'w2', 'w3', 'ws1', 'ws2', 'ws3', 'wr')}
    del _L0_ffn_all

    def _L1_attn_setup():
        import jax, jax.numpy as jnp
        import numpy as np
        import math
        EMBED_DIM = 128
        NUM_HEADS = 16
        HEAD_DIM = EMBED_DIM // NUM_HEADS
        MAX_POS = 64
        SPARSE_TOPK = 32
        B, T = (8, 64)
        key = jax.random.key(seed)
        ks = jax.random.split(key, 12)
        s = 1.0 / math.sqrt(EMBED_DIM)
        inp = {'x': jax.random.normal(ks[0], (B, T, EMBED_DIM), dtype=jnp.float32), 'Wq': jax.random.uniform(ks[1], (EMBED_DIM, EMBED_DIM), jnp.float32, -s, s), 'bq': jax.random.uniform(ks[2], (EMBED_DIM,), jnp.float32, -s, s), 'Wk': jax.random.uniform(ks[3], (EMBED_DIM, EMBED_DIM), jnp.float32, -s, s), 'bk': jax.random.uniform(ks[4], (EMBED_DIM,), jnp.float32, -s, s), 'Wv': jax.random.uniform(ks[5], (EMBED_DIM, EMBED_DIM), jnp.float32, -s, s), 'bv': jax.random.uniform(ks[6], (EMBED_DIM,), jnp.float32, -s, s), 'Wo': jax.random.uniform(ks[7], (EMBED_DIM, EMBED_DIM), jnp.float32, -s, s), 'bo': jax.random.uniform(ks[8], (EMBED_DIM,), jnp.float32, -s, s), 'head_gates': jnp.ones((NUM_HEADS,), dtype=jnp.float32), 'rel_bias': 0.02 * jax.random.normal(ks[9], (2 * MAX_POS - 1, NUM_HEADS), dtype=jnp.float32)}
        return inp
    _L1_attn_all = _L1_attn_setup()
    _L1_attn_in = {k: v for k, v in _L1_attn_all.items() if k in ('Wq', 'bq', 'Wk', 'bk', 'Wv', 'bv', 'Wo', 'bo', 'head_gates', 'rel_bias')}
    del _L1_attn_all

    def _L1_xattn_setup():
        import jax, jax.numpy as jnp
        import numpy as np
        D_MODEL = 128
        H = 16
        D_K = D_MODEL // H
        NEG = -100000000000.0

        def _split_heads(x):
            B, N, _ = x.shape
            return x.reshape(B, N, H, D_K).transpose(0, 2, 1, 3)
        key = jax.random.key(seed)
        ks = jax.random.split(key, 12)
        B, N, D = (4, 256, D_MODEL)
        s = 1.0 / np.sqrt(D)
        return {'query': jax.random.normal(ks[0], (B, N, D), jnp.float32), 'key': jax.random.normal(ks[1], (B, N, D), jnp.float32), 'value': jax.random.normal(ks[2], (B, N, D), jnp.float32), 'mask': jax.random.randint(ks[3], (B, 1, N, N), 0, 2, jnp.int32), 'Wq': jax.random.normal(ks[4], (D, D_MODEL), jnp.float32) * s, 'bq': jnp.zeros((D_MODEL,), jnp.float32), 'Wk': jax.random.normal(ks[5], (D, D_MODEL), jnp.float32) * s, 'bk': jnp.zeros((D_MODEL,), jnp.float32), 'Wv': jax.random.normal(ks[6], (D, D_MODEL), jnp.float32) * s, 'bv': jnp.zeros((D_MODEL,), jnp.float32), 'Wo': jax.random.normal(ks[7], (D_MODEL, D_MODEL), jnp.float32) * s, 'bo': jnp.zeros((D_MODEL,), jnp.float32)}
    _L1_xattn_all = _L1_xattn_setup()
    _L1_xattn_in = {k: v for k, v in _L1_xattn_all.items() if k in ('Wq', 'bq', 'Wk', 'bk', 'Wv', 'bv', 'Wo', 'bo')}
    del _L1_xattn_all

    def _L1_ffn_setup():
        import jax, jax.numpy as jnp
        import numpy as np
        D_MODEL, D_FF, N_EXPERTS, TOP_K = (128, 512, 8, 2)
        B, S = (2, 256)
        key = jax.random.key(seed)
        ks = jax.random.split(key, 7)
        scale = 0.02
        return {'x': jax.random.normal(ks[0], (B, S, D_MODEL), dtype=jnp.float32), 'W1': jax.random.normal(ks[1], (N_EXPERTS, D_MODEL, D_FF), dtype=jnp.float32) * scale, 'b1': jnp.zeros((N_EXPERTS, D_FF), dtype=jnp.float32), 'W2': jax.random.normal(ks[2], (N_EXPERTS, D_FF, D_MODEL), dtype=jnp.float32) * scale, 'b2': jnp.zeros((N_EXPERTS, D_MODEL), dtype=jnp.float32), 'Wg': jax.random.normal(ks[3], (D_MODEL, N_EXPERTS), dtype=jnp.float32) * scale, 'bg': jnp.zeros((N_EXPERTS,), dtype=jnp.float32)}
    _L1_ffn_all = _L1_ffn_setup()
    _L1_ffn_in = {k: v for k, v in _L1_ffn_all.items() if k in ('W1', 'b1', 'W2', 'b2', 'Wg', 'bg')}
    del _L1_ffn_all

    def _L2_attn_setup():
        import jax, jax.numpy as jnp
        import numpy as np

        def log_g(x):
            pos = jnp.log(jnp.maximum(x, 0.0) + 0.5)
            neg = -jax.nn.softplus(-x)
            return jnp.where(x >= 0, pos, neg)

        def parallel_scan_log(log_coeffs, log_values):
            a_star = jnp.cumsum(log_coeffs, axis=1)
            log_h0_plus_b_star = jax.lax.cumlogsumexp(log_values - a_star, axis=1)
            log_h = a_star + log_h0_plus_b_star
            return jnp.exp(log_h)
        key = jax.random.key(seed)
        k1, k2 = jax.random.split(key)
        B, S, D = (8, 512, 128)
        x = jax.random.normal(k1, (B, S, D), dtype=jnp.float32)
        W_hg = jax.random.normal(k2, (2 * D, D), dtype=jnp.float32) * (1.0 / np.sqrt(D))
        return {'x': x, 'W_hg': W_hg}
    _L2_attn_all = _L2_attn_setup()
    _L2_attn_in = {k: v for k, v in _L2_attn_all.items() if k in ('W_hg',)}
    del _L2_attn_all

    def _L2_xattn_setup():
        import jax, jax.numpy as jnp
        import numpy as np
        L = 2
        D = 128
        HS = 128
        NH = 16
        DH = 64
        FF = 512
        ROT = 32
        B, SQ, SK = (64, 128, 64)
        EPS = 1e-08

        def rmsnorm(x, w):
            norm = jnp.sqrt(jnp.sum(x * x, axis=-1, keepdims=True)) * x.shape[-1] ** (-0.5)
            return x / jnp.maximum(norm, EPS) * w

        def rope_freqs(n):
            inv_freq = 1.0 / 10000.0 ** (jnp.arange(0, ROT, 2, dtype=jnp.float32) / ROT)
            f = jnp.arange(n, dtype=jnp.float32)[:, None] * inv_freq[None, :]
            return jnp.concatenate([f, f], axis=-1)[None, None]

        def apply_rope(t, freqs):
            rd = freqs.shape[-1]
            t1, tp = (t[..., :rd], t[..., rd:])
            half = rd // 2
            a, b = (t1[..., :half], t1[..., half:])
            rot = jnp.concatenate([-b, a], axis=-1)
            t1 = t1 * jnp.cos(freqs) + rot * jnp.sin(freqs)
            return jnp.concatenate([t1, tp], axis=-1)

        def attention(x, ctx, Wq, Wk, Wv, Wo, bo, pe_q, pe_k, mask):
            b, n, _ = x.shape
            m = ctx.shape[1]
            q = (x @ Wq).reshape(b, n, NH, DH).transpose(0, 2, 1, 3) * DH ** (-0.5)
            k = (ctx @ Wk).reshape(b, m, NH, DH).transpose(0, 2, 1, 3)
            v = (ctx @ Wv).reshape(b, m, NH, DH).transpose(0, 2, 1, 3)
            q = apply_rope(q, pe_q)
            k = apply_rope(k, pe_k)
            sim = jnp.einsum('bhid,bhjd->bhij', q, k)
            if mask is not None:
                sim = jnp.where(mask[:, None, None, :], sim, -jnp.finfo(sim.dtype).max)
            attn = jax.nn.softmax(sim, axis=-1)
            out = jnp.einsum('bhij,bhjd->bhid', attn, v)
            out = out.transpose(0, 2, 1, 3).reshape(b, n, NH * DH)
            return out @ Wo + bo
        key = jax.random.key(seed)
        ks = jax.random.split(key, 24)
        s = 0.02
        inp = {'x': jax.random.normal(ks[0], (B, SQ, D), jnp.float32), 'chunked_seq': jax.random.normal(ks[1], (B, SK, HS), jnp.float32), 'mask': jnp.ones((B, SQ), dtype=bool), 'attn_norm_w': jnp.ones((L, D), jnp.float32), 'Wq': jax.random.normal(ks[2], (L, D, NH * DH), jnp.float32) * s, 'Wk': jax.random.normal(ks[3], (L, D, NH * DH), jnp.float32) * s, 'Wv': jax.random.normal(ks[4], (L, D, NH * DH), jnp.float32) * s, 'Wo': jax.random.normal(ks[5], (L, NH * DH, D), jnp.float32) * s, 'bo': jnp.zeros((L, D), jnp.float32), 'cross_norm_w': jnp.ones((L, D), jnp.float32), 'cWq': jax.random.normal(ks[6], (L, D, NH * DH), jnp.float32) * s, 'cWk': jax.random.normal(ks[7], (HS, NH * DH), jnp.float32) * s if False else jax.random.normal(ks[7], (L, HS, NH * DH), jnp.float32) * s, 'cWv': jax.random.normal(ks[8], (L, HS, NH * DH), jnp.float32) * s, 'cWo': jax.random.normal(ks[9], (L, NH * DH, D), jnp.float32) * s, 'cbo': jnp.zeros((L, D), jnp.float32), 'ff_norm_w': jnp.ones((L, D), jnp.float32), 'ff_w1': jax.random.normal(ks[10], (L, D, FF), jnp.float32) * s, 'ff_b1': jnp.zeros((L, FF), jnp.float32), 'ff_w2': jax.random.normal(ks[11], (L, FF, D), jnp.float32) * s, 'ff_b2': jnp.zeros((L, D), jnp.float32), 'norm_out_w': jnp.ones((D,), jnp.float32), 'proj_w': jax.random.normal(ks[12], (D, HS), jnp.float32) * s, 'proj_b': jnp.zeros((HS,), jnp.float32)}
        return inp
    _L2_xattn_all = _L2_xattn_setup()
    _L2_xattn_in = {k: v for k, v in _L2_xattn_all.items() if k in ('attn_norm_w', 'Wq', 'Wk', 'Wv', 'Wo', 'bo', 'cross_norm_w', 'cWq', 'cWk', 'cWv', 'cWo', 'cbo', 'ff_norm_w', 'ff_w1', 'ff_b1', 'ff_w2', 'ff_b2', 'norm_out_w', 'proj_w', 'proj_b')}
    del _L2_xattn_all

    def _L2_ffn_setup():
        import jax, jax.numpy as jnp
        import numpy as np
        EPS = 1e-05

        def rmsnorm(x):
            return x * jax.lax.rsqrt(jnp.mean(x * x, axis=-1, keepdims=True) + EPS)

        def act_quant(x):
            scale = 127.0 / jnp.clip(jnp.max(jnp.abs(x), axis=-1, keepdims=True), 1e-05)
            q = jnp.clip(jnp.round(x * scale), -128.0, 127.0) / scale
            return x + jax.lax.stop_gradient(q - x)

        def weight_quant(w):
            scale = 1.0 / jnp.clip(jnp.mean(jnp.abs(w)), 1e-05)
            q = jnp.clip(jnp.round(w * scale), -1.0, 1.0) / scale
            return w + jax.lax.stop_gradient(q - w)

        def bitlinear(x, w, b):
            xq = act_quant(rmsnorm(x))
            wq = weight_quant(w)
            return jnp.einsum('bsd,fd->bsf', xq, wq) + b
        key = jax.random.key(seed)
        k0, k1, k2 = jax.random.split(key, 3)
        B, S, D, F = (2, 1024, 128, 512)
        x = jax.random.normal(k0, (B, S, D), dtype=jnp.float32)
        w1 = jax.random.normal(k1, (F, D), dtype=jnp.float32) * (1.0 / np.sqrt(D))
        b1 = jnp.zeros((F,), dtype=jnp.float32)
        w2 = jax.random.normal(k2, (D, F), dtype=jnp.float32) * (1.0 / np.sqrt(F))
        b2 = jnp.zeros((D,), dtype=jnp.float32)
        return {'x': x, 'w1': w1, 'b1': b1, 'w2': w2, 'b2': b2}
    _L2_ffn_all = _L2_ffn_setup()
    _L2_ffn_in = {k: v for k, v in _L2_ffn_all.items() if k in ('w1', 'b1', 'w2', 'b2')}
    del _L2_ffn_all

    def _L3_attn_setup():
        import jax, jax.numpy as jnp
        import numpy as np
        key = jax.random.key(seed)
        ks = jax.random.split(key, 6)
        B, T, D, N = (8, 512, 128, 16)
        s = 0.02
        return {'x': jax.random.normal(ks[0], (B, T, D), jnp.float32), 'Wd': jax.random.normal(ks[1], (D, D), jnp.float32) * s, 'bd': jnp.zeros((D,), jnp.float32), 'Wb': jax.random.normal(ks[2], (D, N), jnp.float32) * s, 'bb': jnp.zeros((N,), jnp.float32), 'Wc': jax.random.normal(ks[3], (D, N), jnp.float32) * s, 'bc': jnp.zeros((N,), jnp.float32), 'Wo': jax.random.normal(ks[4], (D, D), jnp.float32) * s, 'bo': jnp.zeros((D,), jnp.float32), 'A': jax.random.normal(ks[5], (D, N), jnp.float32) * 0.01}
    _L3_attn_all = _L3_attn_setup()
    _L3_attn_in = {k: v for k, v in _L3_attn_all.items() if k in ('Wd', 'bd', 'Wb', 'bb', 'Wc', 'bc', 'Wo', 'bo', 'A')}
    del _L3_attn_all

    def _L3_xattn_setup():
        import jax, jax.numpy as jnp
        import numpy as np
        B, SQ, SKV, E, H = (4, 256, 256, 128, 16)
        HD = E // H

        def stablemax(x):
            s = jnp.where(x >= 0, x + 1.0, 1.0 / (1.0 - x))
            return s / jnp.sum(s, axis=-1, keepdims=True)
        key = jax.random.key(seed)
        ks = jax.random.split(key, 6)
        scale = 1.0 / np.sqrt(E)
        return {'query': jax.random.normal(ks[0], (B, SQ, E), jnp.float32), 'key_value': jax.random.normal(ks[1], (B, SKV, E), jnp.float32), 'Wq': jax.random.normal(ks[2], (E, E), jnp.float32) * scale, 'bq': jnp.zeros((E,), jnp.float32), 'Wk': jax.random.normal(ks[3], (E, E), jnp.float32) * scale, 'bk': jnp.zeros((E,), jnp.float32), 'Wv': jax.random.normal(ks[4], (E, E), jnp.float32) * scale, 'bv': jnp.zeros((E,), jnp.float32), 'Wo': jax.random.normal(ks[5], (E, E), jnp.float32) * scale, 'bo': jnp.zeros((E,), jnp.float32)}
    _L3_xattn_all = _L3_xattn_setup()
    _L3_xattn_in = {k: v for k, v in _L3_xattn_all.items() if k in ('Wq', 'bq', 'Wk', 'bk', 'Wv', 'bv', 'Wo', 'bo')}
    del _L3_xattn_all

    def _L3_ffn_setup():
        import jax, jax.numpy as jnp
        import numpy as np
        D_MODEL = 128
        HIDDEN = 512
        NUM_EXPERTS = 8
        TOP_K = 2
        key = jax.random.key(seed)
        k_x, k_g, k_in, k_out = jax.random.split(key, 4)
        bound_in = 1.0 / HIDDEN
        bound_out = 1.0 / D_MODEL
        x = jax.random.normal(k_x, (2, 256, D_MODEL), dtype=jnp.float32)
        w_gate = jax.random.uniform(k_g, (NUM_EXPERTS, D_MODEL), dtype=jnp.float32, minval=-D_MODEL ** (-0.5), maxval=D_MODEL ** (-0.5))
        w_in = jax.random.uniform(k_in, (NUM_EXPERTS, HIDDEN, D_MODEL), dtype=jnp.float32, minval=-bound_in, maxval=bound_in)
        w_out = jax.random.uniform(k_out, (NUM_EXPERTS, D_MODEL, HIDDEN), dtype=jnp.float32, minval=-bound_out, maxval=bound_out)
        return {'x': x, 'w_gate': w_gate, 'w_in': w_in, 'w_out': w_out}
    _L3_ffn_all = _L3_ffn_setup()
    _L3_ffn_in = {k: v for k, v in _L3_ffn_all.items() if k in ('w_gate', 'w_in', 'w_out')}
    del _L3_ffn_all
    return {'x': x, 'ctx_1024': ctx_1024, 'mask_BxSxS2_ik1': mask_BxSxS2_ik1, 'mask_Bx1xSxS2_ik1': mask_Bx1xSxS2_ik1, 'mask_BxS_bf1': mask_BxS_bf1, 'L0_attn_W': _L0_attn_in['W'], 'L0_attn_b': _L0_attn_in['b'], 'L0_xattn_gamma': _L0_xattn_in['gamma'], 'L0_xattn_beta': _L0_xattn_in['beta'], 'L0_ffn_w1': _L0_ffn_in['w1'], 'L0_ffn_w2': _L0_ffn_in['w2'], 'L0_ffn_w3': _L0_ffn_in['w3'], 'L0_ffn_ws1': _L0_ffn_in['ws1'], 'L0_ffn_ws2': _L0_ffn_in['ws2'], 'L0_ffn_ws3': _L0_ffn_in['ws3'], 'L0_ffn_wr': _L0_ffn_in['wr'], 'L1_attn_Wq': _L1_attn_in['Wq'], 'L1_attn_bq': _L1_attn_in['bq'], 'L1_attn_Wk': _L1_attn_in['Wk'], 'L1_attn_bk': _L1_attn_in['bk'], 'L1_attn_Wv': _L1_attn_in['Wv'], 'L1_attn_bv': _L1_attn_in['bv'], 'L1_attn_Wo': _L1_attn_in['Wo'], 'L1_attn_bo': _L1_attn_in['bo'], 'L1_attn_head_gates': _L1_attn_in['head_gates'], 'L1_attn_rel_bias': _L1_attn_in['rel_bias'], 'L1_xattn_Wq': _L1_xattn_in['Wq'], 'L1_xattn_bq': _L1_xattn_in['bq'], 'L1_xattn_Wk': _L1_xattn_in['Wk'], 'L1_xattn_bk': _L1_xattn_in['bk'], 'L1_xattn_Wv': _L1_xattn_in['Wv'], 'L1_xattn_bv': _L1_xattn_in['bv'], 'L1_xattn_Wo': _L1_xattn_in['Wo'], 'L1_xattn_bo': _L1_xattn_in['bo'], 'L1_ffn_W1': _L1_ffn_in['W1'], 'L1_ffn_b1': _L1_ffn_in['b1'], 'L1_ffn_W2': _L1_ffn_in['W2'], 'L1_ffn_b2': _L1_ffn_in['b2'], 'L1_ffn_Wg': _L1_ffn_in['Wg'], 'L1_ffn_bg': _L1_ffn_in['bg'], 'L2_attn_W_hg': _L2_attn_in['W_hg'], 'L2_xattn_attn_norm_w': _L2_xattn_in['attn_norm_w'], 'L2_xattn_Wq': _L2_xattn_in['Wq'], 'L2_xattn_Wk': _L2_xattn_in['Wk'], 'L2_xattn_Wv': _L2_xattn_in['Wv'], 'L2_xattn_Wo': _L2_xattn_in['Wo'], 'L2_xattn_bo': _L2_xattn_in['bo'], 'L2_xattn_cross_norm_w': _L2_xattn_in['cross_norm_w'], 'L2_xattn_cWq': _L2_xattn_in['cWq'], 'L2_xattn_cWk': _L2_xattn_in['cWk'], 'L2_xattn_cWv': _L2_xattn_in['cWv'], 'L2_xattn_cWo': _L2_xattn_in['cWo'], 'L2_xattn_cbo': _L2_xattn_in['cbo'], 'L2_xattn_ff_norm_w': _L2_xattn_in['ff_norm_w'], 'L2_xattn_ff_w1': _L2_xattn_in['ff_w1'], 'L2_xattn_ff_b1': _L2_xattn_in['ff_b1'], 'L2_xattn_ff_w2': _L2_xattn_in['ff_w2'], 'L2_xattn_ff_b2': _L2_xattn_in['ff_b2'], 'L2_xattn_norm_out_w': _L2_xattn_in['norm_out_w'], 'L2_xattn_proj_w': _L2_xattn_in['proj_w'], 'L2_xattn_proj_b': _L2_xattn_in['proj_b'], 'L2_ffn_w1': _L2_ffn_in['w1'], 'L2_ffn_b1': _L2_ffn_in['b1'], 'L2_ffn_w2': _L2_ffn_in['w2'], 'L2_ffn_b2': _L2_ffn_in['b2'], 'L3_attn_Wd': _L3_attn_in['Wd'], 'L3_attn_bd': _L3_attn_in['bd'], 'L3_attn_Wb': _L3_attn_in['Wb'], 'L3_attn_bb': _L3_attn_in['bb'], 'L3_attn_Wc': _L3_attn_in['Wc'], 'L3_attn_bc': _L3_attn_in['bc'], 'L3_attn_Wo': _L3_attn_in['Wo'], 'L3_attn_bo': _L3_attn_in['bo'], 'L3_attn_A': _L3_attn_in['A'], 'L3_xattn_Wq': _L3_xattn_in['Wq'], 'L3_xattn_bq': _L3_xattn_in['bq'], 'L3_xattn_Wk': _L3_xattn_in['Wk'], 'L3_xattn_bk': _L3_xattn_in['bk'], 'L3_xattn_Wv': _L3_xattn_in['Wv'], 'L3_xattn_bv': _L3_xattn_in['bv'], 'L3_xattn_Wo': _L3_xattn_in['Wo'], 'L3_xattn_bo': _L3_xattn_in['bo'], 'L3_ffn_w_gate': _L3_ffn_in['w_gate'], 'L3_ffn_w_in': _L3_ffn_in['w_in'], 'L3_ffn_w_out': _L3_ffn_in['w_out']}

def reference(x, ctx_1024, mask_BxSxS2_ik1, mask_Bx1xSxS2_ik1, mask_BxS_bf1, L0_attn_W, L0_attn_b, L0_xattn_gamma, L0_xattn_beta, L0_ffn_w1, L0_ffn_w2, L0_ffn_w3, L0_ffn_ws1, L0_ffn_ws2, L0_ffn_ws3, L0_ffn_wr, L1_attn_Wq, L1_attn_bq, L1_attn_Wk, L1_attn_bk, L1_attn_Wv, L1_attn_bv, L1_attn_Wo, L1_attn_bo, L1_attn_head_gates, L1_attn_rel_bias, L1_xattn_Wq, L1_xattn_bq, L1_xattn_Wk, L1_xattn_bk, L1_xattn_Wv, L1_xattn_bv, L1_xattn_Wo, L1_xattn_bo, L1_ffn_W1, L1_ffn_b1, L1_ffn_W2, L1_ffn_b2, L1_ffn_Wg, L1_ffn_bg, L2_attn_W_hg, L2_xattn_attn_norm_w, L2_xattn_Wq, L2_xattn_Wk, L2_xattn_Wv, L2_xattn_Wo, L2_xattn_bo, L2_xattn_cross_norm_w, L2_xattn_cWq, L2_xattn_cWk, L2_xattn_cWv, L2_xattn_cWo, L2_xattn_cbo, L2_xattn_ff_norm_w, L2_xattn_ff_w1, L2_xattn_ff_b1, L2_xattn_ff_w2, L2_xattn_ff_b2, L2_xattn_norm_out_w, L2_xattn_proj_w, L2_xattn_proj_b, L2_ffn_w1, L2_ffn_b1, L2_ffn_w2, L2_ffn_b2, L3_attn_Wd, L3_attn_bd, L3_attn_Wb, L3_attn_bb, L3_attn_Wc, L3_attn_bc, L3_attn_Wo, L3_attn_bo, L3_attn_A, L3_xattn_Wq, L3_xattn_bq, L3_xattn_Wk, L3_xattn_bk, L3_xattn_Wv, L3_xattn_bv, L3_xattn_Wo, L3_xattn_bo, L3_ffn_w_gate, L3_ffn_w_in, L3_ffn_w_out):
    import jax
    import jax.numpy as jnp

    def _L0_attn_ref(x, W, b):
        import jax, jax.numpy as jnp
        import numpy as np
        import math
        N_EMBD = 128
        N_HEAD = 16
        N_LAYER = 12
        B, T, C = x.shape
        H = N_HEAD
        D = C // H
        qkv = jnp.einsum('btc,oc->bto', x, W) + b
        q, k, v = jnp.split(qkv, 3, axis=-1)
        q = q.reshape(B, T, H, D).transpose(0, 2, 1, 3)
        k = k.reshape(B, T, H, D).transpose(0, 2, 1, 3)
        v = v.reshape(B, T, H, D).transpose(0, 2, 1, 3)
        att = jnp.einsum('bhtd,bhsd->bhts', q, k) / math.sqrt(D)
        causal = jnp.tril(jnp.ones((T, T), dtype=bool))
        att = jnp.where(causal, att, -jnp.inf)
        att = jax.nn.softmax(att, axis=-1)
        y = jnp.einsum('bhts,bhsd->bhtd', att, v)
        return y.transpose(0, 2, 1, 3).reshape(B, T, C)

    def _L0_xattn_ref(q, k, v, mask, gamma, beta):
        import jax, jax.numpy as jnp
        import numpy as np
        NEG = -9000000000000000.0
        EPS = 1e-05
        d_k = q.shape[-1]
        logits = jnp.einsum('bsd,btd->bst', q, k) / jnp.sqrt(jnp.asarray(d_k, q.dtype))
        logits = jnp.where(mask == 0, jnp.asarray(NEG, logits.dtype), logits)
        attn = jax.nn.softmax(logits, axis=-1)
        x = jnp.einsum('bst,btd->bsd', attn, v)
        mu = jnp.mean(x, axis=-1, keepdims=True)
        var = jnp.mean(jnp.square(x - mu), axis=-1, keepdims=True)
        xhat = (x - mu) * jax.lax.rsqrt(var + EPS)
        return xhat * gamma + beta

    def _L0_ffn_ref(x, w1, w2, w3, ws1, ws2, ws3, wr):
        import jax, jax.numpy as jnp
        import numpy as np
        B, T, C = (4, 1024, 128)
        E, I, IS, K = (8, 128, 32, 6)
        b, t, c = x.shape
        xf = x.reshape(-1, c)
        out_shared = jax.nn.silu(xf @ ws1) * (xf @ ws2) @ ws3
        probs = jax.nn.softmax(xf @ wr, axis=-1)
        topk_w, topk_i = jax.lax.top_k(probs, K)
        topk_w = topk_w / jnp.sum(topk_w, axis=-1, keepdims=True)
        onehot = jax.nn.one_hot(topk_i, E, dtype=x.dtype)
        w_full = jnp.einsum('nk,nke->ne', topk_w, onehot)
        h = jax.nn.silu(jnp.einsum('nc,eci->nei', xf, w1)) * jnp.einsum('nc,eci->nei', xf, w2)
        out_routed = jnp.einsum('nei,eic,ne->nc', h, w3, w_full)
        return (out_shared + out_routed).reshape(b, t, c)

    def _L1_attn_ref(x, Wq, bq, Wk, bk, Wv, bv, Wo, bo, head_gates, rel_bias):
        import jax, jax.numpy as jnp
        import numpy as np
        import math
        EMBED_DIM = 128
        NUM_HEADS = 16
        HEAD_DIM = EMBED_DIM // NUM_HEADS
        MAX_POS = 64
        SPARSE_TOPK = 32
        B, T = (8, 64)
        Bb, Tt, C = x.shape
        H, D = (NUM_HEADS, HEAD_DIM)
        q = (x @ Wq.T + bq).reshape(Bb, Tt, H, D).transpose(0, 2, 1, 3)
        k = (x @ Wk.T + bk).reshape(Bb, Tt, H, D).transpose(0, 2, 1, 3)
        v = (x @ Wv.T + bv).reshape(Bb, Tt, H, D).transpose(0, 2, 1, 3)
        scores = jnp.einsum('bhqd,bhkd->bhqk', q, k) / math.sqrt(D)
        idx = jnp.arange(Tt)
        rel = idx[None, :] - idx[:, None] + (MAX_POS - 1)
        pos_bias = rel_bias[rel].transpose(2, 0, 1)[None]
        scores = scores + pos_bias
        if SPARSE_TOPK > 0:
            topk_vals, _ = jax.lax.top_k(scores, SPARSE_TOPK)
            thresh = topk_vals[..., -1:]
            scores = jnp.where(scores >= thresh, scores, -jnp.inf)
        weights = jax.nn.softmax(scores, axis=-1)
        gated = weights * head_gates[None, :, None, None]
        attn_out = jnp.einsum('bhqk,bhkd->bhqd', gated, v)
        attn_out = attn_out.transpose(0, 2, 1, 3).reshape(Bb, Tt, C)
        return attn_out @ Wo.T + bo

    def _L1_xattn_ref(query, key, value, mask, Wq, bq, Wk, bk, Wv, bv, Wo, bo):
        import jax, jax.numpy as jnp
        import numpy as np
        D_MODEL = 128
        H = 16
        D_K = D_MODEL // H
        NEG = -100000000000.0

        def _split_heads(x):
            B, N, _ = x.shape
            return x.reshape(B, N, H, D_K).transpose(0, 2, 1, 3)
        q = _split_heads(query @ Wq + bq)
        k = _split_heads(key @ Wk + bk)
        v = _split_heads(value @ Wv + bv)
        scores = jnp.einsum('bhqd,bhkd->bhqk', q, k) / jnp.sqrt(jnp.float32(D_K))
        scores = jnp.where(mask == 0, jnp.float32(NEG), scores)
        attn = jax.nn.softmax(scores, axis=-1)
        out = jnp.einsum('bhqk,bhkd->bhqd', attn, v)
        B, _, N, _ = out.shape
        out = out.transpose(0, 2, 1, 3).reshape(B, N, D_MODEL)
        return out @ Wo + bo

    def _L1_ffn_ref(x, W1, b1, W2, b2, Wg, bg):
        import jax, jax.numpy as jnp
        import numpy as np
        D_MODEL, D_FF, N_EXPERTS, TOP_K = (128, 512, 8, 2)
        B, S = (2, 256)
        Bx, Sx, d = x.shape
        E = W1.shape[0]
        logits = jnp.einsum('bsd,de->bse', x, Wg) + bg
        topk_scores, topk_idx = jax.lax.top_k(logits, TOP_K)
        topk_scores = jax.nn.softmax(topk_scores, axis=-1)
        tokens = x.reshape(-1, d)
        idx_flat = topk_idx.reshape(-1, TOP_K)
        sc_flat = topk_scores.reshape(-1, TOP_K)
        comb = (jax.nn.one_hot(idx_flat, E, dtype=x.dtype) * sc_flat[..., None]).sum(axis=1)
        h = jnp.einsum('td,edf->etf', tokens, W1) + b1[:, None, :]
        even = (jnp.arange(E) % 2 == 0)[:, None, None]
        a = jnp.where(even, jax.nn.gelu(h, approximate=False), jax.nn.silu(h))
        y = jnp.einsum('etf,efd->etd', a, W2) + b2[:, None, :]
        out = jnp.einsum('te,etd->td', comb, y)
        return out.reshape(Bx, Sx, d)

    def _L2_attn_ref(x, W_hg):
        import jax, jax.numpy as jnp
        import numpy as np

        def log_g(x):
            pos = jnp.log(jnp.maximum(x, 0.0) + 0.5)
            neg = -jax.nn.softplus(-x)
            return jnp.where(x >= 0, pos, neg)

        def parallel_scan_log(log_coeffs, log_values):
            a_star = jnp.cumsum(log_coeffs, axis=1)
            log_h0_plus_b_star = jax.lax.cumlogsumexp(log_values - a_star, axis=1)
            log_h = a_star + log_h0_plus_b_star
            return jnp.exp(log_h)
        hg = jnp.einsum('bsd,ed->bse', x, W_hg)
        hidden, gate = jnp.split(hg, 2, axis=-1)
        log_coeffs = -jax.nn.softplus(gate)
        log_z = -jax.nn.softplus(-gate)
        log_tilde_h = log_g(hidden)
        log_values = log_z + log_tilde_h
        out = parallel_scan_log(log_coeffs, log_values)
        return out

    def _L2_xattn_ref(x, chunked_seq, mask, attn_norm_w, Wq, Wk, Wv, Wo, bo, cross_norm_w, cWq, cWk, cWv, cWo, cbo, ff_norm_w, ff_w1, ff_b1, ff_w2, ff_b2, norm_out_w, proj_w, proj_b):
        import jax, jax.numpy as jnp
        import numpy as np
        L = 2
        D = 128
        HS = 128
        NH = 16
        DH = 64
        FF = 512
        ROT = 32
        B, SQ, SK = (64, 128, 64)
        EPS = 1e-08

        def rmsnorm(x, w):
            norm = jnp.sqrt(jnp.sum(x * x, axis=-1, keepdims=True)) * x.shape[-1] ** (-0.5)
            return x / jnp.maximum(norm, EPS) * w

        def rope_freqs(n):
            inv_freq = 1.0 / 10000.0 ** (jnp.arange(0, ROT, 2, dtype=jnp.float32) / ROT)
            f = jnp.arange(n, dtype=jnp.float32)[:, None] * inv_freq[None, :]
            return jnp.concatenate([f, f], axis=-1)[None, None]

        def apply_rope(t, freqs):
            rd = freqs.shape[-1]
            t1, tp = (t[..., :rd], t[..., rd:])
            half = rd // 2
            a, b = (t1[..., :half], t1[..., half:])
            rot = jnp.concatenate([-b, a], axis=-1)
            t1 = t1 * jnp.cos(freqs) + rot * jnp.sin(freqs)
            return jnp.concatenate([t1, tp], axis=-1)

        def attention(x, ctx, Wq, Wk, Wv, Wo, bo, pe_q, pe_k, mask):
            b, n, _ = x.shape
            m = ctx.shape[1]
            q = (x @ Wq).reshape(b, n, NH, DH).transpose(0, 2, 1, 3) * DH ** (-0.5)
            k = (ctx @ Wk).reshape(b, m, NH, DH).transpose(0, 2, 1, 3)
            v = (ctx @ Wv).reshape(b, m, NH, DH).transpose(0, 2, 1, 3)
            q = apply_rope(q, pe_q)
            k = apply_rope(k, pe_k)
            sim = jnp.einsum('bhid,bhjd->bhij', q, k)
            if mask is not None:
                sim = jnp.where(mask[:, None, None, :], sim, -jnp.finfo(sim.dtype).max)
            attn = jax.nn.softmax(sim, axis=-1)
            out = jnp.einsum('bhij,bhjd->bhid', attn, v)
            out = out.transpose(0, 2, 1, 3).reshape(b, n, NH * DH)
            return out @ Wo + bo
        pe_q = rope_freqs(x.shape[-2])
        pe_k = rope_freqs(chunked_seq.shape[-2])
        for l in range(L):
            h = rmsnorm(x, attn_norm_w[l])
            x = attention(h, h, Wq[l], Wk[l], Wv[l], Wo[l], bo[l], pe_q, pe_q, mask) + x
            h = rmsnorm(x, cross_norm_w[l])
            x = attention(h, chunked_seq, cWq[l], cWk[l], cWv[l], cWo[l], cbo[l], pe_q, pe_k, None) + x
            h = rmsnorm(x, ff_norm_w[l])
            x = jax.nn.gelu(h @ ff_w1[l] + ff_b1[l], approximate=False) @ ff_w2[l] + ff_b2[l] + x
        x = rmsnorm(x, norm_out_w)
        return x @ proj_w + proj_b

    def _L2_ffn_ref(x, w1, b1, w2, b2):
        import jax, jax.numpy as jnp
        import numpy as np
        EPS = 1e-05

        def rmsnorm(x):
            return x * jax.lax.rsqrt(jnp.mean(x * x, axis=-1, keepdims=True) + EPS)

        def act_quant(x):
            scale = 127.0 / jnp.clip(jnp.max(jnp.abs(x), axis=-1, keepdims=True), 1e-05)
            q = jnp.clip(jnp.round(x * scale), -128.0, 127.0) / scale
            return x + jax.lax.stop_gradient(q - x)

        def weight_quant(w):
            scale = 1.0 / jnp.clip(jnp.mean(jnp.abs(w)), 1e-05)
            q = jnp.clip(jnp.round(w * scale), -1.0, 1.0) / scale
            return w + jax.lax.stop_gradient(q - w)

        def bitlinear(x, w, b):
            xq = act_quant(rmsnorm(x))
            wq = weight_quant(w)
            return jnp.einsum('bsd,fd->bsf', xq, wq) + b
        h = bitlinear(x, w1, b1)
        h = jax.nn.gelu(h, approximate=False)
        return bitlinear(h, w2, b2)

    def _L3_attn_ref(x, Wd, bd, Wb, bb, Wc, bc, Wo, bo, A):
        import jax, jax.numpy as jnp
        import numpy as np
        delta = jax.nn.softplus(x @ Wd + bd)
        dbar = jnp.mean(delta, axis=-1, keepdims=True)
        Bt = x @ Wb + bb
        Ct = x @ Wc + bc
        sA = jax.nn.sigmoid(jnp.mean(A, axis=0))
        a = 1.0 - dbar
        b = dbar * Bt * sA

        def step(h, ab):
            at, bt = ab
            h = h * at + bt
            return (h, h)
        h0 = jnp.zeros((x.shape[0], A.shape[1]), x.dtype)
        _, hs = jax.lax.scan(step, h0, (jnp.swapaxes(a, 0, 1), jnp.swapaxes(b, 0, 1)))
        hs = jnp.swapaxes(hs, 0, 1)
        y = jnp.sum(hs * Ct, axis=-1, keepdims=True) * x
        return y @ Wo + bo

    def _L3_xattn_ref(query, key_value, Wq, bq, Wk, bk, Wv, bv, Wo, bo):
        import jax, jax.numpy as jnp
        import numpy as np
        B, SQ, SKV, E, H = (4, 256, 256, 128, 16)
        HD = E // H

        def stablemax(x):
            s = jnp.where(x >= 0, x + 1.0, 1.0 / (1.0 - x))
            return s / jnp.sum(s, axis=-1, keepdims=True)
        b = query.shape[0]
        q = query @ Wq.T + bq
        k = key_value @ Wk.T + bk
        v = key_value @ Wv.T + bv
        q = q.reshape(b, -1, H, HD).transpose(0, 2, 1, 3)
        k = k.reshape(b, -1, H, HD).transpose(0, 2, 1, 3)
        v = v.reshape(b, -1, H, HD).transpose(0, 2, 1, 3)
        scores = jnp.einsum('bhqd,bhkd->bhqk', q, k) / np.sqrt(HD).astype(np.float32)
        attn = stablemax(scores)
        context = jnp.einsum('bhqk,bhkd->bhqd', attn, v)
        context = context.transpose(0, 2, 1, 3).reshape(b, -1, E)
        return context @ Wo.T + bo

    def _L3_ffn_ref(x, w_gate, w_in, w_out):
        import jax, jax.numpy as jnp
        import numpy as np
        D_MODEL = 128
        HIDDEN = 512
        NUM_EXPERTS = 8
        TOP_K = 2
        B, S, D = x.shape
        E = w_in.shape[0]
        xt = x.reshape(-1, D)
        logits = (xt @ w_gate.T).astype(jnp.float32)
        top_logits, top_idx = jax.lax.top_k(logits, TOP_K)
        top_gates = jax.nn.softmax(top_logits, axis=-1).astype(x.dtype)
        gates = (jax.nn.one_hot(top_idx, E, dtype=x.dtype) * top_gates[..., None]).sum(axis=1)
        y = jnp.zeros_like(xt)
        for e in range(E):
            h = xt @ w_in[e].T
            y = y + gates[:, e:e + 1] * (h @ w_out[e].T)
        return y.reshape(B, S, D)
    x = x + _L0_attn_ref(_layernorm(x, axis=-1), L0_attn_W, L0_attn_b)
    x = x + _L0_xattn_ref(_layernorm(x, axis=-1), ctx_1024, ctx_1024, mask_BxSxS2_ik1, L0_xattn_gamma, L0_xattn_beta)
    x = x + _L0_ffn_ref(_layernorm(x, axis=-1), L0_ffn_w1, L0_ffn_w2, L0_ffn_w3, L0_ffn_ws1, L0_ffn_ws2, L0_ffn_ws3, L0_ffn_wr)
    x = x + _L1_attn_ref(_layernorm(x, axis=-1), L1_attn_Wq, L1_attn_bq, L1_attn_Wk, L1_attn_bk, L1_attn_Wv, L1_attn_bv, L1_attn_Wo, L1_attn_bo, L1_attn_head_gates, L1_attn_rel_bias)
    x = x + _L1_xattn_ref(_layernorm(x, axis=-1), ctx_1024, ctx_1024, mask_Bx1xSxS2_ik1, L1_xattn_Wq, L1_xattn_bq, L1_xattn_Wk, L1_xattn_bk, L1_xattn_Wv, L1_xattn_bv, L1_xattn_Wo, L1_xattn_bo)
    x = x + _L1_ffn_ref(_layernorm(x, axis=-1), L1_ffn_W1, L1_ffn_b1, L1_ffn_W2, L1_ffn_b2, L1_ffn_Wg, L1_ffn_bg)
    x = x + _L2_attn_ref(_layernorm(x, axis=-1), L2_attn_W_hg)
    x = x + _L2_xattn_ref(_layernorm(x, axis=-1), ctx_1024, mask_BxS_bf1, L2_xattn_attn_norm_w, L2_xattn_Wq, L2_xattn_Wk, L2_xattn_Wv, L2_xattn_Wo, L2_xattn_bo, L2_xattn_cross_norm_w, L2_xattn_cWq, L2_xattn_cWk, L2_xattn_cWv, L2_xattn_cWo, L2_xattn_cbo, L2_xattn_ff_norm_w, L2_xattn_ff_w1, L2_xattn_ff_b1, L2_xattn_ff_w2, L2_xattn_ff_b2, L2_xattn_norm_out_w, L2_xattn_proj_w, L2_xattn_proj_b)
    x = x + _L2_ffn_ref(_layernorm(x, axis=-1), L2_ffn_w1, L2_ffn_b1, L2_ffn_w2, L2_ffn_b2)
    x = x + _L3_attn_ref(_layernorm(x, axis=-1), L3_attn_Wd, L3_attn_bd, L3_attn_Wb, L3_attn_bb, L3_attn_Wc, L3_attn_bc, L3_attn_Wo, L3_attn_bo, L3_attn_A)
    x = x + _L3_xattn_ref(_layernorm(x, axis=-1), ctx_1024, L3_xattn_Wq, L3_xattn_bq, L3_xattn_Wk, L3_xattn_bk, L3_xattn_Wv, L3_xattn_bv, L3_xattn_Wo, L3_xattn_bo)
    x = x + _L3_ffn_ref(_layernorm(x, axis=-1), L3_ffn_w_gate, L3_ffn_w_in, L3_ffn_w_out)
    return x

_drawn_inputs = setup_inputs


def setup_inputs(seed=0):
    import zlib

    import numpy as np

    out = dict(_drawn_inputs(seed))
    spreads = {'L0_xattn_gamma': (1.0, 0.2),
     'L0_xattn_beta': (0.0, 0.1),
     'L1_attn_head_gates': (1.0, 0.6),
     'L1_xattn_bq': (0.0, 0.513),
     'L1_xattn_bk': (0.0, 2.0),
     'L1_xattn_bv': (0.0, 0.1),
     'L1_xattn_bo': (0.0, 0.1),
     'L1_ffn_b1': (0.0, 0.726),
     'L1_ffn_b2': (0.0, 0.268),
     'L1_ffn_bg': (0.0, 0.1),
     'L2_xattn_attn_norm_w': (1.0, 0.6),
     'L2_xattn_bo': (0.0, 0.455),
     'L2_xattn_cross_norm_w': (1.0, 0.6),
     'L2_xattn_cbo': (0.0, 1.814),
     'L2_xattn_ff_norm_w': (1.0, 0.6),
     'L2_xattn_ff_b1': (0.0, 0.8),
     'L2_xattn_ff_b2': (0.0, 1.923),
     'L2_xattn_norm_out_w': (1.0, 0.6),
     'L2_xattn_proj_b': (0.0, 0.277),
     'L2_ffn_b1': (0.0, 0.1),
     'L2_ffn_b2': (0.0, 0.1),
     'L3_attn_bd': (0.0, 2.0),
     'L3_attn_bb': (0.0, 0.8),
     'L3_attn_bc': (0.0, 0.8),
     'L3_attn_bo': (0.0, 0.403),
     'L3_xattn_bq': (0.0, 2.0),
     'L3_xattn_bk': (0.0, 2.0),
     'L3_xattn_bv': (0.0, 0.375),
     'L3_xattn_bo': (0.0, 0.38)}
    factors = {'L0_attn_W': 5.493,
     'L0_ffn_w1': 8.0,
     'L0_ffn_w2': 8.0,
     'L0_ffn_w3': 8.0,
     'L0_ffn_ws1': 8.0,
     'L0_ffn_ws2': 8.0,
     'L0_ffn_ws3': 8.0,
     'L0_ffn_wr': 8.0,
     'L1_attn_bq': 5.898,
     'L1_attn_bk': 64.0,
     'L1_attn_bv': 2.831,
     'L1_attn_rel_bias': 21.387,
     'L1_ffn_W1': 2.868,
     'L2_xattn_Wq': 8.0,
     'L2_xattn_Wk': 8.0,
     'L2_xattn_Wv': 3.125,
     'L2_xattn_Wo': 3.524,
     'L2_xattn_cWq': 8.0,
     'L2_xattn_cWk': 8.0,
     'L2_xattn_cWv': 5.068,
     'L2_xattn_cWo': 4.31,
     'L2_xattn_ff_w1': 5.77,
     'L2_xattn_ff_w2': 5.432,
     'L3_attn_Wd': 8.0,
     'L3_attn_Wb': 4.539,
     'L3_attn_Wc': 4.643,
     'L3_attn_Wo': 4.123,
     'L3_attn_A': 64.0,
     'L3_ffn_w_gate': 32.182,
     'L3_ffn_w_in': 29.692,
     'L3_ffn_w_out': 30.135}
    for name, (base, spread) in spreads.items():
        noise = np.random.default_rng([zlib.crc32(name.encode()), seed]).standard_normal(out[name].shape)
        drawn = base * np.exp(spread * noise) if base else spread * noise
        out[name] = jnp.asarray(drawn.astype(out[name].dtype))
    for name, factor in factors.items():
        out[name] = (out[name] * factor).astype(out[name].dtype)
    return out
```

```python
from contextlib import ExitStack

import numpy as np
import concourse.bass as bass
from concourse import mybir

F32 = mybir.dt.float32
BF16 = mybir.dt.bfloat16
I32 = mybir.dt.int32
U8 = mybir.dt.uint8
ALU = mybir.AluOpType
ACT = mybir.ActivationFunctionType
AXX = mybir.AxisListType.X

P = 128
B, T, C = 2, 512, 128
NT = B * T // P
TB = T // P
KC = 77
H = 16
BANK = 512
NEG = -1.0e30
ROUND = 12582912.0
SUBLAYERS = (0, 1, 2, 3, 4, 5, 6, 7, 8, 9, 10, 11)


class Signal:

    def __init__(self, nc, ctx, name):
        self.sem = ctx.enter_context(nc.semaphore(name))
        self.base = 0
        self.count = 0

    def step(self):
        self.count += 1
        return 1

    def at(self, n):
        return self.base + n

    def next_region(self):
        self.base = self.count


class Chain:

    def __init__(self, nc, ctx, name):
        self.sem = ctx.enter_context(nc.semaphore(name))
        self.count = 0

    def link(self, eng, ins):
        self.count += 1
        ins.then_inc(self.sem, 1)
        eng.wait_ge(self.sem, self.count)


def wide(ap, n, axis):
    return ap.unsqueeze(axis).broadcast_to(list(ap.shape[:axis]) + [n] + list(ap.shape[axis:]))


class Core:

    SIGNALS = ("norm_stats", "norm_scale", "norm_rows", "norm_turned", "norm_taken", "mm_done", "mm_taken",
               "raw_ready", "swap_done", "cos_done", "rope_done", "s_done", "s_taken", "max_done", "exp_done", "turn_done",
               "turn_taken", "pv_done", "o_done", "t_turned", "t_taken", "out_done", "out_added", "act_done",
               "prod_done", "y_done", "y_added", "gates_done", "aux_pe", "aux_dve", "aux_act", "aux_pool")

    def __init__(self, nc, ctx):
        self.nc = nc
        self.dve_chain = Chain(nc, ctx, "dve_chain")
        self.act_chain = Chain(nc, ctx, "act_chain")
        self.pool_chain = Chain(nc, ctx, "pool_chain")
        self.sig = {n: Signal(nc, ctx, n) for n in self.SIGNALS}
        self.bank = [ctx.enter_context(nc.psum_tensor(f"bank{i}", [P, BANK], F32)) for i in range(8)]

        def sb(name, shape, dt=F32):
            return ctx.enter_context(nc.sbuf_tensor(name, shape, dt))

        self.x_sb = sb("x_sb", [P, NT, C])
        self.y_sb = sb("y_sb", [P, NT, C])
        self.xn = sb("xn", [P, NT, C])
        self.xn_t = sb("xn_t", [P, B * T])
        self.stats = sb("stats", [P, NT, 6])
        self.mv = sb("mv", [P, NT, 2])
        self.spread = sb("spread", [P, NT])
        self.rstd = sb("rstd", [P, NT])
        self.minus_half = sb("minus_half", [P, NT])

    def end_region(self):
        for s in self.sig.values():
            s.next_region()



def normalise(core, src, ident, mean_free=True, weight=None, keep_rows=None, loads=()):
    nc, sig = core.nc, core.sig
    with nc.Block() as block:
        @block.vector
        def _(dve):
            link = core.dve_chain.link
            for s, v in loads:
                dve.wait_ge(s, v)
            for t in range(NT):
                last = nc.vector.bn_stats(core.stats[:, t, :], src[:, t, :])
            link(dve, last)
            for t in range(NT):
                last = nc.vector.bn_aggr(core.mv[:, t, :], core.stats[:, t, :])
            link(dve, last)
            mean, var = core.mv[:, :, 0], core.mv[:, :, 1]
            if mean_free:
                nc.vector.tensor_scalar(core.spread[:], var, 1e-5, None, ALU.add).then_inc(
                    sig["norm_stats"].sem, sig["norm_stats"].step())
            else:
                link(dve, nc.vector.tensor_tensor(core.spread[:], mean, mean, ALU.mult))
                link(dve, nc.vector.tensor_tensor(core.spread[:], core.spread[:], var, ALU.add))
                nc.vector.tensor_scalar(core.spread[:], core.spread[:], 1e-16, None, ALU.max).then_inc(
                    sig["norm_stats"].sem, sig["norm_stats"].step())
            dve.wait_ge(sig["norm_scale"].sem, sig["norm_scale"].at(1))
            for t in range(NT):
                if mean_free:
                    ins = nc.vector.tensor_scalar(core.xn[:, t, :], src[:, t, :], core.mv[:, t, 0:1],
                                                  core.rstd[:, t:t + 1], ALU.subtract, ALU.mult)
                else:
                    ins = nc.vector.tensor_scalar(core.xn[:, t, :], src[:, t, :], core.rstd[:, t:t + 1],
                                                  None, ALU.mult)
                ins.then_inc(sig["norm_rows"].sem, sig["norm_rows"].step())
            if keep_rows is not None:
                dve.wait_ge(sig["norm_rows"].sem, sig["norm_rows"].at(NT))
                nc.vector.tensor_copy(keep_rows[:], core.xn[:])

        @block.gpsimd
        def _(pool):
            pool.wait_ge(sig["norm_stats"].sem, sig["norm_stats"].at(1))
            nc.gpsimd.tensor_tensor(core.rstd[:], core.spread[:], core.minus_half[:], ALU.pow).then_inc(
                sig["norm_scale"].sem, sig["norm_scale"].step())

        @block.tensor
        def _(pe):
            for t in range(NT):
                pe.wait_ge(sig["norm_rows"].sem, sig["norm_rows"].at(t + 1))
                ins = nc.tensor.transpose(core.bank[t // TB][:, (t % TB) * P:(t % TB + 1) * P],
                                          core.xn[:, t, :], ident)
                if t % TB == TB - 1:
                    ins.then_inc(sig["norm_turned"].sem, sig["norm_turned"].step())

        @block.scalar
        def _(act):
            for b in range(B):
                act.wait_ge(sig["norm_turned"].sem, sig["norm_turned"].at(b + 1))
                nc.scalar.activation(core.xn_t[:, b * T:(b + 1) * T], core.bank[b][:], ACT.Copy if weight is None
                                     else ACT.Identity, scale=1.0 if weight is None else weight)
    core.end_region()



def project(core, jobs, rope=None):
    nc, sig = core.nc, core.sig
    NB = 4
    turned = [i for i, j in enumerate(jobs) if j[5]]
    by_act = [i for i, j in enumerate(jobs) if j[5] or i % 2 == 0]
    by_dve = [i for i in range(len(jobs)) if i not in by_act]

    def wait_taken(eng, i):
        if i in by_act:
            eng.wait_ge(sig["act_done"].sem, sig["act_done"].at(by_act.index(i) + 1))
        else:
            eng.wait_ge(sig["prod_done"].sem, sig["prod_done"].at(by_dve.index(i) + 1))

    with nc.Block() as block:
        @block.tensor
        def _(pe):
            def swap(n):
                i = turned[n]
                pe.wait_ge(sig["act_done"].sem, sig["act_done"].at(by_act.index(i) + 1))
                if n >= 2:
                    pe.wait_ge(sig["swap_done"].sem, sig["swap_done"].at(n - 1))
                nd = jobs[i][0].shape[-1]
                nc.tensor.matmul(core.bank[NB + n % 2][:, :nd], rope[0], rope[3][:, n % 3, :nd],
                                 start=True, stop=True).then_inc(sig["raw_ready"].sem, sig["raw_ready"].step())

            swapped = 0
            for i, (dst, lhs, rhs, col, row, turn) in enumerate(jobs):
                if i >= NB:
                    wait_taken(pe, i - NB)
                m, n = lhs.shape[-1], rhs.shape[-1]
                out = core.bank[i % NB][:m, :n]
                ins = nc.tensor.matmul(out, lhs, rhs, start=True, stop=row is None)
                if row is not None:
                    ins = nc.tensor.matmul(out, core.ones_row[0:1, :m], row, start=False, stop=True)
                ins.then_inc(sig["mm_done"].sem, sig["mm_done"].step())
                while swapped < len(turned) and turned[swapped] <= i - 2:
                    swap(swapped)
                    swapped += 1
            while swapped < len(turned):
                swap(swapped)
                swapped += 1

        @block.scalar
        def _(act):
            for i in by_act:
                dst, lhs, rhs, col, row, turn = jobs[i]
                act.wait_ge(sig["mm_done"].sem, sig["mm_done"].at(i + 1))
                if turn:
                    n = turned.index(i)
                    if n >= 3:
                        act.wait_ge(sig["raw_ready"].sem, sig["raw_ready"].at(n - 2))
                        act.wait_ge(sig["cos_done"].sem, sig["cos_done"].at(n - 2))
                    dst = rope[3][:, n % 3, :dst.shape[-1]]
                src = core.bank[i % NB][:lhs.shape[-1], :rhs.shape[-1]]
                nc.scalar.activation(dst, src, ACT.Identity, bias=0.0 if col is None else col).then_inc(
                    sig["act_done"].sem, sig["act_done"].step())

        @block.gpsimd
        def _(pool):
            for n, i in enumerate(turned):
                nd = jobs[i][0].shape[-1]
                pool.wait_ge(sig["act_done"].sem, sig["act_done"].at(by_act.index(i) + 1))
                if n >= 3:
                    pool.wait_ge(sig["rope_done"].sem, sig["rope_done"].at(n - 2))
                nc.gpsimd.tensor_tensor(rope[4][:, n % 3, :nd], rope[3][:, n % 3, :nd], rope[1][:, :nd],
                                        ALU.mult).then_inc(sig["cos_done"].sem, sig["cos_done"].step())

        @block.vector
        def _(dve):
            def turn_one(n):
                dst = jobs[turned[n]][0]
                nd = dst.shape[-1]
                dve.wait_ge(sig["raw_ready"].sem, sig["raw_ready"].at(n + 1))
                if n >= 2:
                    dve.wait_ge(sig["rope_done"].sem, sig["rope_done"].at(n - 1))
                nc.vector.tensor_tensor(rope[5][:, n % 2, :nd], core.bank[NB + n % 2][:, :nd], rope[2][:, :nd],
                                        ALU.mult).then_inc(sig["swap_done"].sem, sig["swap_done"].step())
                dve.wait_ge(sig["swap_done"].sem, sig["swap_done"].at(n + 1))
                dve.wait_ge(sig["cos_done"].sem, sig["cos_done"].at(n + 1))
                nc.vector.tensor_tensor(dst, rope[4][:, n % 3, :nd], rope[5][:, n % 2, :nd], ALU.add).then_inc(
                    sig["rope_done"].sem, sig["rope_done"].step())

            for i in range(len(jobs)):
                if i in by_dve:
                    dst, lhs, rhs, col, row, _ = jobs[i]
                    dve.wait_ge(sig["mm_done"].sem, sig["mm_done"].at(i + 1))
                    src = core.bank[i % NB][:lhs.shape[-1], :rhs.shape[-1]]
                    if col is None:
                        ins = nc.vector.tensor_copy(dst, src)
                    else:
                        ins = nc.vector.tensor_scalar(dst, src, col, None, ALU.add)
                    ins.then_inc(sig["prod_done"].sem, sig["prod_done"].step())
                if i in turned:
                    turn_one(turned.index(i))
    core.end_region()



class Tail:

    def __init__(self, core, dst, o_sb, o_t, wo, row, nch, ident, banks, out_bank):
        self.core, self.dst, self.o_sb, self.o_t, self.wo = core, dst, o_sb, o_t, wo
        self.row, self.nch, self.ident, self.banks, self.out_bank = row, nch, ident, banks, out_bank

    def rounds(self):
        return -(-self.nch // 4)

    def turn(self, pe, u):
        core, sig = self.core, self.core.sig
        pe.wait_ge(sig["o_done"].sem, sig["o_done"].at(u + 1))
        for j in range(self.rounds()):
            r = self.rounds() * u + j
            if r >= len(self.banks):
                pe.wait_ge(sig["t_taken"].sem, sig["t_taken"].at(r - len(self.banks) + 1))
            for c in range(4 * j, min(4 * j + 4, self.nch)):
                ins = core.nc.tensor.transpose(self.banks[r % len(self.banks)][:, (c % 4) * P:(c % 4 + 1) * P],
                                               self.o_sb[:, c * P:(c + 1) * P], self.ident)
            ins.then_inc(sig["t_turned"].sem, sig["t_turned"].step())

    def copy(self, act, u):
        core, sig = self.core, self.core.sig
        for j in range(self.rounds()):
            r = self.rounds() * u + j
            n = min(4, self.nch - 4 * j) * P
            act.wait_ge(sig["t_turned"].sem, sig["t_turned"].at(r + 1))
            if u >= 1:
                act.wait_ge(sig["out_done"].sem, sig["out_done"].at(u))
            core.nc.scalar.activation(self.o_t[:, j * BANK:j * BANK + n], self.banks[r % len(self.banks)][:, :n],
                                      ACT.Copy).then_inc(sig["t_taken"].sem, sig["t_taken"].step())

    def product(self, pe, u):
        core, sig = self.core, self.core.sig
        pe.wait_ge(sig["t_taken"].sem, sig["t_taken"].at(self.rounds() * (u + 1)))
        if u >= 1:
            pe.wait_ge(sig["out_added"].sem, sig["out_added"].at(u))
        for c in range(self.nch):
            core.nc.tensor.matmul(self.out_bank[:, :C], self.o_t[:, c * P:(c + 1) * P],
                                  self.wo[:, c * C:(c + 1) * C], start=c == 0, stop=False)
        core.nc.tensor.matmul(self.out_bank[:, :C], core.ones_row[0:1, :], self.row, start=False,
                              stop=True).then_inc(sig["out_done"].sem, sig["out_done"].step())

    def add(self, dve, u, tile):
        core, sig = self.core, self.core.sig
        dve.wait_ge(sig["out_done"].sem, sig["out_done"].at(u + 1))
        core.nc.vector.tensor_tensor(self.dst[:, tile, :], self.dst[:, tile, :], self.out_bank[:, :C],
                                     ALU.add).then_inc(sig["out_added"].sem, sig["out_added"].step())



def self_attention(core, ctx, b, q_of, k_of, v_of, hd, scale, dst, ident, tail=None, causal=None, key_mask=None,
                   top=None, gate=None):
    nc, sig = core.nc, core.sig
    units = [(qt, h) for qt in range(TB) for h in range(H)]
    U = len(units)
    NS, NE, NX = (2 if hd == 64 else 3), 2, 3

    def sb(name, shape, dt=F32):
        return ctx.enter_context(nc.sbuf_tensor(f"{name}_{nc.next_id()}", shape, dt))

    e_sb = sb("e_sb", [P, NX, T])
    e_t = sb("e_t", [P, NE, T])
    s_sb = sb("s_sb", [P, 2, T]) if top else None
    work = sb("work", [P, 2, T]) if top else None
    best = sb("best", [P, 2, 32]) if top else None
    nmax = sb("nmax", [P, NS])
    den = sb("den", [P, 2, H])
    rden = sb("rden", [P, H])
    o_sb = sb("o_sb", [P, H * hd])
    s_bank = core.bank[0:NS]
    t_bank = core.bank[3:5]
    o_bank = core.bank[5:7] if hd == 64 else core.bank[5:6]
    HB = BANK // hd if hd == 64 else H

    def chunks(qt):
        return qt + 1 if causal else TB

    if tail is not None:
        tail.o_sb = o_sb

    with nc.Block() as block:
        @block.tensor
        def _(pe):
            def scores(u):
                qt, h = units[u]
                n = chunks(qt) * P
                if u >= NS:
                    pe.wait_ge(sig["exp_done"].sem, sig["exp_done"].at(u - NS + 1))
                    if top:
                        pe.wait_ge(sig["s_taken"].sem, sig["s_taken"].at(u - NS + 1))
                out = s_bank[u % NS][:, :n]
                ins = nc.tensor.matmul(out, q_of(h, qt), k_of(h)[:, :n], start=True,
                                       stop=not (causal or key_mask))
                if causal:
                    ins = nc.tensor.matmul(out[:, n - P:n], causal[0], causal[1], start=False, stop=True)
                if key_mask:
                    ins = nc.tensor.matmul(out, key_mask[0], key_mask[1], start=False, stop=True)
                ins.then_inc(sig["s_done"].sem, sig["s_done"].step())

            def turn(u):
                qt, h = units[u]
                pe.wait_ge(sig["prod_done" if top else "exp_done"].sem,
                           sig["prod_done" if top else "exp_done"].at(u + 1))
                if u >= 2:
                    pe.wait_ge(sig["turn_taken"].sem, sig["turn_taken"].at(u - 1))
                for k in range(chunks(qt)):
                    ins = nc.tensor.transpose(t_bank[u % 2][:, k * P:(k + 1) * P],
                                              e_sb[:, u % NX, k * P:(k + 1) * P], ident)
                ins.then_inc(sig["turn_done"].sem, sig["turn_done"].step())

            def values(u):
                qt, h = units[u]
                pe.wait_ge(sig["turn_taken"].sem, sig["turn_taken"].at(u + 1))
                if h == 0 and qt >= 1:
                    pe.wait_ge(sig["o_done"].sem, sig["o_done"].at(qt))
                out = o_bank[h // HB][:, (h % HB) * hd:(h % HB + 1) * hd]
                for k in range(chunks(qt)):
                    ins = nc.tensor.matmul(out, e_t[:, u % NE, k * P:(k + 1) * P], v_of(h, k),
                                           start=k == 0, stop=k == chunks(qt) - 1)
                ins.then_inc(sig["pv_done"].sem, sig["pv_done"].step())

            for i in range(U + 8):
                if i < U:
                    scores(i)
                if 2 <= i < U + 2:
                    turn(i - 2)
                if 3 <= i < U + 3:
                    values(i - 3)
                if tail is not None and i >= H + 3 and (i - 3) % H == 1:
                    tail.turn(pe, (i - 3) // H - 1)
                if tail is not None and i >= H + 5 and (i - 5) % H == 1:
                    tail.product(pe, (i - 5) // H - 1)

        @block.vector
        def _(dve):
            link = core.dve_chain.link

            def maxima(u):
                qt, h = units[u]
                n = chunks(qt) * P
                dve.wait_ge(sig["s_done"].sem, sig["s_done"].at(u + 1))
                if u >= NS:
                    dve.wait_ge(sig["exp_done"].sem, sig["exp_done"].at(u - NS + 1))
                if not top:
                    ins = nc.vector.tensor_reduce(nmax[:, u % NS:u % NS + 1], s_bank[u % NS][:, :n], AXX, ALU.max)
                    link(dve, ins)
                    nc.vector.tensor_scalar(nmax[:, u % NS:u % NS + 1], nmax[:, u % NS:u % NS + 1], -scale, None,
                                            ALU.mult).then_inc(sig["max_done"].sem, sig["max_done"].step())
                    return
                if u >= 2:
                    dve.wait_ge(sig["prod_done"].sem, sig["prod_done"].at(u - 1))
                s, w, bst = s_sb[:, u % 2, :], work[:, u % 2, :], best[:, u % 2, :]
                link(dve, nc.vector.scalar_tensor_tensor(out=s, in0=s_bank[u % NS][:, :], scalar=scale,
                                                         in1=top[0](h, qt), op0=ALU.mult, op1=ALU.add))
                link(dve, nc.vector.max(bst[:, 0:8], s))
                nc.vector.tensor_scalar(nmax[:, u % NS:u % NS + 1], bst[:, 0:1], -1.0, None, ALU.mult).then_inc(
                    sig["max_done"].sem, sig["max_done"].step())
                for r in range(1, top[1] // 8):
                    link(dve, nc.vector.match_replace(w, bst[:, 8 * (r - 1):8 * r], s if r == 1 else w, -3.0e38))
                    ins = nc.vector.max(bst[:, 8 * r:8 * r + 8], w)
                    if r < top[1] // 8 - 1:
                        link(dve, ins)
                    else:
                        ins.then_inc(sig["s_taken"].sem, sig["s_taken"].step())

            def keep(u):
                qt, h = units[u]
                dve.wait_ge(sig["s_taken"].sem, sig["s_taken"].at(u + 1))
                dve.wait_ge(sig["exp_done"].sem, sig["exp_done"].at(u + 1))
                e = e_sb[:, u % NX, :]
                nc.vector.scalar_tensor_tensor(out=e, in0=s_sb[:, u % 2, :], scalar=best[:, u % 2, 31:32], in1=e,
                                               op0=ALU.is_ge, op1=ALU.mult,
                                               accum_out=den[:, qt % 2, h:h + 1]).then_inc(
                    sig["prod_done"].sem, sig["prod_done"].step())

            def copy(u):
                qt, h = units[u]
                n = chunks(qt) * P
                dve.wait_ge(sig["turn_done"].sem, sig["turn_done"].at(u + 1))
                if u >= NE:
                    dve.wait_ge(sig["pv_done"].sem, sig["pv_done"].at(u - NE + 1))
                nc.vector.tensor_copy(e_t[:, u % NE, :n], t_bank[u % 2][:, :n]).then_inc(
                    sig["turn_taken"].sem, sig["turn_taken"].step())

            def outputs(qt):
                dve.wait_ge(sig["exp_done"].sem, sig["exp_done"].at((qt + 1) * H))
                if top:
                    dve.wait_ge(sig["prod_done"].sem, sig["prod_done"].at((qt + 1) * H))
                link(dve, nc.vector.reciprocal(rden[:], den[:, qt % 2, :]))
                if gate is not None:
                    link(dve, nc.vector.tensor_tensor(rden[:], rden[:], gate, ALU.mult))
                dve.wait_ge(sig["pv_done"].sem, sig["pv_done"].at((qt + 1) * H))
                if tail is not None and qt >= 1:
                    dve.wait_ge(sig["t_turned"].sem, sig["t_turned"].at(tail.rounds() * qt))
                for j, bank in enumerate(o_bank):
                    hs = slice(j * HB, (j + 1) * HB)
                    ins = nc.vector.tensor_tensor(
                        o_sb[:, j * HB * hd:(j + 1) * HB * hd].rearrange("p (h d) -> p h d", d=hd),
                        bank[:, :HB * hd].rearrange("p (h d) -> p h d", d=hd), wide(rden[:, hs], hd, 2), ALU.mult)
                ins.then_inc(sig["o_done"].sem, sig["o_done"].step())
                if tail is None:
                    dve.wait_ge(sig["o_done"].sem, sig["o_done"].at(qt + 1))
                    tile = b * TB + qt
                    nc.vector.tensor_tensor(dst[:, tile, :], dst[:, tile, :], o_sb[:], ALU.add).then_inc(
                        sig["out_added"].sem, sig["out_added"].step())
                    dve.wait_ge(sig["out_added"].sem, sig["out_added"].at(qt + 1))

            for i in range(U + 8):
                if i < U:
                    maxima(i)
                if top and 1 <= i < U + 1:
                    keep(i - 1)
                if not top and 2 <= i < U + 2:
                    copy(i - 2)
                if i >= H + 3 and (i - 3) % H == 0:
                    outputs((i - 3) // H - 1)
                if tail is not None and i >= H + 6 and (i - 6) % H == 1:
                    tail.add(dve, (i - 6) // H - 1, b * TB + (i - 6) // H - 1)

        @block.scalar
        def _(act):
            def exps(u):
                qt, h = units[u]
                n = chunks(qt) * P
                act.wait_ge(sig["max_done"].sem, sig["max_done"].at(u + 1))
                if u >= NX:
                    act.wait_ge(sig["turn_done"].sem, sig["turn_done"].at(u - NX + 1))
                if h == 0 and qt >= 2:
                    act.wait_ge(sig["o_done"].sem, sig["o_done"].at(qt - 1))
                if top:
                    ins = nc.scalar.activation(e_sb[:, u % NX, :], s_sb[:, u % 2, :], ACT.Exp,
                                               bias=nmax[:, u % NS:u % NS + 1])
                else:
                    ins = nc.scalar.activation(e_sb[:, u % NX, :n], s_bank[u % NS][:, :n], ACT.Exp,
                                               bias=nmax[:, u % NS:u % NS + 1], scale=scale,
                                               accum_out=den[:, qt % 2, h:h + 1])
                ins.then_inc(sig["exp_done"].sem, sig["exp_done"].step())

            def copy(u):
                act.wait_ge(sig["turn_done"].sem, sig["turn_done"].at(u + 1))
                if u >= NE:
                    act.wait_ge(sig["pv_done"].sem, sig["pv_done"].at(u - NE + 1))
                nc.scalar.activation(e_t[:, u % NE, :], t_bank[u % 2][:, :], ACT.Copy).then_inc(
                    sig["turn_taken"].sem, sig["turn_taken"].step())

            for i in range(U + 8):
                if i < U:
                    exps(i)
                if top and 2 <= i < U + 2:
                    copy(i - 2)
                if tail is not None and i >= H + 3 and (i - 3) % H == 1:
                    tail.copy(act, (i - 3) // H - 1)
    core.end_region()



def context_attention(core, ctx, units, G, q_of, k_of, v_of, hd, scale, ident, tail=None, mask=None, stable=False,
                      finish=None):
    nc, sig = core.nc, core.sig

    def sb(name, shape, dt=F32):
        return ctx.enter_context(nc.sbuf_tensor(f"{name}_{nc.next_id()}", shape, dt))

    in_bank = {C: [slice(0, G)], 8: [slice(j, H, 4) for j in range(4)],
               64: [slice(8 * j + p, 8 * j + 8, 2) for j in range(2) for p in range(2)]}[hd]
    place = {g: (j, n) for j, s in enumerate(in_bank) for n, g in enumerate(range(s.start, s.stop, s.step or 1))}
    n_block = G // len(in_bank)
    s_bank = core.bank[0:4]
    t_bank = (core.bank[4], core.bank[7])
    o_bank = core.bank[5:7]
    e_sb = sb("ce_sb", [P, G, KC])
    s_sb = sb("cs_sb", [P, G, KC])
    t_sb = sb("ct_sb", [P, G, KC]) if stable else None
    e_t = sb("ce_t", [P, G, P])
    mx = sb("cmx", [P, G])
    den = sb("cden", [P, G])
    rden = sb("crden", [P, G])
    o_sb = sb("co_sb", [P, G * hd])
    HB = min(G, BANK // hd)
    NQ = G // 4
    if tail is not None:
        tail.o_sb = o_sb
    NU = len(units)

    with nc.Block() as block:
        @block.tensor
        def _(pe):
            def scores(u):
                if u >= 1:
                    pe.wait_ge(sig["s_taken"].sem, sig["s_taken"].at(u))
                for g in range(G):
                    j, n = place[g]
                    ins = nc.tensor.matmul(s_bank[j][:, n * KC:(n + 1) * KC],
                                           q_of(units[u], g), k_of(units[u], g), start=True, stop=True)
                ins.then_inc(sig["s_done"].sem, sig["s_done"].step())

            def turns(u):
                pe.wait_ge(sig["exp_done"].sem, sig["exp_done"].at(u + 1))
                for j in range(NQ):
                    n = NQ * u + j
                    if n >= 2:
                        pe.wait_ge(sig["turn_taken"].sem, sig["turn_taken"].at(n - 1))
                    for g in range(4 * j, 4 * j + 4):
                        ins = nc.tensor.transpose(t_bank[n % 2][:KC, (g % 4) * P:(g % 4 + 1) * P],
                                                  e_sb[:, g, :], ident)
                    ins.then_inc(sig["turn_done"].sem, sig["turn_done"].step())

            def values(u):
                if u >= 1:
                    pe.wait_ge(sig["o_done"].sem, sig["o_done"].at(u))
                    if tail is not None:
                        pe.wait_ge(sig["out_added"].sem, sig["out_added"].at(u))
                pe.wait_ge(sig["turn_taken"].sem, sig["turn_taken"].at(NQ * (u + 1)))
                for g in range(G):
                    ins = nc.tensor.matmul(o_bank[g // HB][:, (g % HB) * hd:(g % HB + 1) * hd], e_t[:KC, g, :],
                                           v_of(units[u], g), start=True, stop=True)
                ins.then_inc(sig["pv_done"].sem, sig["pv_done"].step())

            scores(0)
            for u in range(NU):
                if u + 1 < NU:
                    scores(u + 1)
                turns(u)
                if tail is not None and u >= 1:
                    tail.product(pe, u - 1)
                values(u)
                if tail is not None:
                    tail.turn(pe, u)
            if tail is not None:
                tail.product(pe, NU - 1)

        @block.vector
        def _(dve):
            link = core.dve_chain.link

            def front(u):
                dve.wait_ge(sig["s_done"].sem, sig["s_done"].at(u + 1))
                for j, g in enumerate(in_bank):
                    src = s_bank[j][:, :n_block * KC].rearrange("p (g k) -> p g k", k=KC)
                    if stable:
                        nc.vector.tensor_scalar(s_sb[:, g, :], src, scale, 0.0, ALU.mult, ALU.max)
                        ins = nc.vector.tensor_scalar(t_sb[:, g, :], src, scale, 0.0, ALU.mult, ALU.min)
                    elif mask is not None:
                        ins = nc.vector.scalar_tensor_tensor(out=s_sb[:, g, :], in0=src, scalar=scale,
                                                             in1=mask[0](units[u], g), op0=ALU.mult, op1=ALU.mult)
                    else:
                        ins = nc.vector.tensor_scalar(s_sb[:, g, :], src, scale, None, ALU.mult)
                ins.then_inc(sig["s_taken"].sem, sig["s_taken"].step())
                dve.wait_ge(sig["s_taken"].sem, sig["s_taken"].at(u + 1))
                if stable:
                    link(dve, nc.vector.tensor_scalar(t_sb[:], t_sb[:], -1.0, None, ALU.add))
                    link(dve, nc.vector.reciprocal(t_sb[:], t_sb[:]))
                    if u >= 1:
                        dve.wait_ge(sig["turn_done"].sem, sig["turn_done"].at(NQ * u))
                    nc.vector.tensor_tensor(e_sb[:], s_sb[:], t_sb[:], ALU.subtract).then_inc(
                        sig["exp_done"].sem, sig["exp_done"].step())
                    return
                if mask is not None:
                    link(dve, nc.vector.tensor_tensor(s_sb[:], s_sb[:], mask[1](units[u], slice(0, G)), ALU.add))
                link(dve, nc.vector.tensor_reduce(mx[:], s_sb[:], AXX, ALU.max))
                nc.vector.tensor_tensor(s_sb[:], s_sb[:], wide(mx[:], KC, 2), ALU.subtract).then_inc(
                    sig["max_done"].sem, sig["max_done"].step())

            def back(u):
                dve.wait_ge(sig["exp_done"].sem, sig["exp_done"].at(u + 1))
                link(dve, nc.vector.tensor_reduce(den[:], e_sb[:], AXX, ALU.add))
                link(dve, nc.vector.reciprocal(rden[:], den[:]))
                dve.wait_ge(sig["pv_done"].sem, sig["pv_done"].at(u + 1))
                if tail is not None and u >= 1:
                    dve.wait_ge(sig["t_turned"].sem, sig["t_turned"].at(tail.rounds() * u))
                for j in range(-(-G // HB)):
                    ins = nc.vector.tensor_tensor(
                        o_sb[:, j * HB * hd:(j + 1) * HB * hd].rearrange("p (h d) -> p h d", d=hd),
                        o_bank[j][:, :HB * hd].rearrange("p (h d) -> p h d", d=hd),
                        wide(rden[:, j * HB:(j + 1) * HB], hd, 2), ALU.mult)
                ins.then_inc(sig["o_done"].sem, sig["o_done"].step())
                if finish is not None:
                    dve.wait_ge(sig["o_done"].sem, sig["o_done"].at(u + 1))
                    finish(dve, u, o_sb)

            for u in range(NU):
                front(u)
                if tail is not None and u >= 1:
                    tail.add(dve, u - 1, units[u - 1])
                back(u)
            if tail is not None:
                tail.add(dve, NU - 1, units[NU - 1])

        @block.scalar
        def _(act):
            for u in range(NU):
                if not stable:
                    act.wait_ge(sig["max_done"].sem, sig["max_done"].at(u + 1))
                    if u >= 1:
                        act.wait_ge(sig["turn_done"].sem, sig["turn_done"].at(NQ * u))
                    nc.scalar.activation(e_sb[:], s_sb[:], ACT.Exp).then_inc(
                        sig["exp_done"].sem, sig["exp_done"].step())
                for j in range(NQ):
                    n = NQ * u + j
                    act.wait_ge(sig["turn_done"].sem, sig["turn_done"].at(n + 1))
                    if u >= 1:
                        act.wait_ge(sig["pv_done"].sem, sig["pv_done"].at(u))
                    nc.scalar.activation(e_t[:KC, 4 * j:4 * j + 4, :],
                                         t_bank[n % 2][:KC, :].rearrange("p (g q) -> p g q", q=P),
                                         ACT.Copy).then_inc(sig["turn_taken"].sem, sig["turn_taken"].step())
                if tail is not None:
                    tail.copy(act, u)

        @block.gpsimd
        def _(pool):
            if finish is not None:
                for u in range(NU):
                    pool.wait_ge(sig["norm_stats"].sem, sig["norm_stats"].at(u + 1))
                    nc.gpsimd.tensor_tensor(core.rstd[:, 0:G], core.spread[:, 0:G], core.minus_half[:, 0:G],
                                            ALU.pow).then_inc(sig["norm_scale"].sem, sig["norm_scale"].step())
    core.end_region()



def route(core, ctx, wr, row, k, tri, tiles=NT):
    nc, sig = core.nc, core.sig
    E = 8

    def sb(name, shape):
        return ctx.enter_context(nc.sbuf_tensor(f"{name}_{nc.next_id()}", shape, F32))

    logits, gates, ex = sb("logits", [P, NT, E]), sb("gates", [P, NT, E]), sb("gate_exp", [P, NT, E])
    larger, equal = sb("larger", [P, NT, E, E]), sb("equal", [P, NT, E, E])
    rank, mx, tot = sb("rank", [P, NT, E]), sb("gate_max", [P, NT]), sb("gate_sum", [P, NT])
    with nc.Block() as block:
        @block.tensor
        def _(pe):
            for t in range(NT):
                out = core.bank[0][:, t * E:(t + 1) * E]
                ins = nc.tensor.matmul(out, core.xn_t[:, t * P:(t + 1) * P], wr, start=True, stop=row is None)
                if row is not None:
                    ins = nc.tensor.matmul(out, core.ones_row[0:1, :], row, start=False, stop=True)
            ins.then_inc(sig["mm_done"].sem, sig["mm_done"].step())

        @block.vector
        def _(dve):
            link = core.dve_chain.link
            dve.wait_ge(sig["mm_done"].sem, sig["mm_done"].at(1))
            link(dve, nc.vector.tensor_copy(logits[:], core.bank[0][:, :NT * E].rearrange("p (t e) -> p t e", e=E)))
            mine = wide(logits[:], E, 3)
            other = wide(logits[:], E, 2)
            nc.vector.tensor_tensor(larger[:], other, mine, ALU.is_gt)
            link(dve, nc.vector.tensor_tensor(equal[:], other, mine, ALU.is_equal))
            link(dve, nc.vector.tensor_tensor(
                equal[:].rearrange("p t e j -> p t (e j)"), equal[:].rearrange("p t e j -> p t (e j)"),
                wide(tri, NT, 1), ALU.mult))
            link(dve, nc.vector.tensor_tensor(larger[:], larger[:], equal[:], ALU.add))
            nc.vector.tensor_reduce(mx[:], logits[:], AXX, ALU.max)
            link(dve, nc.vector.tensor_reduce(rank[:], larger[:], AXX, ALU.add))
            nc.vector.tensor_tensor(ex[:], logits[:], wide(mx[:], E, 2), ALU.subtract).then_inc(
                sig["max_done"].sem, sig["max_done"].step())
            dve.wait_ge(sig["exp_done"].sem, sig["exp_done"].at(1))
            link(dve, nc.vector.tensor_scalar(rank[:], rank[:], float(k), None, ALU.is_lt))
            link(dve, nc.vector.tensor_tensor(gates[:], ex[:], rank[:], ALU.mult))
            link(dve, nc.vector.tensor_reduce(tot[:], gates[:], AXX, ALU.add))
            link(dve, nc.vector.reciprocal(tot[:], tot[:]))
            nc.vector.tensor_tensor(gates[:], gates[:], wide(tot[:], E, 2), ALU.mult)

        @block.scalar
        def _(act):
            act.wait_ge(sig["max_done"].sem, sig["max_done"].at(1))
            nc.scalar.activation(ex[:], ex[:], ACT.Exp).then_inc(sig["exp_done"].sem, sig["exp_done"].step())
    core.end_region()
    return gates



def feed_forward(core, ctx, dst, jobs, gates=None):
    nc, sig = core.nc, core.sig
    hid = ctx.enter_context(nc.sbuf_tensor(f"hid_{nc.next_id()}", [P, 2, 4, BANK], F32))
    silu = ctx.enter_context(nc.sbuf_tensor(f"silu_{nc.next_id()}", [P, 2, BANK], F32))
    runs = [(j, half) for j in jobs for half in range(B)]
    chunks = [(r, c) for r, (j, half) in enumerate(runs) for c in range(j[5])]
    first = {r: sum(j[5] for j, _ in runs[:r]) for r in range(len(runs) + 1)}
    gated = [n for n, (r, c) in enumerate(chunks) if runs[r][0][1] is not None]

    def hidden_ready(eng, n):
        if n in gated:
            eng.wait_ge(sig["prod_done"].sem, sig["prod_done"].at(gated.index(n) + 1))
        else:
            eng.wait_ge(sig["act_done"].sem, sig["act_done"].at(n + 1))

    with nc.Block() as block:
        @block.tensor
        def _(pe):
            def up(n):
                r, c = chunks[n]
                (w, second, down, bias, fn, nch, gate), half = runs[r]
                if n >= 2:
                    hidden_ready(pe, n - 2)
                x = core.xn_t[:, half * T:(half + 1) * T]
                m = w(c).shape[-1]
                ins = nc.tensor.matmul(core.bank[n % 2][:m, :], w(c), x, start=True, stop=True)
                if second is not None:
                    ins = nc.tensor.matmul(core.bank[2 + n % 2][:m, :], second(c), x, start=True, stop=True)
                ins.then_inc(sig["mm_done"].sem, sig["mm_done"].step())

            def down_part(r):
                (w, second, down, bias, fn, nch, gate), half = runs[r]
                hidden_ready(pe, first[r + 1] - 1)
                if r >= 2:
                    pe.wait_ge(sig["y_added"].sem, sig["y_added"].at(r - 1))
                m = w(0).shape[-1]
                for t in range(TB):
                    out = core.bank[4 + r % 2][:, t * P:(t + 1) * P]
                    for c in range(nch):
                        ins = nc.tensor.matmul(out, hid[:m, r % 2, c, t * P:(t + 1) * P], down(c),
                                               start=c == 0, stop=c == nch - 1)
                ins.then_inc(sig["y_done"].sem, sig["y_done"].step())

            for n in range(len(chunks)):
                r, c = chunks[n]
                up(n)
                if r >= 1 and c == runs[r][0][5] - 1:
                    down_part(r - 1)
            down_part(len(runs) - 1)

        @block.scalar
        def _(act):
            for n, (r, c) in enumerate(chunks):
                (w, second, down, bias, fn, nch, gate), half = runs[r]
                act.wait_ge(sig["mm_done"].sem, sig["mm_done"].at(n + 1))
                m = w(c).shape[-1]
                if second is not None:
                    if n >= 2:
                        act.wait_ge(sig["prod_done"].sem, sig["prod_done"].at(gated.index(n) - 1))
                    out = silu[:m, n % 2, :]
                else:
                    if r >= 2:
                        act.wait_ge(sig["y_done"].sem, sig["y_done"].at(r - 1))
                    out = hid[:m, r % 2, c, :]
                nc.scalar.activation(out, core.bank[n % 2][:m, :], fn, bias=0.0 if bias is None else bias(c)).then_inc(
                    sig["act_done"].sem, sig["act_done"].step())

        @block.vector
        def _(dve):
            def add(r):
                (w, second, down, bias, fn, nch, gate), half = runs[r]
                dve.wait_ge(sig["y_done"].sem, sig["y_done"].at(r + 1))
                if r >= 1:
                    dve.wait_ge(sig["y_added"].sem, sig["y_added"].at(r))
                bank = core.bank[4 + r % 2]
                if gate is None:
                    ins = nc.vector.tensor_tensor(dst[:, half * TB:(half + 1) * TB, :].rearrange("p t c -> p (t c)"),
                                                  dst[:, half * TB:(half + 1) * TB, :].rearrange("p t c -> p (t c)"),
                                                  bank[:], ALU.add)
                else:
                    for t in range(TB):
                        tile = half * TB + t
                        ins = nc.vector.scalar_tensor_tensor(
                            out=dst[:, tile, :], in0=bank[:, t * P:(t + 1) * P],
                            scalar=gates[:, tile, gate:gate + 1], in1=dst[:, tile, :], op0=ALU.mult, op1=ALU.add)
                ins.then_inc(sig["y_added"].sem, sig["y_added"].step())

            for n, (r, c) in enumerate(chunks):
                (w, second, down, bias, fn, nch, gate), half = runs[r]
                if second is not None:
                    dve.wait_ge(sig["act_done"].sem, sig["act_done"].at(n + 1))
                    if r >= 2:
                        dve.wait_ge(sig["y_done"].sem, sig["y_done"].at(r - 1))
                    m = w(c).shape[-1]
                    nc.vector.tensor_tensor(hid[:m, r % 2, c, :], silu[:m, n % 2, :], core.bank[2 + n % 2][:m, :],
                                            ALU.mult).then_inc(sig["prod_done"].sem, sig["prod_done"].step())
                if r >= 1 and c == nch - 1:
                    add(r - 1)
            add(len(runs) - 1)
    core.end_region()


def add_rows(core, dst, row):
    nc, sig = core.nc, core.sig
    with nc.Block() as block:
        @block.tensor
        def _(pe):
            for t in range(TB):
                ins = nc.tensor.matmul(core.bank[7][:, t * P:(t + 1) * P], core.ones_row[0:1, :], row,
                                       start=True, stop=True)
            ins.then_inc(sig["mm_done"].sem, sig["mm_done"].step())

        @block.vector
        def _(dve):
            dve.wait_ge(sig["mm_done"].sem, sig["mm_done"].at(1))
            for half in range(B):
                nc.vector.tensor_tensor(dst[:, half * TB:(half + 1) * TB, :].rearrange("p t c -> p (t c)"),
                                        dst[:, half * TB:(half + 1) * TB, :].rearrange("p t c -> p (t c)"),
                                        core.bank[7][:], ALU.add)
    core.end_region()



def gated_recurrence(core, ctx, w_hg, ident):
    nc, sig = core.nc, core.sig

    def sb(name):
        return ctx.enter_context(nc.sbuf_tensor(f"{name}_{nc.next_id()}", [P, B, T], F32))

    decay, update, low, value, state = sb("decay"), sb("update"), sb("low"), sb("value"), sb("state")
    with nc.Block() as block:
        @block.tensor
        def _(pe):
            for b in range(B):
                for j in range(2):
                    ins = nc.tensor.matmul(core.bank[2 * b + j][:], w_hg[:, j * P:(j + 1) * P],
                                           core.xn_t[:, b * T:(b + 1) * T], start=True, stop=True)
                ins.then_inc(sig["mm_done"].sem, sig["mm_done"].step())
            for b in range(B):
                pe.wait_ge(sig["prod_done"].sem, sig["prod_done"].at(b + 1))
                for t in range(TB):
                    ins = nc.tensor.transpose(core.bank[4 + b][:, t * P:(t + 1) * P],
                                              state[:, b, t * P:(t + 1) * P], ident)
                ins.then_inc(sig["turn_done"].sem, sig["turn_done"].step())

        @block.scalar
        def _(act):
            for b in range(B):
                act.wait_ge(sig["mm_done"].sem, sig["mm_done"].at(b + 1))
                nc.scalar.activation(decay[:, b, :], core.bank[2 * b + 1][:], ACT.Sigmoid, scale=-1.0)
                nc.scalar.activation(update[:, b, :], core.bank[2 * b + 1][:], ACT.Sigmoid)
                act.wait_ge(sig["aux_dve"].sem, sig["aux_dve"].at(b + 1))
                nc.scalar.activation(value[:, b, :], low[:, b, :], ACT.Sigmoid).then_inc(
                    sig["act_done"].sem, sig["act_done"].step())

        @block.vector
        def _(dve):
            link = core.dve_chain.link
            for b in range(B):
                dve.wait_ge(sig["mm_done"].sem, sig["mm_done"].at(b + 1))
                nc.vector.tensor_scalar(low[:, b, :], core.bank[2 * b][:], 0.0, None, ALU.min).then_inc(
                    sig["aux_dve"].sem, sig["aux_dve"].step())
            for b in range(B):
                dve.wait_ge(sig["act_done"].sem, sig["act_done"].at(b + 1))
                link(dve, nc.vector.scalar_tensor_tensor(out=value[:, b, :], in0=core.bank[2 * b][:], scalar=0.0,
                                                         in1=value[:, b, :], op0=ALU.max, op1=ALU.add))
                link(dve, nc.vector.tensor_tensor(value[:, b, :], value[:, b, :], update[:, b, :], ALU.mult))
                nc.vector.tensor_tensor_scan(out=state[:, b, :], data0=decay[:, b, :], data1=value[:, b, :],
                                             initial=0.0, op0=ALU.mult, op1=ALU.add).then_inc(
                    sig["prod_done"].sem, sig["prod_done"].step())
            for b in range(B):
                dve.wait_ge(sig["turn_done"].sem, sig["turn_done"].at(b + 1))
                half = core.x_sb[:, b * TB:(b + 1) * TB, :].rearrange("p t c -> p (t c)")
                nc.vector.tensor_tensor(half, half, core.bank[4 + b][:], ALU.add)
    core.end_region()


def state_space(core, ctx, w):
    nc, sig = core.nc, core.sig
    S = 16

    def sb(name, shape):
        return ctx.enter_context(nc.sbuf_tensor(f"{name}_{nc.next_id()}", shape, F32))

    z, low = sb("delta_in", [P, B, T]), sb("delta_low", [P, B, T])
    dbar, decay, bt, ct, hs = (sb(n, [S, B, T]) for n in ("dbar", "ss_decay", "ss_bt", "ss_ct", "ss_h"))
    sa, ysum = sb("ss_a", [S, 1]), sb("ss_y", [P, NT])
    with nc.Block() as block:
        @block.tensor
        def _(pe):
            for b in range(B):
                x = core.xn_t[:, b * T:(b + 1) * T]
                nc.tensor.matmul(core.bank[b][:], w["ss_wd"], x, start=True, stop=True)
                nc.tensor.matmul(core.bank[2 + b][:S, :], w["ss_wb"], x, start=True, stop=True)
                ins = nc.tensor.matmul(core.bank[4 + b][:S, :], w["ss_wc"], x, start=True, stop=True)
                ins.then_inc(sig["mm_done"].sem, sig["mm_done"].step())
            nc.tensor.matmul(core.bank[6][:S, 0:1], w["ss_a"], w["mean_col"][:, 0:1], start=True, stop=True).then_inc(
                sig["aux_pe"].sem, sig["aux_pe"].step())
            for b in range(B):
                pe.wait_ge(sig["prod_done"].sem, sig["prod_done"].at(b + 1))
                nc.tensor.matmul(core.bank[b][:S, :], w["mean_col"], z[:, b, :], start=True, stop=True).then_inc(
                    sig["s_done"].sem, sig["s_done"].step())
            for b in range(B):
                pe.wait_ge(sig["o_done"].sem, sig["o_done"].at(b + 1))
                if b == 0:
                    pe.wait_ge(sig["aux_dve"].sem, sig["aux_dve"].at(1))
                for t in range(TB):
                    ins = nc.tensor.matmul(core.bank[6 + b][:, t:t + 1],
                                           hs[:, b, t * P:(t + 1) * P], w["ones"][:S, 0:1], start=True, stop=True)
                ins.then_inc(sig["pv_done"].sem, sig["pv_done"].step())
            for b in range(B):
                pe.wait_ge(sig["act_done"].sem, sig["act_done"].at(2 * b + 2))
                for t in range(TB):
                    tile = b * TB + t
                    nc.tensor.matmul(core.bank[2 + b][:, t * P:(t + 1) * P], core.xn_t[:, tile * P:(tile + 1) * P],
                                     w["ss_wo"], start=True, stop=True)
                    ins = nc.tensor.matmul(core.bank[4 + b][:, t * P:(t + 1) * P], core.ones_row[0:1, :],
                                           w["ss_bo"], start=True, stop=True)
                ins.then_inc(sig["y_done"].sem, sig["y_done"].step())

        @block.scalar
        def _(act):
            for b in range(B):
                act.wait_ge(sig["mm_done"].sem, sig["mm_done"].at(b + 1))
                nc.scalar.activation(bt[:, b, :], core.bank[2 + b][:S, :], ACT.Identity, bias=w["ss_bb"][:S, :]).then_inc(
                    sig["act_done"].sem, sig["act_done"].step())
                nc.scalar.activation(ct[:, b, :], core.bank[4 + b][:S, :], ACT.Identity, bias=w["ss_bc"][:S, :]).then_inc(
                    sig["act_done"].sem, sig["act_done"].step())
            for b in range(B):
                act.wait_ge(sig["aux_dve"].sem, sig["aux_dve"].at(b + 2))
                nc.scalar.activation(low[:, b, :], low[:, b, :], ACT.Exp, scale=-1.0).then_inc(
                    sig["aux_act"].sem, sig["aux_act"].step())
            for b in range(B):
                act.wait_ge(sig["aux_act"].sem, sig["aux_act"].at(b + 1))
                nc.scalar.activation(low[:, b, :], low[:, b, :], ACT.Ln, bias=1.0).then_inc(
                    sig["exp_done"].sem, sig["exp_done"].step())
            act.wait_ge(sig["aux_dve"].sem, sig["aux_dve"].at(1))
            nc.scalar.activation(sa[:], sa[:], ACT.Sigmoid).then_inc(sig["max_done"].sem, sig["max_done"].step())

        @block.vector
        def _(dve):
            link = core.dve_chain.link
            dve.wait_ge(sig["aux_pe"].sem, sig["aux_pe"].at(1))
            nc.vector.tensor_copy(sa[:], core.bank[6][:S, 0:1]).then_inc(sig["aux_dve"].sem, sig["aux_dve"].step())
            for b in range(B):
                link(dve, nc.vector.tensor_scalar(z[:, b, :], core.bank[b][:], w["ss_bd"], None, ALU.add))
                nc.vector.scalar_tensor_tensor(out=low[:, b, :], in0=z[:, b, :], scalar=-1.0, in1=z[:, b, :],
                                               op0=ALU.mult, op1=ALU.max).then_inc(
                    sig["aux_dve"].sem, sig["aux_dve"].step())
            for b in range(B):
                dve.wait_ge(sig["exp_done"].sem, sig["exp_done"].at(b + 1))
                nc.vector.scalar_tensor_tensor(out=z[:, b, :], in0=z[:, b, :], scalar=0.0, in1=low[:, b, :],
                                               op0=ALU.max, op1=ALU.add).then_inc(
                    sig["prod_done"].sem, sig["prod_done"].step())
            dve.wait_ge(sig["max_done"].sem, sig["max_done"].at(1))
            dve.wait_ge(sig["act_done"].sem, sig["act_done"].at(2 * B))
            for b in range(B):
                dve.wait_ge(sig["s_done"].sem, sig["s_done"].at(b + 1))
                nc.vector.tensor_scalar(decay[:, b, :], core.bank[b][:S, :], -1.0, 1.0, ALU.mult, ALU.add)
                link(dve, nc.vector.tensor_tensor(bt[:, b, :], core.bank[b][:S, :], bt[:, b, :], ALU.mult))
                link(dve, nc.vector.tensor_scalar(bt[:, b, :], bt[:, b, :], sa[:], None, ALU.mult))
                link(dve, nc.vector.tensor_tensor_scan(out=hs[:, b, :], data0=decay[:, b, :], data1=bt[:, b, :],
                                                       initial=0.0, op0=ALU.mult, op1=ALU.add))
                nc.vector.tensor_tensor(hs[:, b, :], hs[:, b, :], ct[:, b, :], ALU.mult).then_inc(
                    sig["o_done"].sem, sig["o_done"].step())
            for b in range(B):
                dve.wait_ge(sig["pv_done"].sem, sig["pv_done"].at(b + 1))
                link(dve, nc.vector.tensor_copy(ysum[:, b * TB:(b + 1) * TB], core.bank[6 + b][:, 0:TB]))
                dve.wait_ge(sig["y_done"].sem, sig["y_done"].at(b + 1))
                for t in range(TB):
                    tile = b * TB + t
                    ins = nc.vector.scalar_tensor_tensor(
                        out=core.x_sb[:, tile, :], in0=core.bank[2 + b][:, t * P:(t + 1) * P],
                        scalar=ysum[:, tile:tile + 1], in1=core.x_sb[:, tile, :], op0=ALU.mult, op1=ALU.add)
                link(dve, ins)
                half = core.x_sb[:, b * TB:(b + 1) * TB, :].rearrange("p t c -> p (t c)")
                nc.vector.tensor_tensor(half, half, core.bank[4 + b][:], ALU.add)
    core.end_region()



def bit_feed_forward(core, ctx, w1_t, w2_t, b1_rows, b2_row, ident, ones):
    nc, sig = core.nc, core.sig
    F = 4 * P

    def sb(name, shape, dt=F32):
        return ctx.enter_context(nc.sbuf_tensor(f"{name}_{nc.next_id()}", shape, dt))

    asum, wmean, wscale = sb("asum", [P, 2]), sb("wmean", [P, 2]), sb("wscale", [P, 2])
    wtmp = sb("wtmp", [P, F])
    w1q, w2q = sb("w1q", [P, F], BF16), sb("w2q", [P, F], BF16)
    sq = sb("sq", [P, NT, C])
    ms, amax, qscale, step1 = (sb(n, [P, NT]) for n in ("ms", "amax", "qscale", "step1"))
    ms2, amax2, qscale2, step2, r2, inv2 = (sb(n, [P, NT]) for n in ("ms2", "amax2", "qscale2", "step2", "r2", "inv2"))
    xq_t = sb("xq_t", [P, NT, P], BF16)
    hid = sb("bhid", [P, 2, F])
    sq2 = sb("sq2", [P, F])
    hq_t = sb("hq_t", [P, 2, 4, P], BF16)

    with nc.Block() as block:
        @block.vector
        def _(dve):
            link = core.dve_chain.link
            nc.vector.tensor_reduce(asum[:, 0:1], w1_t, AXX, ALU.add, apply_absolute_value=True)
            nc.vector.tensor_reduce(asum[:, 1:2], w2_t, AXX, ALU.add, apply_absolute_value=True).then_inc(
                sig["aux_dve"].sem, sig["aux_dve"].step())
            link(dve, nc.vector.tensor_tensor(sq[:], core.xn[:], core.xn[:], ALU.mult))
            link(dve, nc.vector.tensor_reduce(ms[:], sq[:], AXX, ALU.add))
            nc.vector.tensor_scalar(core.spread[:], ms[:], 1.0 / C, 1e-5, ALU.mult, ALU.add).then_inc(
                sig["norm_stats"].sem, sig["norm_stats"].step())
            dve.wait_ge(sig["aux_pe"].sem, sig["aux_pe"].at(1))
            link(dve, nc.vector.tensor_scalar(wmean[:], core.bank[0][:, 0:2], 1.0 / (C * F), 1e-5, ALU.mult, ALU.max))
            link(dve, nc.vector.reciprocal(wscale[:], wmean[:]))
            for j, (w, q) in enumerate(((w1_t, w1q), (w2_t, w2q))):
                link(dve, nc.vector.tensor_scalar(wtmp[:], w, wscale[:, j:j + 1], ROUND, ALU.mult, ALU.add))
                link(dve, nc.vector.tensor_scalar(wtmp[:], wtmp[:], -ROUND, 1.0, ALU.add, ALU.min))
                link(dve, nc.vector.tensor_scalar(q[:], wtmp[:], -1.0, None, ALU.max))
            dve.wait_ge(sig["norm_scale"].sem, sig["norm_scale"].at(1))
            link(dve, nc.vector.tensor_tensor(core.xn[:], core.xn[:], wide(core.rstd[:], C, 2), ALU.mult))
            link(dve, nc.vector.tensor_reduce(amax[:], core.xn[:], AXX, ALU.max, apply_absolute_value=True))
            link(dve, nc.vector.tensor_scalar(amax[:], amax[:], 1e-5, None, ALU.max))
            link(dve, nc.vector.reciprocal(qscale[:], amax[:]))
            link(dve, nc.vector.tensor_scalar(qscale[:], qscale[:], 127.0, None, ALU.mult))
            link(dve, nc.vector.tensor_scalar(step1[:], amax[:], wmean[:, 0:1], 1.0 / 127.0, ALU.mult, ALU.mult))
            link(dve, nc.vector.tensor_tensor(core.xn[:], core.xn[:], wide(qscale[:], C, 2), ALU.mult))
            link(dve, nc.vector.tensor_scalar(core.xn[:], core.xn[:], ROUND, None, ALU.add))
            nc.vector.tensor_scalar(core.xn[:], core.xn[:], -ROUND, None, ALU.add).then_inc(
                sig["norm_rows"].sem, sig["norm_rows"].step())

        @block.gpsimd
        def _(pool):
            pool.wait_ge(sig["norm_stats"].sem, sig["norm_stats"].at(1))
            nc.gpsimd.tensor_tensor(core.rstd[:], core.spread[:], core.minus_half[:], ALU.pow).then_inc(
                sig["norm_scale"].sem, sig["norm_scale"].step())

        @block.tensor
        def _(pe):
            pe.wait_ge(sig["aux_dve"].sem, sig["aux_dve"].at(1))
            nc.tensor.matmul(core.bank[0][:, 0:2], ones, asum[:], start=True, stop=True).then_inc(
                sig["aux_pe"].sem, sig["aux_pe"].step())
            pe.wait_ge(sig["norm_rows"].sem, sig["norm_rows"].at(1))
            for t in range(NT):
                ins = nc.tensor.transpose(core.bank[1 + t // TB][:, (t % TB) * P:(t % TB + 1) * P],
                                          core.xn[:, t, :], ident)
            ins.then_inc(sig["norm_turned"].sem, sig["norm_turned"].step())

        @block.scalar
        def _(act):
            act.wait_ge(sig["norm_turned"].sem, sig["norm_turned"].at(1))
            for b in range(B):
                nc.scalar.activation(xq_t[:, b * TB:(b + 1) * TB, :].rearrange("p t c -> p (t c)"),
                                     core.bank[1 + b][:], ACT.Copy)
    core.end_region()

    with nc.Block() as block:
        @block.tensor
        def _(pe):
            def first(t):
                if t >= 2:
                    pe.wait_ge(sig["s_taken"].sem, sig["s_taken"].at(t - 1))
                nc.tensor.matmul(core.bank[t % 2][:], xq_t[:, t, :], w1q[:], start=True, stop=True).then_inc(
                    sig["mm_done"].sem, sig["mm_done"].step())

            first(0)
            for t in range(NT):
                if t + 1 < NT:
                    first(t + 1)
                pe.wait_ge(sig["prod_done"].sem, sig["prod_done"].at(t + 1))
                if t >= 2:
                    pe.wait_ge(sig["turn_taken"].sem, sig["turn_taken"].at(t - 1))
                for c in range(4):
                    ins = nc.tensor.transpose(core.bank[2 + t % 2][:, c * P:(c + 1) * P],
                                              hid[:, t % 2, c * P:(c + 1) * P], ident)
                ins.then_inc(sig["turn_done"].sem, sig["turn_done"].step())
                pe.wait_ge(sig["turn_taken"].sem, sig["turn_taken"].at(t + 1))
                if t >= 2:
                    pe.wait_ge(sig["y_added"].sem, sig["y_added"].at(t - 1))
                for c in range(4):
                    nc.tensor.matmul(core.bank[4 + t % 2][:, 0:C], hq_t[:, t % 2, c, :], w2q[:, c * P:(c + 1) * P],
                                     start=c == 0, stop=c == 3)
                nc.tensor.matmul(core.bank[6 + t % 2][:, 0:C], core.ones_row[0:1, :], b2_row, start=True,
                                 stop=True).then_inc(sig["y_done"].sem, sig["y_done"].step())

        @block.scalar
        def _(act):
            for t in range(NT):
                act.wait_ge(sig["s_taken"].sem, sig["s_taken"].at(t + 1))
                nc.scalar.activation(hid[:, t % 2, :], hid[:, t % 2, :], ACT.Gelu).then_inc(
                    sig["act_done"].sem, sig["act_done"].step())
                act.wait_ge(sig["turn_done"].sem, sig["turn_done"].at(t + 1))
                if t >= 2:
                    act.wait_ge(sig["y_done"].sem, sig["y_done"].at(t - 1))
                nc.scalar.activation(hq_t[:, t % 2, :, :].rearrange("p c q -> p (c q)"), core.bank[2 + t % 2][:],
                                     ACT.Copy).then_inc(sig["turn_taken"].sem, sig["turn_taken"].step())

        @block.gpsimd
        def _(pool):
            for t in range(NT):
                pool.wait_ge(sig["norm_stats"].sem, sig["norm_stats"].at(t + 1))
                nc.gpsimd.tensor_tensor(r2[:, t:t + 1], ms2[:, t:t + 1], core.minus_half[:, 0:1], ALU.pow).then_inc(
                    sig["norm_scale"].sem, sig["norm_scale"].step())

        @block.vector
        def _(dve):
            link = core.dve_chain.link

            def col(a, t):
                return a[:, t:t + 1]

            def dequant(t):
                dve.wait_ge(sig["mm_done"].sem, sig["mm_done"].at(t + 1))
                if t >= 2:
                    dve.wait_ge(sig["turn_done"].sem, sig["turn_done"].at(t - 1))
                nc.vector.scalar_tensor_tensor(out=hid[:, t % 2, :], in0=core.bank[t % 2][:], scalar=col(step1, t),
                                               in1=b1_rows, op0=ALU.mult, op1=ALU.add).then_inc(
                    sig["s_taken"].sem, sig["s_taken"].step())

            for t in range(NT):
                dequant(t)
                h = hid[:, t % 2, :]
                dve.wait_ge(sig["act_done"].sem, sig["act_done"].at(t + 1))
                nc.vector.tensor_reduce(col(amax2, t), h, AXX, ALU.max, apply_absolute_value=True)
                link(dve, nc.vector.tensor_tensor(sq2[:], h, h, ALU.mult))
                link(dve, nc.vector.tensor_reduce(col(ms2, t), sq2[:], AXX, ALU.add))
                link(dve, nc.vector.tensor_scalar(col(ms2, t), col(ms2, t), 1.0 / F, 1e-5, ALU.mult, ALU.add))
                nc.vector.tensor_copy(col(inv2, t), col(ms2, t)).then_inc(sig["norm_stats"].sem, sig["norm_stats"].step())
                dve.wait_ge(sig["norm_scale"].sem, sig["norm_scale"].at(t + 1))
                link(dve, nc.vector.tensor_scalar(col(amax2, t), col(amax2, t), col(r2, t), 1e-5, ALU.mult, ALU.max))
                link(dve, nc.vector.reciprocal(col(qscale2, t), col(amax2, t)))
                link(dve, nc.vector.tensor_scalar(col(qscale2, t), col(qscale2, t), 127.0, None, ALU.mult))
                nc.vector.tensor_scalar(col(step2, t), col(amax2, t), wmean[:, 1:2], 1.0 / 127.0, ALU.mult, ALU.mult)
                link(dve, nc.vector.tensor_scalar(h, h, col(r2, t), col(qscale2, t), ALU.mult, ALU.mult))
                link(dve, nc.vector.tensor_scalar(h, h, ROUND, None, ALU.add))
                nc.vector.tensor_scalar(h, h, -ROUND, None, ALU.add).then_inc(
                    sig["prod_done"].sem, sig["prod_done"].step())
                dve.wait_ge(sig["y_done"].sem, sig["y_done"].at(t + 1))
                link(dve, nc.vector.scalar_tensor_tensor(out=core.x_sb[:, t, :], in0=core.bank[4 + t % 2][:, 0:C],
                                                         scalar=col(step2, t), in1=core.x_sb[:, t, :],
                                                         op0=ALU.mult, op1=ALU.add))
                nc.vector.tensor_tensor(core.x_sb[:, t, :], core.x_sb[:, t, :], core.bank[6 + t % 2][:, 0:C],
                                        ALU.add).then_inc(sig["y_added"].sem, sig["y_added"].step())
    core.end_region()



def linear_experts(core, ctx, w_in, w_out_t, gates):
    nc, sig = core.nc, core.sig
    E = 8
    both = ctx.enter_context(nc.sbuf_tensor("expert_product", [P, E, C], F32))
    with nc.Block() as block:
        @block.tensor
        def _(pe):
            for e in range(E):
                for c in range(4):
                    k = (e * 4 + c) * P
                    ins = nc.tensor.matmul(core.bank[e // 4][:, (e % 4) * C:(e % 4 + 1) * C], w_in[:, k:k + P],
                                           w_out_t[:, k:k + P], start=c == 0, stop=c == 3)
                if e % 4 == 3:
                    ins.then_inc(sig["mm_done"].sem, sig["mm_done"].step())
            pe.wait_ge(sig["act_done"].sem, sig["act_done"].at(2))
            for n in range(2 * NT):
                t, half = n // 2, n % 2
                if n >= 4:
                    pe.wait_ge(sig["y_added"].sem, sig["y_added"].at(n - 3))
                nc.tensor.matmul(core.bank[2 + n % 4][:], core.xn_t[:, t * P:(t + 1) * P],
                                 both[:, 4 * half:4 * half + 4, :].rearrange("p e c -> p (e c)"),
                                 start=True, stop=True).then_inc(sig["y_done"].sem, sig["y_done"].step())

        @block.scalar
        def _(act):
            for half in range(2):
                act.wait_ge(sig["mm_done"].sem, sig["mm_done"].at(half + 1))
                nc.scalar.activation(both[:, 4 * half:4 * half + 4, :].rearrange("p e c -> p (e c)"),
                                     core.bank[half][:], ACT.Copy).then_inc(
                    sig["act_done"].sem, sig["act_done"].step())

        @block.vector
        def _(dve):
            link = core.dve_chain.link
            for n in range(2 * NT):
                t, half = n // 2, n % 2
                dve.wait_ge(sig["y_done"].sem, sig["y_done"].at(n + 1))
                for e in range(4):
                    g = 4 * half + e
                    ins = nc.vector.scalar_tensor_tensor(
                        out=core.x_sb[:, t, :], in0=core.bank[2 + n % 4][:, e * C:(e + 1) * C],
                        scalar=gates[:, t, g:g + 1], in1=core.x_sb[:, t, :], op0=ALU.mult, op1=ALU.add)
                    if e < 3:
                        link(dve, ins)
                ins.then_inc(sig["y_added"].sem, sig["y_added"].step())
                dve.wait_ge(sig["y_added"].sem, sig["y_added"].at(n + 1))
    core.end_region()



CONSTANTS = [("ident", P), ("diagonal", P), ("ones", P), ("mean_col", 16), ("tri", 64), ("gamma", C), ("beta", C),
             ("head_gates", H), ("ctx_t", B * KC), ("ctx_rows", B * C), ("bit_b1", 512),
             ("l0_wq", 512), ("l0_wk", 512), ("l0_wv", C), ("l0_bq", 4), ("l0_bk", 4)]
SMALL = [(f"{n}_{m}", c) for n in ("l1", "l1x", "l3x")
         for m, c in (("wq", 512), ("wk", 512), ("wv", C), ("wo", C), ("bq", 4), ("bk", 4))] + [
    ("l1f_b1", 32), ("l1f_b2", C), ("l1f_wg", 8), ("w_hg", 256), ("bit_w1", 512), ("bit_w2", 512),
    ("ss_wd", C), ("ss_wb", 16), ("ss_wc", 16), ("ss_wo", C), ("ss_a", 16), ("ss_bd", 1), ("ss_bb", 1), ("ss_bc", 1),
    ("proj_w", C), ("norm_w", 7), ("ff_b1", 8), ("l3f_wg", 8)]
ROPE = [("swap", P), ("cos", T), ("sin", T)]
ROWS = [("l0_bv", C), ("l1_bv", C), ("l1_bo", C), ("l1x_bv", C), ("l1x_bo", C), ("l1f_bg", 8), ("bo0", C),
        ("bo1", C), ("cbo0", C), ("cbo1", C), ("fb0", C), ("fb1", C), ("proj_b", C), ("bit_b2", C), ("ss_bo", C),
        ("l3x_bv", C), ("l3x_bo", C), ("ones_row", P)]
FFN0 = [("w1", 1024), ("w2", 1024), ("w3", 1024), ("ws1", 32), ("ws2", 32), ("ws3", C), ("wr", 8)]
FFN1 = [("up", 4096), ("down", 4096)]
SELF = [("wq", 1024), ("wk", 1024), ("wv", 1024), ("wo", 1024)]
CROSS = SELF + [("fw1", 512), ("fw2", 512)]
FFN3 = [("w_in", 4096), ("w_out", 4096)]
RELS = 2 * T - 1
TOEPLITZ = T + (TB - 1) * P


def width(pack):
    return sum(c for _, c in pack)


def views(tile, pack, at=0):
    out = {}
    for name, c in pack:
        out[name] = tile[:, at:at + c]
        at += c
    return out


def decoder(nc, d):
    with ExitStack() as ctx:
        core = Core(nc, ctx)
        sig = core.sig

        def sb(name, shape, dt=F32):
            return ctx.enter_context(nc.sbuf_tensor(name, shape, dt))

        const_sb, small_sb = sb("const_sb", [P, width(CONSTANTS)]), sb("small_sb", [P, width(SMALL)])
        rows_sb = sb("rows_sb", [1, width(ROWS)])
        arena = sb("arena", [P, H * TOEPLITZ])
        arena2 = sb("arena2", [P, width(FFN1)])
        diag_bf, ident_bf = sb("diag_bf", [P, P], BF16), sb("ident_bf", [P, P], BF16)
        key_row, ones_bf = sb("key_row", [1, B * T], BF16), sb("ones_bf", [1, P], BF16)
        w = {**views(const_sb, CONSTANTS), **views(small_sb, SMALL)}
        row = {n: v[0:1, :] for n, v in views(rows_sb, ROWS).items()}
        w["ss_bo"] = row["ss_bo"]
        core.ones_row = row["ones_row"]
        ident = w["ident"]
        load = {n: ctx.enter_context(nc.semaphore(f"load_{n}")) for n in (
            "x", "const", "small", "masks", "key_mask", "toeplitz", "ffn0", "ffn1", "self0", "cross0", "self1", "cross1", "rope",
            "ffn3", "out")}
        parts = 4

        def fetch(eng, dst, src, name):
            n = dst.shape[-1] // parts
            for i in range(parts):
                eng.dma_start(dst[:, i * n:(i + 1) * n], src[:, i * n:(i + 1) * n]).then_inc(load[name], 16)

        LOADED = 16 * parts
        slot0, slot1, slot2 = 0, width(SELF), width(SELF) + width(CROSS)

        with ExitStack() as scope:
            mask_sb = scope.enter_context(nc.sbuf_tensor("mask_sb", [P, NT, KC], I32))
            m01 = scope.enter_context(nc.sbuf_tensor("m01", [P, NT, KC], F32))
            mneg = scope.enter_context(nc.sbuf_tensor("mneg", [P, NT, KC], F32))
            key_u8 = scope.enter_context(nc.sbuf_tensor("key_u8", [1, B * T], U8))
            key_f = scope.enter_context(nc.sbuf_tensor("key_f", [1, B * T], F32))
            with nc.Block() as block:
                @block.sync
                def _(sp):
                    sp.dma_start(core.x_sb[:], d["x"]).then_inc(load["x"], 16)
                    sp.dma_start(const_sb[:], d["constants"]).then_inc(load["const"], 16)
                    sp.dma_start(rows_sb[:], d["rows"]).then_inc(load["const"], 16)
                    sp.dma_start(mask_sb[:], d["mask0"]).then_inc(load["masks"], 16)
                    sp.dma_start(key_u8[:], d["key_mask"]).then_inc(load["key_mask"], 16)
                    fetch(sp, arena2[:, :width(FFN0)], d["ffn0"], "ffn0")
                    sp.dma_start(small_sb[:], d["small"]).then_inc(load["small"], 16)
                    if 3 in SUBLAYERS:
                        base = d["relative"]
                        for h in range(H):
                            src = bass.AP(base.tensor, h * RELS, [[1, P], [1, TOEPLITZ]])
                            sp.dma_start(arena[:, h * TOEPLITZ:(h + 1) * TOEPLITZ], src).then_inc(
                                load["toeplitz"], 16)

                @block.vector
                def _(dve):
                    link = core.dve_chain.link
                    nc.vector.memset(core.minus_half[:], -0.5)
                    nc.vector.memset(ones_bf[:], 1.0)
                    dve.wait_ge(load["const"], 32)
                    nc.vector.tensor_copy(diag_bf[:], w["diagonal"])
                    nc.vector.tensor_copy(ident_bf[:], ident)
                    dve.wait_ge(load["key_mask"], 16)
                    link(dve, nc.vector.tensor_copy(key_f[:], key_u8[:]))
                    link(dve, nc.vector.tensor_scalar(key_f[:], key_f[:], 0.0, None, ALU.is_equal))
                    nc.vector.tensor_scalar(key_row[:], key_f[:], NEG, None, ALU.mult)
                    dve.wait_ge(load["masks"], 16)
                    link(dve, nc.vector.tensor_scalar(m01[:], mask_sb[:], 0, None, ALU.not_equal))
                    nc.vector.tensor_scalar(mneg[:], m01[:], -1.0, 9.0e15, ALU.add, ALU.mult)
                    dve.wait_ge(load["x"], 16)
            core.end_region()

            def qk_small(name, q, k):
                return ([(q[:, s, :], w[f"{name}_wq"][:, s * P:(s + 1) * P], None, w[f"{name}_bq"][:, s:s + 1], None,
                          False) for s in range(4)],
                        [(k[:, s, :], w[f"{name}_wk"][:, s * P:(s + 1) * P], None, w[f"{name}_bk"][:, s:s + 1], None,
                          False) for s in range(4)])

            def head8(a, h):
                return a[32 * (h % 4):32 * (h % 4) + 8, h // 4, :]

            def small_self(name, top=None, gate=None, causal=None, wo=None, bo=None):
                for b in range(B):
                    with ExitStack() as s:
                        def tb(n, shape):
                            return s.enter_context(nc.sbuf_tensor(f"{n}_{nc.next_id()}", shape, F32))
                        q, k, v = tb("q8", [P, 4, T]), tb("k8", [P, 4, T]), tb("v8", [P, TB, C])
                        xt = core.xn_t[:, b * T:(b + 1) * T]
                        jobs = []
                        for dst, lhs, _, colb, _, _ in sum(qk_small(name, q, k), []):
                            jobs.append((dst, lhs, xt, colb, None, False))
                        for t in range(TB):
                            jobs.append((v[:, t, :], xt[:, t * P:(t + 1) * P], w[f"{name}_wv"], None,
                                         row[f"{name}_bv"], False))
                        project(core, jobs)
                        tail = None
                        if wo is not None:
                            tail = Tail(core, core.x_sb, None, tb("o_t", [P, BANK])[:, :P], wo, bo, 1, ident,
                                        [core.bank[6]], core.bank[7])
                        self_attention(core, s, b, lambda h, qt: head8(q, h)[:, qt * P:(qt + 1) * P],
                                       lambda h: head8(k, h), lambda h, c: v[:, c, h * 8:(h + 1) * 8], 8, 8 ** -0.5,
                                       core.x_sb, ident, tail=tail, causal=causal, top=top, gate=gate)

            if 0 in SUBLAYERS:
                normalise(core, core.x_sb, ident)
                small_self("l0", causal=(ident_bf[:], diag_bf[:]))

            if 1 in SUBLAYERS:
                normalise(core, core.x_sb, ident)
                with ExitStack() as s:
                    def finish(dve, u, o_sb):
                        link = core.dve_chain.link
                        for g in range(TB):
                            last = nc.vector.bn_stats(core.stats[:, g, :], o_sb[:, g * C:(g + 1) * C])
                        link(dve, last)
                        for g in range(TB):
                            last = nc.vector.bn_aggr(core.mv[:, g, :], core.stats[:, g, :])
                        link(dve, last)
                        nc.vector.tensor_scalar(core.spread[:, 0:TB], core.mv[:, 0:TB, 1], 1e-5, None,
                                                ALU.add).then_inc(sig["norm_stats"].sem, sig["norm_stats"].step())
                        dve.wait_ge(sig["norm_scale"].sem, sig["norm_scale"].at(u + 1))
                        for g in range(TB):
                            last = nc.vector.tensor_scalar(o_sb[:, g * C:(g + 1) * C], o_sb[:, g * C:(g + 1) * C],
                                                           core.mv[:, g, 0:1], core.rstd[:, g:g + 1], ALU.subtract,
                                                           ALU.mult)
                        link(dve, last)
                        o3 = o_sb[:].rearrange("p (g c) -> p g c", c=C)
                        link(dve, nc.vector.tensor_tensor(o3, o3, wide(w["gamma"], TB, 1), ALU.mult))
                        link(dve, nc.vector.tensor_tensor(o3, o3, wide(w["beta"], TB, 1), ALU.add))
                        tiles = core.x_sb[:, u * TB:(u + 1) * TB, :]
                        link(dve, nc.vector.tensor_tensor(tiles, tiles, o3, ALU.add))

                    context_attention(
                        core, s, [0, 1], TB, lambda u, g: core.xn_t[:, (u * TB + g) * P:(u * TB + g + 1) * P],
                        lambda u, g: w["ctx_t"][:, u * KC:(u + 1) * KC],
                        lambda u, g: w["ctx_rows"][:KC, u * C:(u + 1) * C], C, C ** -0.5, ident,
                        mask=(lambda u, g: m01[:, u * TB + g.start:u * TB + g.stop, :],
                              lambda u, g: mneg[:, u * TB + g.start:u * TB + g.stop, :]), finish=finish)

        if 2 in SUBLAYERS:
            normalise(core, core.x_sb, ident, loads=[(load["ffn0"], LOADED)])
            with ExitStack() as s:
                f = views(arena2, FFN0)
                gates = route(core, s, f["wr"], None, 6, w["tri"])
                jobs = [(lambda c: f["ws1"], lambda c: f["ws2"], lambda c: f["ws3"][:32, :], None, ACT.Silu, 1, None)]
                for e in range(8):
                    jobs.append((lambda c, e=e: f["w1"][:, e * P:(e + 1) * P], lambda c, e=e: f["w2"][:, e * P:(e + 1) * P],
                                 lambda c, e=e: f["w3"][:, e * P:(e + 1) * P], None, ACT.Silu, 1, e))
                feed_forward(core, s, core.x_sb, jobs, gates)

        def fetch_region(what, after=()):
            with nc.Block() as block:
                @block.sync
                def _(sp):
                    for name, value in after:
                        sp.wait_ge(load[name], value)
                    for dst, src, name in what:
                        fetch(sp, dst, src, name)
            core.end_region()

        if 5 in SUBLAYERS:
            fetch_region([(arena2[:, :], d["ffn1"], "ffn1")], [("ffn0", LOADED)])

        if 3 in SUBLAYERS:
            normalise(core, core.x_sb, ident, loads=[(load["toeplitz"], 16 * H), (load["small"], 16)])
            def bias(h, qt):
                last = h * TOEPLITZ + T - 1 + qt * P
                whole = arena[:, :]
                return bass.AP(whole.tensor, last, [list(whole.ap[0]), [-1, T]])
            small_self("l1", top=(bias, 32), gate=w["head_gates"], wo=w["l1_wo"], bo=row["l1_bo"])

        if 7 in SUBLAYERS:
            fetch_region([(arena[:, slot0:slot0 + width(SELF)], d["self0"], "self0"),
                          (arena[:, slot1:slot1 + width(CROSS)], d["cross0"], "cross0"),
                          (arena[:, slot2:slot2 + width(SELF)], d["self1"], "self1")])

        def small_context(name, mask=None, stable=False):
            with ExitStack() as s:
                def tb(n, shape):
                    return s.enter_context(nc.sbuf_tensor(f"{n}_{nc.next_id()}", shape, F32))
                q, k, v = tb("q8", [P, 4, B * T]), tb("k8", [P, 4, B * KC]), tb("v8", [P, B, C])
                qj, kj = qk_small(name, q, k)
                jobs = []
                for dst, lhs, _, colb, _, _ in kj:
                    jobs.append((dst, lhs, w["ctx_t"], colb, None, False))
                for b in range(B):
                    jobs.append((v[:KC, b, :], w["ctx_t"][:, b * KC:(b + 1) * KC], w[f"{name}_wv"], None,
                                 row[f"{name}_bv"], False))
                for b in range(B):
                    for dst, lhs, _, colb, _, _ in qj:
                        jobs.append((dst[:, b * T:(b + 1) * T], lhs, core.xn_t[:, b * T:(b + 1) * T], colb, None, False))
                project(core, jobs)
                tail = Tail(core, core.x_sb, None, tb("o_t", [P, P]), w[f"{name}_wo"], row[f"{name}_bo"], 1, ident,
                            [core.bank[5]], core.bank[5])
                context_attention(core, s, list(range(NT)), H,
                                  lambda t, h: head8(q, h)[:, t * P:(t + 1) * P],
                                  lambda t, h: head8(k, h)[:, t // TB * KC:(t // TB + 1) * KC],
                                  lambda t, h: v[:KC, t // TB, h * 8:(h + 1) * 8], 8, 8 ** -0.5, ident, tail=tail,
                                  mask=mask, stable=stable)

        if 4 in SUBLAYERS:
            with ExitStack() as s:
                mask_sb = s.enter_context(nc.sbuf_tensor("mask4_sb", [P, NT, KC], I32))
                m01 = s.enter_context(nc.sbuf_tensor("m01_4", [P, NT, KC], F32))
                mneg = s.enter_context(nc.sbuf_tensor("mneg_4", [P, NT, KC], F32))
                with nc.Block() as block:
                    @block.sync
                    def _(sp):
                        sp.dma_start(mask_sb[:], d["mask4"]).then_inc(load["masks"], 16)

                    @block.vector
                    def _(dve):
                        dve.wait_ge(load["masks"], 32)
                        core.dve_chain.link(dve, nc.vector.tensor_scalar(m01[:], mask_sb[:], 0, None, ALU.not_equal))
                        nc.vector.tensor_scalar(mneg[:], m01[:], -1.0, 1.0e11, ALU.add, ALU.mult)
                core.end_region()
                normalise(core, core.x_sb, ident, loads=[(load["small"], 16)])
                small_context("l1x", mask=(lambda t, g: wide(m01[:, t, :], len(range(*g.indices(H))), 1),
                                           lambda t, g: wide(mneg[:, t, :], len(range(*g.indices(H))), 1)))

        if 5 in SUBLAYERS:
            normalise(core, core.x_sb, ident, loads=[(load["ffn1"], LOADED), (load["small"], 16)])
            with ExitStack() as s:
                f = views(arena2, FFN1)
                gates = route(core, s, w["l1f_wg"], row["l1f_bg"], 2, w["tri"])
                gates_t = s.enter_context(nc.sbuf_tensor("gates_t", [8, NT, P], F32))
                with nc.Block() as block:
                    @block.tensor
                    def _(pe):
                        for t in range(NT):
                            ins = nc.tensor.transpose(core.bank[t // TB][:8, (t % TB) * P:(t % TB + 1) * P],
                                                      gates[:, t, :], ident)
                        ins.then_inc(sig["turn_done"].sem, sig["turn_done"].step())
                        pe.wait_ge(sig["turn_taken"].sem, sig["turn_taken"].at(B))
                        for t in range(NT):
                            ins = nc.tensor.matmul(core.bank[2 + t // TB][:, (t % TB) * P:(t % TB + 1) * P],
                                                   gates_t[:, t, :], w["l1f_b2"][:8, :], start=True, stop=True)
                        ins.then_inc(sig["y_done"].sem, sig["y_done"].step())

                    @block.scalar
                    def _(act):
                        act.wait_ge(sig["turn_done"].sem, sig["turn_done"].at(1))
                        for b in range(B):
                            nc.scalar.activation(
                                gates_t[:, b * TB:(b + 1) * TB, :].rearrange("p t c -> p (t c)"),
                                core.bank[b][:8, :], ACT.Copy).then_inc(sig["turn_taken"].sem, sig["turn_taken"].step())

                    @block.vector
                    def _(dve):
                        dve.wait_ge(sig["y_done"].sem, sig["y_done"].at(1))
                        for b in range(B):
                            half = core.x_sb[:, b * TB:(b + 1) * TB, :].rearrange("p t c -> p (t c)")
                            nc.vector.tensor_tensor(half, half, core.bank[2 + b][:], ALU.add)
                core.end_region()
                jobs = []
                for e in list(range(0, 8, 2)) + list(range(1, 8, 2)):
                    jobs.append((lambda c, e=e: f["up"][:, (e * 4 + c) * P:(e * 4 + c + 1) * P], None,
                                 lambda c, e=e: f["down"][:, (e * 4 + c) * P:(e * 4 + c + 1) * P],
                                 lambda c, e=e: w["l1f_b1"][:, e * 4 + c:e * 4 + c + 1],
                                 ACT.Silu if e % 2 else ACT.Gelu, 4, e))
                feed_forward(core, s, core.x_sb, jobs, gates)

        if 6 in SUBLAYERS:
            normalise(core, core.x_sb, ident, loads=[(load["small"], 16)])
            with ExitStack() as s:
                gated_recurrence(core, s, w["w_hg"], ident)

        if 7 in SUBLAYERS:
            with ExitStack() as s7:
                rope_sb = s7.enter_context(nc.sbuf_tensor("rope_sb", [P, width(ROPE)], F32))
                r = views(rope_sb, ROPE)
                with nc.Block() as block:
                    @block.sync
                    def _(sp):
                        sp.dma_start(rope_sb[:], d["rope"]).then_inc(load["rope"], 16)
                core.end_region()
                normalise(core, core.x_sb, ident, keep_rows=core.y_sb,
                          loads=[(load["small"], 16), (load["rope"], 16)])
                for l in range(2):
                    ws = views(arena, SELF, slot0 if l == 0 else slot2)
                    wc = views(arena, CROSS, slot1)
                    normalise(core, core.y_sb, ident, mean_free=False, weight=w["norm_w"][:, l:l + 1],
                              loads=[(load[f"self{l}"], LOADED)])
                    for b in range(B):
                        with ExitStack() as s:
                            def tb(n, shape):
                                return s.enter_context(nc.sbuf_tensor(f"{n}_{nc.next_id()}", shape, F32))
                            q = arena2[:, 0:8 * T].rearrange("p (s t) -> p s t", s=8)
                            k = arena2[:, 8 * T:16 * T].rearrange("p (s t) -> p s t", s=8)
                            v = tb("v64", [P, TB, 1024])
                            xt = core.xn_t[:, b * T:(b + 1) * T]
                            with ExitStack() as s2:
                                bufs = [s2.enter_context(nc.sbuf_tensor(f"rope_{n}_{nc.next_id()}", [P, m, T], F32))
                                        for n, m in (("raw", 3), ("part", 3), ("swapped", 2))]
                                jobs = []
                                for c in range(8):
                                    jobs.append((q[:, c, :], ws["wq"][:, c * P:(c + 1) * P], xt, None, None, True))
                                    jobs.append((v[:, c // 2, (c % 2) * T:(c % 2 + 1) * T],
                                                 xt[:, (c // 2) * P:(c // 2 + 1) * P],
                                                 ws["wv"][:, (c % 2) * T:(c % 2 + 1) * T], None, None, False))
                                    jobs.append((k[:, c, :], ws["wk"][:, c * P:(c + 1) * P], xt, None, None, True))
                                project(core, jobs, rope=(r["swap"], r["cos"], r["sin"], *bufs))
                            tail = Tail(core, core.y_sb, None, tb("o_t", [P, 1024]), ws["wo"], row[f"bo{l}"], 8,
                                        ident, [core.bank[7]], core.bank[2])
                            self_attention(
                                core, s, b,
                                lambda h, qt: q[64 * (h % 2):64 * (h % 2) + 64, h // 2, qt * P:(qt + 1) * P],
                                lambda h: k[64 * (h % 2):64 * (h % 2) + 64, h // 2, :],
                                lambda h, c: v[:, c, h * 64:(h + 1) * 64], 64, 64 ** -0.5, core.y_sb, ident,
                                tail=tail, key_mask=(ones_bf[:], key_row[0:1, b * T:(b + 1) * T]))
                    normalise(core, core.y_sb, ident, mean_free=False, weight=w["norm_w"][:, 2 + l:3 + l],
                              loads=[(load[f"cross{l}"], LOADED)])
                    for b in range(B):
                        with ExitStack() as s:
                            def tb(n, shape):
                                return s.enter_context(nc.sbuf_tensor(f"{n}_{nc.next_id()}", shape, F32))
                            q = arena2[:, 0:8 * T].rearrange("p (s t) -> p s t", s=8)
                            k = arena2[:, 8 * T:8 * T + 8 * KC].rearrange("p (s t) -> p s t", s=8)
                            v = tb("v64", [P, 1024])
                            xt = core.xn_t[:, b * T:(b + 1) * T]
                            ct = w["ctx_t"][:, b * KC:(b + 1) * KC]
                            with ExitStack() as s2:
                                bufs = [s2.enter_context(nc.sbuf_tensor(f"rope_{n}_{nc.next_id()}", [P, m, T], F32))
                                        for n, m in (("raw", 3), ("part", 3), ("swapped", 2))]
                                jobs = []
                                for c in range(8):
                                    jobs.append((q[:, c, :], wc["wq"][:, c * P:(c + 1) * P], xt, None, None, True))
                                    jobs.append((k[:, c, :], wc["wk"][:, c * P:(c + 1) * P], ct, None, None, True))
                                for c in range(2):
                                    jobs.append((v[:KC, c * T:(c + 1) * T], ct, wc["wv"][:, c * T:(c + 1) * T], None,
                                                 None, False))
                                project(core, jobs, rope=(r["swap"], r["cos"], r["sin"], *bufs))
                            tail = Tail(core, core.y_sb, None, tb("o_t", [P, 1024]), wc["wo"], row[f"cbo{l}"], 8,
                                        ident, [core.bank[5], core.bank[6]], core.bank[5])
                            context_attention(
                                core, s, [b * TB + t for t in range(TB)], H,
                                lambda t, h: q[64 * (h % 2):64 * (h % 2) + 64, h // 2,
                                               (t % TB) * P:(t % TB + 1) * P],
                                lambda t, h: k[64 * (h % 2):64 * (h % 2) + 64, h // 2, :],
                                lambda t, h: v[:KC, h * 64:(h + 1) * 64], 64, 64 ** -0.5, ident, tail=tail)
                    normalise(core, core.y_sb, ident, mean_free=False, weight=w["norm_w"][:, 4 + l:5 + l])
                    with ExitStack() as s:
                        feed_forward(core, s, core.y_sb, [(
                            lambda c: wc["fw1"][:, c * P:(c + 1) * P], None, lambda c: wc["fw2"][:, c * P:(c + 1) * P],
                            lambda c: w["ff_b1"][:, 4 * l + c:4 * l + c + 1], ACT.Gelu, 4, None)])
                    add_rows(core, core.y_sb, row[f"fb{l}"])
                    if l == 0:
                        fetch_region([(arena[:, slot1:slot1 + width(CROSS)], d["cross1"], "cross1")])
                normalise(core, core.y_sb, ident, mean_free=False, weight=w["norm_w"][:, 6:7])
                with nc.Block() as block:
                    @block.tensor
                    def _(pe):
                        for t in range(NT):
                            out = core.bank[t // TB][:, (t % TB) * P:(t % TB + 1) * P]
                            nc.tensor.matmul(out, core.xn_t[:, t * P:(t + 1) * P], w["proj_w"], start=True, stop=False)
                            nc.tensor.matmul(out, core.ones_row[0:1, :], row["proj_b"], start=False,
                                             stop=True).then_inc(sig["y_done"].sem, sig["y_done"].step())

                    @block.vector
                    def _(dve):
                        for b in range(B):
                            dve.wait_ge(sig["y_done"].sem, sig["y_done"].at((b + 1) * TB))
                            half = core.x_sb[:, b * TB:(b + 1) * TB, :].rearrange("p t c -> p (t c)")
                            nc.vector.tensor_tensor(half, half, core.bank[b][:], ALU.add)
                core.end_region()

        if 11 in SUBLAYERS:
            fetch_region([(arena2[:, :], d["ffn3"], "ffn3")], [("ffn1" if 5 in SUBLAYERS else "ffn0", LOADED)])

        if 8 in SUBLAYERS:
            normalise(core, core.x_sb, ident, loads=[(load["small"], 16)])
            with ExitStack() as s:
                bit_feed_forward(core, s, w["bit_w1"], w["bit_w2"], w["bit_b1"], row["bit_b2"], ident, w["ones"])

        if 9 in SUBLAYERS:
            normalise(core, core.x_sb, ident, loads=[(load["small"], 16)])
            with ExitStack() as s:
                state_space(core, s, w)

        if 10 in SUBLAYERS:
            normalise(core, core.x_sb, ident, loads=[(load["small"], 16)])
            small_context("l3x", stable=True)

        if 11 in SUBLAYERS:
            normalise(core, core.x_sb, ident, loads=[(load["ffn3"], LOADED), (load["small"], 16)])
            with ExitStack() as s:
                gates = route(core, s, w["l3f_wg"], None, 2, w["tri"])
                f = views(arena2, FFN3)
                linear_experts(core, s, f["w_in"], f["w_out"], gates)

        with nc.Block() as block:
            @block.sync
            def _(sp):
                sp.dma_start(d["out"], core.x_sb[:]).then_inc(load["out"], 16)
                sp.wait_ge(load["out"], 16)
        core.end_region()



def pack_arrays(pack, arrays):
    out = np.zeros((P, width(pack)), np.float32)
    at = 0
    for name, c in pack:
        a = arrays[name]
        assert a.shape[1] == c, (name, a.shape, c)
        out[:a.shape[0], at:at + c] = a
        at += c
    return out


def heads_of_8(wt, bias):
    wide_w = np.zeros((C, 4, 4, 32), np.float32)
    wide_w[..., :8] = wt.reshape(C, 4, 4, 8)
    wide_b = np.zeros((4, 4, 32), np.float32)
    wide_b[..., :8] = bias.reshape(4, 4, 8)
    return wide_w.reshape(C, 512), wide_b.reshape(4, P).T


def chunked(a):
    n = a.shape[0] // P
    return a.reshape(n, P, -1).transpose(1, 0, 2).reshape(P, -1)


def kernel(**inputs):
    import concourse.bacc as bacc
    from concourse.bass_utils import run_bass_kernel_spmd

    v = {k: np.asarray(a) for k, a in inputs.items()}
    a = {}
    a["ident"] = np.eye(P, dtype=np.float32)
    a["diagonal"] = np.where(np.tril(np.ones((P, P), bool)), 0.0, NEG).astype(np.float32)
    a["ones"] = np.ones((P, P), np.float32)
    a["mean_col"] = np.full((P, 16), 1.0 / P, np.float32)
    a["tri"] = np.broadcast_to(np.tril(np.ones((8, 8), np.float32), -1).reshape(1, 64), (P, 64))
    a["gamma"] = np.broadcast_to(v["L0_xattn_gamma"], (P, C))
    a["beta"] = np.broadcast_to(v["L0_xattn_beta"], (P, C))
    a["head_gates"] = np.broadcast_to(v["L1_attn_head_gates"], (P, H))
    a["ctx_t"] = v["ctx_1024"].transpose(2, 0, 1).reshape(C, B * KC)
    a["ctx_rows"] = v["ctx_1024"].transpose(1, 0, 2).reshape(KC, B * C)
    a["bit_b1"] = np.broadcast_to(v["L2_ffn_b1"], (P, 512))
    w0, b0 = v["L0_attn_W"], v["L0_attn_b"]
    a["l0_wq"], a["l0_bq"] = heads_of_8(w0[:C].T, b0[:C])
    a["l0_wk"], a["l0_bk"] = heads_of_8(w0[C:2 * C].T, b0[C:2 * C])
    a["l0_wv"], a["l0_bv"] = w0[2 * C:].T, b0[None, 2 * C:]
    for n, src, turned in (("l1", "L1_attn", True), ("l1x", "L1_xattn", False), ("l3x", "L3_xattn", True)):
        m = {k: v[f"{src}_W{k}"].T if turned else v[f"{src}_W{k}"] for k in "qkvo"}
        a[f"{n}_wq"], a[f"{n}_bq"] = heads_of_8(m["q"], v[f"{src}_bq"])
        a[f"{n}_wk"], a[f"{n}_bk"] = heads_of_8(m["k"], v[f"{src}_bk"])
        a[f"{n}_wv"], a[f"{n}_wo"] = m["v"], m["o"]
        a[f"{n}_bv"], a[f"{n}_bo"] = v[f"{src}_bv"][None], v[f"{src}_bo"][None]
    a["l1f_b1"] = v["L1_ffn_b1"].reshape(32, P).T
    a["l1f_b2"], a["l1f_wg"], a["l1f_bg"] = v["L1_ffn_b2"], v["L1_ffn_Wg"], v["L1_ffn_bg"][None]
    a["w_hg"] = v["L2_attn_W_hg"].T
    a["bit_w1"], a["bit_w2"], a["bit_b2"] = v["L2_ffn_w1"].T, chunked(v["L2_ffn_w2"].T), v["L2_ffn_b2"][None]
    a["ss_wd"], a["ss_wb"], a["ss_wc"], a["ss_wo"] = (v[f"L3_attn_W{k}"] for k in "dbco")
    a["ss_a"], a["ss_bo"] = v["L3_attn_A"], v["L3_attn_bo"][None]
    a["ss_bd"], a["ss_bb"], a["ss_bc"] = (v[f"L3_attn_b{k}"][:, None] for k in "dbc")
    x2 = "L2_xattn_"
    a["proj_w"], a["proj_b"] = v[x2 + "proj_w"], v[x2 + "proj_b"][None]
    a["norm_w"] = np.stack([v[x2 + "attn_norm_w"][0], v[x2 + "attn_norm_w"][1], v[x2 + "cross_norm_w"][0],
                            v[x2 + "cross_norm_w"][1], v[x2 + "ff_norm_w"][0], v[x2 + "ff_norm_w"][1],
                            v[x2 + "norm_out_w"]], 1)
    a["ff_b1"] = v[x2 + "ff_b1"].reshape(8, P).T
    for l in range(2):
        a[f"bo{l}"], a[f"cbo{l}"], a[f"fb{l}"] = v[x2 + "bo"][l:l + 1], v[x2 + "cbo"][l:l + 1], v[x2 + "ff_b2"][l:l + 1]
    a["l3f_wg"] = v["L3_ffn_w_gate"].T
    a["ones_row"] = np.ones((1, P), np.float32)

    inv = (1.0 / 10000.0 ** (np.arange(0, 32, 2, dtype=np.float32) / np.float32(32))).astype(np.float32)
    angle = (np.arange(T, dtype=np.float32)[:, None] * inv[None, :]).astype(np.float32)
    cos, sin, swap = np.ones((P, T), np.float32), np.zeros((P, T), np.float32), np.zeros((P, P), np.float32)
    for base in (0, 64):
        cos[base:base + 16] = cos[base + 16:base + 32] = np.cos(angle).T
        sin[base:base + 16], sin[base + 16:base + 32] = -np.sin(angle).T, np.sin(angle).T
        for i in range(16):
            swap[base + 16 + i, base + i] = swap[base + i, base + 16 + i] = 1.0

    packs = {"constants": pack_arrays(CONSTANTS, a), "small": pack_arrays(SMALL, a),
             "rows": np.concatenate([a[n] for n, _ in ROWS], 1).astype(np.float32),
             "rope": pack_arrays(ROPE, {"swap": swap, "cos": cos, "sin": sin})}

    def experts(m):
        return m.transpose(1, 0, 2).reshape(m.shape[1], -1)

    packs["ffn0"] = pack_arrays(FFN0, {
        "w1": experts(v["L0_ffn_w1"]), "w2": experts(v["L0_ffn_w2"]), "w3": experts(v["L0_ffn_w3"]),
        "ws1": v["L0_ffn_ws1"], "ws2": v["L0_ffn_ws2"], "ws3": v["L0_ffn_ws3"], "wr": v["L0_ffn_wr"]})
    packs["ffn1"] = pack_arrays(FFN1, {"up": experts(v["L1_ffn_W1"]),
                                       "down": chunked(v["L1_ffn_W2"].reshape(8 * 512, C))})
    packs["ffn3"] = pack_arrays(FFN3, {"w_in": chunked(v["L3_ffn_w_in"].reshape(8 * 512, C)),
                                       "w_out": chunked(v["L3_ffn_w_out"].transpose(0, 2, 1).reshape(8 * 512, C))})
    for l in range(2):
        packs[f"self{l}"] = pack_arrays(SELF, {
            "wq": v[x2 + "Wq"][l], "wk": v[x2 + "Wk"][l], "wv": v[x2 + "Wv"][l], "wo": chunked(v[x2 + "Wo"][l])})
        packs[f"cross{l}"] = pack_arrays(CROSS, {
            "wq": v[x2 + "cWq"][l], "wk": v[x2 + "cWk"][l], "wv": v[x2 + "cWv"][l], "wo": chunked(v[x2 + "cWo"][l]),
            "fw1": v[x2 + "ff_w1"][l], "fw2": chunked(v[x2 + "ff_w2"][l])})

    table = v["L1_attn_rel_bias"]
    at = np.arange(-(T - 1), T) + 63
    at = np.clip(np.where(at < 0, at + table.shape[0], at), 0, table.shape[0] - 1)
    packs["relative"] = np.ascontiguousarray(table[at[::-1]].T)

    def tokens(m):
        return np.ascontiguousarray(m.reshape(NT, P, -1).transpose(1, 0, 2))

    packs["x"] = tokens(v["x"])
    packs["mask0"] = tokens(v["mask_BxSxS2_ik1"].reshape(B * T, KC))
    packs["mask4"] = tokens(v["mask_Bx1xSxS2_ik1"].reshape(B * T, KC))
    packs["key_mask"] = np.ascontiguousarray(v["mask_BxS_bf1"]).view(np.uint8).reshape(1, B * T)

    nc = bacc.Bacc("TRN2", target_bir_lowering=False, num_devices=1)
    d = {n: nc.dram_tensor(f"in_{n}", m.shape, mybir.dt.from_np(m.dtype), kind="ExternalInput").ap()
         for n, m in packs.items()}
    d["out"] = nc.dram_tensor("out_x", (P, NT, C), F32, kind="ExternalOutput").ap()
    decoder(nc, d)
    r = run_bass_kernel_spmd(nc, [{f"in_{n}": m for n, m in packs.items()}], core_ids=[0])
    got = r.results[0]["out_x"]
    return np.ascontiguousarray(got.transpose(1, 0, 2)).reshape(B, T, C)
```

```python
from contextlib import ExitStack

import numpy as np
import concourse.bass as bass
from concourse import mybir

F32 = mybir.dt.float32
BF16 = mybir.dt.bfloat16
I32 = mybir.dt.int32
U8 = mybir.dt.uint8
ALU = mybir.AluOpType
ACT = mybir.ActivationFunctionType
AXX = mybir.AxisListType.X

P = 128
B, T, C = 2, 512, 128
NT = B * T // P
TB = T // P
KC = 77
H = 16
BANK = 512
NEG = -1.0e30
ROUND = 12582912.0
SUBLAYERS = (0, 1, 2, 3, 4, 5, 6, 7, 8, 9, 10, 11)


class Signal:

    def __init__(self, nc, ctx, name):
        self.sem = ctx.enter_context(nc.semaphore(name))
        self.base = 0
        self.count = 0

    def step(self):
        self.count += 1
        return 1

    def at(self, n):
        return self.base + n

    def next_region(self):
        self.base = self.count


class Chain:

    def __init__(self, nc, ctx, name):
        self.sem = ctx.enter_context(nc.semaphore(name))
        self.count = 0

    def link(self, eng, ins):
        self.count += 1
        ins.then_inc(self.sem, 1)
        eng.wait_ge(self.sem, self.count)


def wide(ap, n, axis):
    return ap.unsqueeze(axis).broadcast_to(list(ap.shape[:axis]) + [n] + list(ap.shape[axis:]))


class Core:

    SIGNALS = ("norm_stats", "norm_scale", "norm_rows", "norm_turned", "norm_taken", "mm_done", "mm_taken",
               "raw_ready", "swap_done", "cos_done", "rope_done", "s_done", "s_taken", "max_done", "exp_done", "turn_done",
               "turn_taken", "pv_done", "o_done", "t_turned", "t_taken", "out_done", "out_added", "act_done",
               "prod_done", "y_done", "y_added", "gates_done", "aux_pe", "aux_dve", "aux_act", "aux_pool")

    def __init__(self, nc, ctx):
        self.nc = nc
        self.dve_chain = Chain(nc, ctx, "dve_chain")
        self.act_chain = Chain(nc, ctx, "act_chain")
        self.pool_chain = Chain(nc, ctx, "pool_chain")
        self.sig = {n: Signal(nc, ctx, n) for n in self.SIGNALS}
        self.bank = [ctx.enter_context(nc.psum_tensor(f"bank{i}", [P, BANK], F32)) for i in range(8)]

        def sb(name, shape, dt=F32):
            return ctx.enter_context(nc.sbuf_tensor(name, shape, dt))

        self.x_sb = sb("x_sb", [P, NT, C])
        self.y_sb = sb("y_sb", [P, NT, C])
        self.xn = sb("xn", [P, NT, C])
        self.xn_t = sb("xn_t", [P, B * T])
        self.stats = sb("stats", [P, NT, 6])
        self.mv = sb("mv", [P, NT, 2])
        self.spread = sb("spread", [P, NT])
        self.rstd = sb("rstd", [P, NT])
        self.minus_half = sb("minus_half", [P, NT])

    def end_region(self):
        for s in self.sig.values():
            s.next_region()



def normalise(core, src, ident, mean_free=True, weight=None, keep_rows=None, loads=()):
    nc, sig = core.nc, core.sig
    with nc.Block() as block:
        @block.vector
        def _(dve):
            link = core.dve_chain.link
            for s, v in loads:
                dve.wait_ge(s, v)
            for t in range(NT):
                last = nc.vector.bn_stats(core.stats[:, t, :], src[:, t, :])
            link(dve, last)
            for t in range(NT):
                last = nc.vector.bn_aggr(core.mv[:, t, :], core.stats[:, t, :])
            link(dve, last)
            mean, var = core.mv[:, :, 0], core.mv[:, :, 1]
            if mean_free:
                nc.vector.tensor_scalar(core.spread[:], var, 1e-5, None, ALU.add).then_inc(
                    sig["norm_stats"].sem, sig["norm_stats"].step())
            else:
                link(dve, nc.vector.tensor_tensor(core.spread[:], mean, mean, ALU.mult))
                link(dve, nc.vector.tensor_tensor(core.spread[:], core.spread[:], var, ALU.add))
                nc.vector.tensor_scalar(core.spread[:], core.spread[:], 1e-16, None, ALU.max).then_inc(
                    sig["norm_stats"].sem, sig["norm_stats"].step())
            dve.wait_ge(sig["norm_scale"].sem, sig["norm_scale"].at(1))
            for t in range(NT):
                if mean_free:
                    ins = nc.vector.tensor_scalar(core.xn[:, t, :], src[:, t, :], core.mv[:, t, 0:1],
                                                  core.rstd[:, t:t + 1], ALU.subtract, ALU.mult)
                else:
                    ins = nc.vector.tensor_scalar(core.xn[:, t, :], src[:, t, :], core.rstd[:, t:t + 1],
                                                  None, ALU.mult)
                ins.then_inc(sig["norm_rows"].sem, sig["norm_rows"].step())
            if keep_rows is not None:
                dve.wait_ge(sig["norm_rows"].sem, sig["norm_rows"].at(NT))
                nc.vector.tensor_copy(keep_rows[:], core.xn[:])

        @block.gpsimd
        def _(pool):
            pool.wait_ge(sig["norm_stats"].sem, sig["norm_stats"].at(1))
            nc.gpsimd.tensor_tensor(core.rstd[:], core.spread[:], core.minus_half[:], ALU.pow).then_inc(
                sig["norm_scale"].sem, sig["norm_scale"].step())

        @block.tensor
        def _(pe):
            for t in range(NT):
                pe.wait_ge(sig["norm_rows"].sem, sig["norm_rows"].at(t + 1))
                ins = nc.tensor.transpose(core.bank[t // TB][:, (t % TB) * P:(t % TB + 1) * P],
                                          core.xn[:, t, :], ident)
                if t % TB == TB - 1:
                    ins.then_inc(sig["norm_turned"].sem, sig["norm_turned"].step())

        @block.scalar
        def _(act):
            for b in range(B):
                act.wait_ge(sig["norm_turned"].sem, sig["norm_turned"].at(b + 1))
                nc.scalar.activation(core.xn_t[:, b * T:(b + 1) * T], core.bank[b][:], ACT.Copy if weight is None
                                     else ACT.Identity, scale=1.0 if weight is None else weight)
    core.end_region()



def project(core, jobs, rope=None):
    nc, sig = core.nc, core.sig
    NB = 4
    turned = [i for i, j in enumerate(jobs) if j[5]]
    by_act = [i for i, j in enumerate(jobs) if j[5] or i % 2 == 0]
    by_dve = [i for i in range(len(jobs)) if i not in by_act]

    def wait_taken(eng, i):
        if i in by_act:
            eng.wait_ge(sig["act_done"].sem, sig["act_done"].at(by_act.index(i) + 1))
        else:
            eng.wait_ge(sig["prod_done"].sem, sig["prod_done"].at(by_dve.index(i) + 1))

    with nc.Block() as block:
        @block.tensor
        def _(pe):
            def swap(n):
                i = turned[n]
                pe.wait_ge(sig["act_done"].sem, sig["act_done"].at(by_act.index(i) + 1))
                if n >= 2:
                    pe.wait_ge(sig["swap_done"].sem, sig["swap_done"].at(n - 1))
                nd = jobs[i][0].shape[-1]
                nc.tensor.matmul(core.bank[NB + n % 2][:, :nd], rope[0], rope[3][:, n % 3, :nd],
                                 start=True, stop=True).then_inc(sig["raw_ready"].sem, sig["raw_ready"].step())

            swapped = 0
            for i, (dst, lhs, rhs, col, row, turn) in enumerate(jobs):
                if i >= NB:
                    wait_taken(pe, i - NB)
                m, n = lhs.shape[-1], rhs.shape[-1]
                out = core.bank[i % NB][:m, :n]
                ins = nc.tensor.matmul(out, lhs, rhs, start=True, stop=row is None)
                if row is not None:
                    ins = nc.tensor.matmul(out, core.ones_row[0:1, :m], row, start=False, stop=True)
                ins.then_inc(sig["mm_done"].sem, sig["mm_done"].step())
                while swapped < len(turned) and turned[swapped] <= i - 2:
                    swap(swapped)
                    swapped += 1
            while swapped < len(turned):
                swap(swapped)
                swapped += 1

        @block.scalar
        def _(act):
            for i in by_act:
                dst, lhs, rhs, col, row, turn = jobs[i]
                act.wait_ge(sig["mm_done"].sem, sig["mm_done"].at(i + 1))
                if turn:
                    n = turned.index(i)
                    if n >= 3:
                        act.wait_ge(sig["raw_ready"].sem, sig["raw_ready"].at(n - 2))
                        act.wait_ge(sig["cos_done"].sem, sig["cos_done"].at(n - 2))
                    dst = rope[3][:, n % 3, :dst.shape[-1]]
                src = core.bank[i % NB][:lhs.shape[-1], :rhs.shape[-1]]
                nc.scalar.activation(dst, src, ACT.Identity, bias=0.0 if col is None else col).then_inc(
                    sig["act_done"].sem, sig["act_done"].step())

        @block.gpsimd
        def _(pool):
            for n, i in enumerate(turned):
                nd = jobs[i][0].shape[-1]
                pool.wait_ge(sig["act_done"].sem, sig["act_done"].at(by_act.index(i) + 1))
                if n >= 3:
                    pool.wait_ge(sig["rope_done"].sem, sig["rope_done"].at(n - 2))
                nc.gpsimd.tensor_tensor(rope[4][:, n % 3, :nd], rope[3][:, n % 3, :nd], rope[1][:, :nd],
                                        ALU.mult).then_inc(sig["cos_done"].sem, sig["cos_done"].step())

        @block.vector
        def _(dve):
            def turn_one(n):
                dst = jobs[turned[n]][0]
                nd = dst.shape[-1]
                dve.wait_ge(sig["raw_ready"].sem, sig["raw_ready"].at(n + 1))
                if n >= 2:
                    dve.wait_ge(sig["rope_done"].sem, sig["rope_done"].at(n - 1))
                nc.vector.tensor_tensor(rope[5][:, n % 2, :nd], core.bank[NB + n % 2][:, :nd], rope[2][:, :nd],
                                        ALU.mult).then_inc(sig["swap_done"].sem, sig["swap_done"].step())
                dve.wait_ge(sig["swap_done"].sem, sig["swap_done"].at(n + 1))
                dve.wait_ge(sig["cos_done"].sem, sig["cos_done"].at(n + 1))
                nc.vector.tensor_tensor(dst, rope[4][:, n % 3, :nd], rope[5][:, n % 2, :nd], ALU.add).then_inc(
                    sig["rope_done"].sem, sig["rope_done"].step())

            for i in range(len(jobs)):
                if i in by_dve:
                    dst, lhs, rhs, col, row, _ = jobs[i]
                    dve.wait_ge(sig["mm_done"].sem, sig["mm_done"].at(i + 1))
                    src = core.bank[i % NB][:lhs.shape[-1], :rhs.shape[-1]]
                    if col is None:
                        ins = nc.vector.tensor_copy(dst, src)
                    else:
                        ins = nc.vector.tensor_scalar(dst, src, col, None, ALU.add)
                    ins.then_inc(sig["prod_done"].sem, sig["prod_done"].step())
                if i in turned:
                    turn_one(turned.index(i))
    core.end_region()



class Tail:

    def __init__(self, core, dst, o_sb, o_t, wo, row, nch, ident, banks, out_bank):
        self.core, self.dst, self.o_sb, self.o_t, self.wo = core, dst, o_sb, o_t, wo
        self.row, self.nch, self.ident, self.banks, self.out_bank = row, nch, ident, banks, out_bank

    def rounds(self):
        return -(-self.nch // 4)

    def turn(self, pe, u):
        core, sig = self.core, self.core.sig
        pe.wait_ge(sig["o_done"].sem, sig["o_done"].at(u + 1))
        for j in range(self.rounds()):
            r = self.rounds() * u + j
            if r >= len(self.banks):
                pe.wait_ge(sig["t_taken"].sem, sig["t_taken"].at(r - len(self.banks) + 1))
            for c in range(4 * j, min(4 * j + 4, self.nch)):
                ins = core.nc.tensor.transpose(self.banks[r % len(self.banks)][:, (c % 4) * P:(c % 4 + 1) * P],
                                               self.o_sb[:, c * P:(c + 1) * P], self.ident)
            ins.then_inc(sig["t_turned"].sem, sig["t_turned"].step())

    def copy(self, act, u):
        core, sig = self.core, self.core.sig
        for j in range(self.rounds()):
            r = self.rounds() * u + j
            n = min(4, self.nch - 4 * j) * P
            act.wait_ge(sig["t_turned"].sem, sig["t_turned"].at(r + 1))
            if u >= 1:
                act.wait_ge(sig["out_done"].sem, sig["out_done"].at(u))
            core.nc.scalar.activation(self.o_t[:, j * BANK:j * BANK + n], self.banks[r % len(self.banks)][:, :n],
                                      ACT.Copy).then_inc(sig["t_taken"].sem, sig["t_taken"].step())

    def product(self, pe, u):
        core, sig = self.core, self.core.sig
        pe.wait_ge(sig["t_taken"].sem, sig["t_taken"].at(self.rounds() * (u + 1)))
        if u >= 1:
            pe.wait_ge(sig["out_added"].sem, sig["out_added"].at(u))
        for c in range(self.nch):
            core.nc.tensor.matmul(self.out_bank[:, :C], self.o_t[:, c * P:(c + 1) * P],
                                  self.wo[:, c * C:(c + 1) * C], start=c == 0, stop=False)
        core.nc.tensor.matmul(self.out_bank[:, :C], core.ones_row[0:1, :], self.row, start=False,
                              stop=True).then_inc(sig["out_done"].sem, sig["out_done"].step())

    def add(self, dve, u, tile):
        core, sig = self.core, self.core.sig
        dve.wait_ge(sig["out_done"].sem, sig["out_done"].at(u + 1))
        core.nc.vector.tensor_tensor(self.dst[:, tile, :], self.dst[:, tile, :], self.out_bank[:, :C],
                                     ALU.add).then_inc(sig["out_added"].sem, sig["out_added"].step())



def self_attention(core, ctx, b, q_of, k_pair, head_mask, v_of, hd, dst, ident, wo, bo, causal=None, key_mask=None, top=None, gate=None):
    nc, sig = core.nc, core.sig
    units = [(h, qt) for h in range(H) for qt in range(TB)]
    U = len(units)
    NS, NT2, NE, NTS = 3, 2, 5, 3
    LAG = 3
    pairs = H // 2
    per_group = 1 if hd == 64 else 2
    col = 64 if hd == 64 else 32
    groups = pairs // per_group

    def sb(name, shape, dt=F32):
        return ctx.enter_context(nc.sbuf_tensor(f"{name}_{nc.next_id()}", shape, dt))

    k_one = sb("k_one", [P, 2, T])
    e_sb = sb("e_sb", [P, NE, T])
    e_t = sb("e_t", [P, NTS, TB, T])
    o_t = sb("o_t", [P, 2, T])
    work = sb("work", [P, T]) if top else None
    s_sb = sb("s_sb", [P, 3, T]) if top else None
    best = sb("best", [P, 2, 32]) if top else None
    nmax, den, rden = sb("nmax", [P, U]), sb("den", [P, U]), sb("rden", [P, U])
    s_bank, t_bank, o_bank, y_bank = core.bank[0:3], core.bank[3:5], core.bank[5:7], core.bank[7]

    def chunks(qt):
        return qt + 1 if causal else TB

    def value_step(p):
        return 8 * p + 7 + LAG + 2

    def group_step(g):
        return value_step((g + 1) * per_group - 1) + 2

    steps = group_step(groups - 1) + 3
    value_at = {value_step(p): p for p in range(pairs)}
    group_at = {group_step(g): g for g in range(groups)}

    with nc.Block() as block:
        @block.tensor
        def _(pe):
            def scores(u):
                h, qt = units[u]
                n = chunks(qt) * P
                if qt == 0:
                    pe.wait_ge(sig["aux_pool"].sem, sig["aux_pool"].at(h + 1))
                if u >= NS:
                    freed = sig["s_taken" if top else "exp_done"]
                    pe.wait_ge(freed.sem, freed.at(u - NS + 1))
                out = s_bank[u % NS][:, :n]
                ins = nc.tensor.matmul(out, q_of(h, qt), k_one[:, h % 2, :n], start=True,
                                       stop=not (causal or key_mask or top))
                if causal:
                    ins = nc.tensor.matmul(out[:, n - P:n], causal[0], causal[1], start=False, stop=True)
                if key_mask:
                    ins = nc.tensor.matmul(out, key_mask[0], key_mask[1], start=False, stop=True)
                if top:
                    ins = nc.tensor.matmul(out, top[0], top[1](h, qt), start=False, stop=True)
                ins.then_inc(sig["s_done"].sem, sig["s_done"].step())

            def turn(u):
                h, qt = units[u]
                pe.wait_ge(sig["norm_rows"].sem, sig["norm_rows"].at(u + 1))
                if u >= NT2:
                    pe.wait_ge(sig["turn_taken"].sem, sig["turn_taken"].at(u - NT2 + 1))
                for k in range(chunks(qt)):
                    ins = nc.tensor.transpose(t_bank[u % NT2][:, k * P:(k + 1) * P],
                                              e_sb[:, u % NE, k * P:(k + 1) * P], ident)
                ins.then_inc(sig["turn_done"].sem, sig["turn_done"].step())

            def values(p):
                g, part = p // per_group, p % per_group
                pe.wait_ge(sig["turn_taken"].sem, sig["turn_taken"].at(8 * (p + 1)))
                if part == 0 and g >= 2:
                    pe.wait_ge(sig["o_done"].sem, sig["o_done"].at(g - 1))
                for k in range(TB):
                    at = k * P if causal else 0
                    for h in (2 * p, 2 * p + 1):
                        row = (h * col) % P
                        ins = nc.tensor.matmul(o_bank[g % 2][row:row + col, at:], v_of(h, k), e_t[:, h % NTS, k, at:],
                                               start=k == 0, stop=k == TB - 1)
                ins.then_inc(sig["pv_done"].sem, sig["pv_done"].step())

            def out(g):
                pe.wait_ge(sig["o_done"].sem, sig["o_done"].at(g + 1))
                if g >= 1:
                    pe.wait_ge(sig["out_added"].sem, sig["out_added"].at(g))
                last = g == groups - 1 and bo is not None
                for qt in range(TB):
                    y = y_bank[:, qt * C:(qt + 1) * C]
                    ins = nc.tensor.matmul(y, o_t[:, g % 2, qt * P:(qt + 1) * P], wo(g), start=True, stop=not last)
                    if last:
                        ins = nc.tensor.matmul(y, core.ones_row[0:1, :], bo, start=False, stop=True)
                ins.then_inc(sig["out_done"].sem, sig["out_done"].step())

            for i in range(steps):
                if i < U:
                    scores(i)
                if LAG <= i < U + LAG:
                    turn(i - LAG)
                if i in value_at:
                    values(value_at[i])
                if i in group_at:
                    out(group_at[i])

        @block.gpsimd
        def _(pool):
            for h in range(H):
                if h >= 2:
                    pool.wait_ge(sig["s_done"].sem, sig["s_done"].at(TB * (h - 1)))
                nc.gpsimd.tensor_tensor(k_one[:, h % 2, :], k_pair(h), head_mask(h).broadcast_to([P, T]),
                                        ALU.mult).then_inc(sig["aux_pool"].sem, sig["aux_pool"].step())

        @block.vector
        def _(dve):
            link = core.dve_chain.link

            def maxima(u):
                h, qt = units[u]
                if not top:
                    bank = s_bank[u % NS]
                    dve.wait_ge(sig["s_done"].sem, sig["s_done"].at(u + 1))
                    nc.vector.tensor_reduce(nmax[:, u:u + 1], bank[:, :chunks(qt) * P], AXX, ALU.max,
                                            negate=True).then_inc(sig["max_done"].sem, sig["max_done"].step())
                    return
                dve.wait_ge(sig["s_taken"].sem, sig["s_taken"].at(u + 1))
                bst, scored = best[:, u % 2, :], s_sb[:, u % 3, :]
                link(dve, nc.vector.max(bst[:, 0:8], scored))
                nc.vector.tensor_scalar(nmax[:, u:u + 1], bst[:, 0:1], -1.0, None, ALU.mult).then_inc(
                    sig["max_done"].sem, sig["max_done"].step())
                for r in range(1, top[2] // 8):
                    link(dve, nc.vector.match_replace(work[:], bst[:, 8 * (r - 1):8 * r], scored if r == 1 else work[:],
                                                      -3.0e38))
                    link(dve, nc.vector.max(bst[:, 8 * r:8 * r + 8], work[:]))

            def keep(u):
                dve.wait_ge(sig["exp_done"].sem, sig["exp_done"].at(u + 1))
                e = e_sb[:, u % NE, :]
                ins = nc.vector.scalar_tensor_tensor(out=e, in0=s_sb[:, u % 3, :], scalar=best[:, u % 2, 31:32], in1=e,
                                                     op0=ALU.is_ge, op1=ALU.mult, accum_out=den[:, u:u + 1])
                ins.then_inc(sig["prod_done"].sem, sig["prod_done"].step())
                dve.wait_ge(sig["prod_done"].sem, sig["prod_done"].at(u + 1))

            def factor(u):
                h, qt = units[u]
                if not top:
                    dve.wait_ge(sig["exp_done"].sem, sig["exp_done"].at(u + 1))
                ins = nc.vector.reciprocal(rden[:, u:u + 1], den[:, u:u + 1])
                if gate is not None:
                    link(dve, ins)
                    ins = nc.vector.tensor_scalar(rden[:, u:u + 1], rden[:, u:u + 1], gate[:, h:h + 1], None, ALU.mult)
                ins.then_inc(sig["aux_dve"].sem, sig["aux_dve"].step())

            def divide(u):
                h, qt = units[u]
                e = e_sb[:, u % NE, :chunks(qt) * P]
                dve.wait_ge(sig["aux_dve"].sem, sig["aux_dve"].at(u + 1))
                nc.vector.tensor_scalar(e, e, rden[:, u:u + 1], None, ALU.mult).then_inc(
                    sig["norm_rows"].sem, sig["norm_rows"].step())

            def add(g):
                dve.wait_ge(sig["out_done"].sem, sig["out_done"].at(g + 1))
                if g >= 1:
                    dve.wait_ge(sig["out_added"].sem, sig["out_added"].at(g))
                half = dst[:, b * TB:(b + 1) * TB, :].rearrange("p t c -> p (t c)")
                nc.vector.tensor_tensor(half, half, y_bank[:], ALU.add).then_inc(
                    sig["out_added"].sem, sig["out_added"].step())

            for i in range(steps):
                if i < U:
                    maxima(i)
                if 1 <= i < U + 1:
                    if top:
                        keep(i - 1)
                    factor(i - 1)
                if not top and 1 <= i < U + 1:
                    divide(i - 1)
                if i - 1 in group_at:
                    add(group_at[i - 1])

        @block.scalar
        def _(act):
            def exps(u):
                h, qt = units[u]
                n = chunks(qt) * P
                act.wait_ge(sig["max_done"].sem, sig["max_done"].at(u + 1))
                if u >= NE:
                    act.wait_ge(sig["turn_done"].sem, sig["turn_done"].at(u - NE + 1))
                e, s = e_sb[:, u % NE, :n], s_bank[u % NS][:, :n]
                if top:
                    ins = nc.scalar.activation(e, s_sb[:, u % 3, :], ACT.Exp, bias=nmax[:, u:u + 1])
                else:
                    ins = nc.scalar.activation(e, s, ACT.Exp, bias=nmax[:, u:u + 1], accum_out=den[:, u:u + 1])
                ins.then_inc(sig["exp_done"].sem, sig["exp_done"].step())

            def take_scores(u):
                act.wait_ge(sig["s_done"].sem, sig["s_done"].at(u + 1))
                if u >= 3:
                    act.wait_ge(sig["prod_done"].sem, sig["prod_done"].at(u - 2))
                nc.scalar.activation(s_sb[:, u % 3, :], s_bank[u % NS][:], ACT.Copy).then_inc(
                    sig["s_taken"].sem, sig["s_taken"].step())

            def divide(u):
                act.wait_ge(sig["aux_dve"].sem, sig["aux_dve"].at(u + 1))
                e = e_sb[:, u % NE, :]
                nc.scalar.activation(e, e, ACT.Copy, scale=rden[:, u:u + 1]).then_inc(
                    sig["norm_rows"].sem, sig["norm_rows"].step())

            def copy(u):
                h, qt = units[u]
                n = chunks(qt)
                act.wait_ge(sig["turn_done"].sem, sig["turn_done"].at(u + 1))
                if h >= NTS:
                    act.wait_ge(sig["pv_done"].sem, sig["pv_done"].at((h - NTS) // 2 + 1))
                nc.scalar.activation(e_t[:, h % NTS, 0:n, qt * P:(qt + 1) * P],
                                     t_bank[u % NT2][:, :n * P].rearrange("p (k q) -> p k q", q=P), ACT.Copy).then_inc(
                    sig["turn_taken"].sem, sig["turn_taken"].step())

            def take(g):
                act.wait_ge(sig["pv_done"].sem, sig["pv_done"].at((g + 1) * per_group))
                if g >= 2:
                    act.wait_ge(sig["out_done"].sem, sig["out_done"].at(g - 1))
                nc.scalar.activation(o_t[:, g % 2, :], o_bank[g % 2][:], ACT.Copy).then_inc(
                    sig["o_done"].sem, sig["o_done"].step())

            if top:
                take_scores(0)
            for i in range(steps):
                if top and i + 1 < U:
                    take_scores(i + 1)
                if i < U:
                    exps(i)
                if top and 2 <= i < U + 2:
                    divide(i - 2)
                if LAG <= i < U + LAG:
                    copy(i - LAG)
                if i + 1 in group_at:
                    take(group_at[i + 1])
    core.end_region()



def context_attention(core, ctx, units, G, q_of, k_of, v_of, hd, scale, ident, tail=None, mask=None, stable=False,
                      finish=None):
    nc, sig = core.nc, core.sig

    def sb(name, shape, dt=F32):
        return ctx.enter_context(nc.sbuf_tensor(f"{name}_{nc.next_id()}", shape, dt))

    in_bank = {C: [slice(0, G)], 8: [slice(j, H, 4) for j in range(4)],
               64: [slice(8 * j + p, 8 * j + 8, 2) for j in range(2) for p in range(2)]}[hd]
    place = {g: (j, n) for j, s in enumerate(in_bank) for n, g in enumerate(range(s.start, s.stop, s.step or 1))}
    n_block = G // len(in_bank)
    s_bank = core.bank[0:4]
    t_bank = (core.bank[4], core.bank[7])
    o_bank = core.bank[5:7]
    e_sb = sb("ce_sb", [P, G, KC])
    s_sb = sb("cs_sb", [P, G, KC])
    t_sb = sb("ct_sb", [P, G, KC]) if stable else None
    e_t = sb("ce_t", [P, G, P])
    mx = sb("cmx", [P, G])
    den = sb("cden", [P, G])
    rden = sb("crden", [P, G])
    o_sb = sb("co_sb", [P, G * hd])
    HB = min(G, BANK // hd)
    NQ = G // 4
    if tail is not None:
        tail.o_sb = o_sb
    NU = len(units)

    with nc.Block() as block:
        @block.tensor
        def _(pe):
            def scores(u):
                if u >= 1:
                    pe.wait_ge(sig["s_taken"].sem, sig["s_taken"].at(u))
                for g in range(G):
                    j, n = place[g]
                    ins = nc.tensor.matmul(s_bank[j][:, n * KC:(n + 1) * KC],
                                           q_of(units[u], g), k_of(units[u], g), start=True, stop=True)
                ins.then_inc(sig["s_done"].sem, sig["s_done"].step())

            def turns(u):
                pe.wait_ge(sig["exp_done"].sem, sig["exp_done"].at(u + 1))
                for j in range(NQ):
                    n = NQ * u + j
                    if n >= 2:
                        pe.wait_ge(sig["turn_taken"].sem, sig["turn_taken"].at(n - 1))
                    for g in range(4 * j, 4 * j + 4):
                        ins = nc.tensor.transpose(t_bank[n % 2][:KC, (g % 4) * P:(g % 4 + 1) * P],
                                                  e_sb[:, g, :], ident)
                    ins.then_inc(sig["turn_done"].sem, sig["turn_done"].step())

            def values(u):
                if u >= 1:
                    pe.wait_ge(sig["o_done"].sem, sig["o_done"].at(u))
                    if tail is not None:
                        pe.wait_ge(sig["out_added"].sem, sig["out_added"].at(u))
                pe.wait_ge(sig["turn_taken"].sem, sig["turn_taken"].at(NQ * (u + 1)))
                for g in range(G):
                    ins = nc.tensor.matmul(o_bank[g // HB][:, (g % HB) * hd:(g % HB + 1) * hd], e_t[:KC, g, :],
                                           v_of(units[u], g), start=True, stop=True)
                ins.then_inc(sig["pv_done"].sem, sig["pv_done"].step())

            scores(0)
            for u in range(NU):
                if u + 1 < NU:
                    scores(u + 1)
                turns(u)
                if tail is not None and u >= 1:
                    tail.product(pe, u - 1)
                values(u)
                if tail is not None:
                    tail.turn(pe, u)
            if tail is not None:
                tail.product(pe, NU - 1)

        @block.vector
        def _(dve):
            link = core.dve_chain.link

            def front(u):
                dve.wait_ge(sig["s_done"].sem, sig["s_done"].at(u + 1))
                for j, g in enumerate(in_bank):
                    src = s_bank[j][:, :n_block * KC].rearrange("p (g k) -> p g k", k=KC)
                    if stable:
                        nc.vector.tensor_scalar(s_sb[:, g, :], src, scale, 0.0, ALU.mult, ALU.max)
                        ins = nc.vector.tensor_scalar(t_sb[:, g, :], src, scale, 0.0, ALU.mult, ALU.min)
                    elif mask is not None:
                        ins = nc.vector.scalar_tensor_tensor(out=s_sb[:, g, :], in0=src, scalar=scale,
                                                             in1=mask[0](units[u], g), op0=ALU.mult, op1=ALU.mult)
                    else:
                        ins = nc.vector.tensor_scalar(s_sb[:, g, :], src, scale, None, ALU.mult)
                ins.then_inc(sig["s_taken"].sem, sig["s_taken"].step())
                dve.wait_ge(sig["s_taken"].sem, sig["s_taken"].at(u + 1))
                if stable:
                    link(dve, nc.vector.tensor_scalar(t_sb[:], t_sb[:], -1.0, None, ALU.add))
                    link(dve, nc.vector.reciprocal(t_sb[:], t_sb[:]))
                    if u >= 1:
                        dve.wait_ge(sig["turn_done"].sem, sig["turn_done"].at(NQ * u))
                    nc.vector.tensor_tensor(e_sb[:], s_sb[:], t_sb[:], ALU.subtract).then_inc(
                        sig["exp_done"].sem, sig["exp_done"].step())
                    return
                if mask is not None:
                    link(dve, nc.vector.tensor_tensor(s_sb[:], s_sb[:], mask[1](units[u], slice(0, G)), ALU.add))
                link(dve, nc.vector.tensor_reduce(mx[:], s_sb[:], AXX, ALU.max))
                nc.vector.tensor_tensor(s_sb[:], s_sb[:], wide(mx[:], KC, 2), ALU.subtract).then_inc(
                    sig["max_done"].sem, sig["max_done"].step())

            def back(u):
                dve.wait_ge(sig["exp_done"].sem, sig["exp_done"].at(u + 1))
                link(dve, nc.vector.tensor_reduce(den[:], e_sb[:], AXX, ALU.add))
                link(dve, nc.vector.reciprocal(rden[:], den[:]))
                dve.wait_ge(sig["pv_done"].sem, sig["pv_done"].at(u + 1))
                if tail is not None and u >= 1:
                    dve.wait_ge(sig["t_turned"].sem, sig["t_turned"].at(tail.rounds() * u))
                for j in range(-(-G // HB)):
                    ins = nc.vector.tensor_tensor(
                        o_sb[:, j * HB * hd:(j + 1) * HB * hd].rearrange("p (h d) -> p h d", d=hd),
                        o_bank[j][:, :HB * hd].rearrange("p (h d) -> p h d", d=hd),
                        wide(rden[:, j * HB:(j + 1) * HB], hd, 2), ALU.mult)
                ins.then_inc(sig["o_done"].sem, sig["o_done"].step())
                if finish is not None:
                    dve.wait_ge(sig["o_done"].sem, sig["o_done"].at(u + 1))
                    finish(dve, u, o_sb)

            for u in range(NU):
                front(u)
                if tail is not None and u >= 1:
                    tail.add(dve, u - 1, units[u - 1])
                back(u)
            if tail is not None:
                tail.add(dve, NU - 1, units[NU - 1])

        @block.scalar
        def _(act):
            for u in range(NU):
                if not stable:
                    act.wait_ge(sig["max_done"].sem, sig["max_done"].at(u + 1))
                    if u >= 1:
                        act.wait_ge(sig["turn_done"].sem, sig["turn_done"].at(NQ * u))
                    nc.scalar.activation(e_sb[:], s_sb[:], ACT.Exp).then_inc(
                        sig["exp_done"].sem, sig["exp_done"].step())
                for j in range(NQ):
                    n = NQ * u + j
                    act.wait_ge(sig["turn_done"].sem, sig["turn_done"].at(n + 1))
                    if u >= 1:
                        act.wait_ge(sig["pv_done"].sem, sig["pv_done"].at(u))
                    nc.scalar.activation(e_t[:KC, 4 * j:4 * j + 4, :],
                                         t_bank[n % 2][:KC, :].rearrange("p (g q) -> p g q", q=P),
                                         ACT.Copy).then_inc(sig["turn_taken"].sem, sig["turn_taken"].step())
                if tail is not None:
                    tail.copy(act, u)

        @block.gpsimd
        def _(pool):
            if finish is not None:
                for u in range(NU):
                    pool.wait_ge(sig["norm_stats"].sem, sig["norm_stats"].at(u + 1))
                    nc.gpsimd.tensor_tensor(core.rstd[:, 0:G], core.spread[:, 0:G], core.minus_half[:, 0:G],
                                            ALU.pow).then_inc(sig["norm_scale"].sem, sig["norm_scale"].step())
    core.end_region()


def paired_context_attention(core, ctx, batches, q_of, k_pair, v_of, hd, dst, ident, wo, bo, mask=None,
                             stable=False):
    nc, sig = core.nc, core.sig
    units = [(b, p) for b in batches for p in range(H // 2)]
    U = len(units)
    per_group = 1 if hd == 64 else 2
    col = 64 if hd == 64 else 32
    BL = 2 * TB
    HALF = BL // 2 * KC

    def sb(name, shape, dt=F32):
        return ctx.enter_context(nc.sbuf_tensor(f"{name}_{nc.next_id()}", shape, dt))

    s_sb = sb("p_s", [P, 2, BL, KC])
    low = sb("p_low", [P, BL, KC]) if stable else None
    e_sb = sb("p_e", [P, 3, BL, KC])
    e_t = sb("p_et", [P, 2, 2, T])
    o_t = sb("p_ot", [P, 2, T])
    mx, den, rden = sb("p_mx", [P, U, BL]), sb("p_den", [P, U, BL]), sb("p_rden", [P, U, BL])
    t_bank, o_bank, y_bank = core.bank[4:6], core.bank[6], core.bank[7]
    group_end = {u: u // per_group for u in range(U) if u % per_group == per_group - 1}

    def s_bank(u, j):
        return core.bank[2 * (u % 2) + j]

    with nc.Block() as block:
        @block.tensor
        def _(pe):
            def scores(u):
                b, p = units[u]
                if u >= 2:
                    pe.wait_ge(sig["s_taken"].sem, sig["s_taken"].at(u - 1))
                for qt in range(TB):
                    ins = nc.tensor.matmul(s_bank(u, qt // 2)[:, qt % 2 * 2 * KC:(qt % 2 + 1) * 2 * KC],
                                           q_of(b, p, qt), k_pair(b, p), start=True, stop=True)
                ins.then_inc(sig["s_done"].sem, sig["s_done"].step())

            def turns(u):
                pe.wait_ge(sig["norm_rows"].sem, sig["norm_rows"].at(u + 1))
                for head in range(2):
                    if u >= 1:
                        pe.wait_ge(sig["turn_taken"].sem, sig["turn_taken"].at(2 * u + head - 1))
                    for qt in range(TB):
                        ins = nc.tensor.transpose(t_bank[head][:KC, qt * P:(qt + 1) * P],
                                                  e_sb[:, u % 3, 2 * qt + head, :], ident)
                    ins.then_inc(sig["turn_done"].sem, sig["turn_done"].step())

            def values(u):
                b, p = units[u]
                g = u // per_group
                pe.wait_ge(sig["turn_taken"].sem, sig["turn_taken"].at(2 * (u + 1)))
                if g >= 1 and u % per_group == 0:
                    pe.wait_ge(sig["o_done"].sem, sig["o_done"].at(g))
                for h in (2 * p, 2 * p + 1):
                    at = h * col % P
                    ins = nc.tensor.matmul(o_bank[at:at + col, :], v_of(b, h), e_t[:, u % 2, h % 2, :],
                                           start=True, stop=True)
                ins.then_inc(sig["pv_done"].sem, sig["pv_done"].step())

            def out(g):
                pe.wait_ge(sig["o_done"].sem, sig["o_done"].at(g + 1))
                if g >= 1:
                    pe.wait_ge(sig["out_added"].sem, sig["out_added"].at(g))
                slot = g % (H // 2 // per_group)
                for qt in range(TB):
                    y = y_bank[:, qt * C:(qt + 1) * C]
                    ins = nc.tensor.matmul(y, o_t[:, g % 2, qt * P:(qt + 1) * P], wo(slot), start=True, stop=slot > 0)
                    if slot == 0:
                        ins = nc.tensor.matmul(y, core.ones_row[0:1, :], bo, start=False, stop=True)
                ins.then_inc(sig["out_done"].sem, sig["out_done"].step())

            for i in range(U + 5):
                if i < U:
                    scores(i)
                if 0 <= i - 2 < U:
                    turns(i - 2)
                if 0 <= i - 3 < U:
                    values(i - 3)
                if i - 4 in group_end:
                    out(group_end[i - 4])

        @block.vector
        def _(dve):
            link = core.dve_chain.link

            def front(u):
                b, p = units[u]
                dve.wait_ge(sig["s_done"].sem, sig["s_done"].at(u + 1))
                if u >= 2:
                    dve.wait_ge(sig["exp_done"].sem, sig["exp_done"].at(u - 1))
                s = s_sb[:, u % 2]
                banks = [s_bank(u, j)[:, :HALF].rearrange("p (g k) -> p g k", k=KC) for j in range(2)]
                parts = [slice(0, TB), slice(TB, BL)]
                if stable:
                    if u >= 1:
                        dve.wait_ge(sig["exp_done"].sem, sig["exp_done"].at(u))
                    for bank, g in zip(banks, parts):
                        nc.vector.tensor_scalar(s[:, g, :], bank, 0.0, None, ALU.max)
                        ins = nc.vector.tensor_scalar(low[:, g, :], bank, 0.0, -1.0, ALU.min, ALU.add)
                    ins.then_inc(sig["s_taken"].sem, sig["s_taken"].step())
                    dve.wait_ge(sig["s_taken"].sem, sig["s_taken"].at(u + 1))
                    link(dve, nc.vector.reciprocal(low[:], low[:]))
                    if u >= 3:
                        dve.wait_ge(sig["turn_done"].sem, sig["turn_done"].at(2 * (u - 2)))
                    nc.vector.tensor_tensor(e_sb[:, u % 3], s, low[:], ALU.subtract).then_inc(
                        sig["exp_done"].sem, sig["exp_done"].step())
                    return
                if mask is None:
                    for bank, g in zip(banks, parts):
                        ins = nc.vector.tensor_reduce(mx[:, u, g], bank, AXX, ALU.max)
                    link(dve, ins)
                    for bank, g in zip(banks, parts):
                        ins = nc.vector.tensor_tensor(s[:, g, :], bank, wide(mx[:, u, g], KC, 2), ALU.subtract)
                    ins.then_inc(sig["s_taken"].sem, sig["s_taken"].step())
                    return
                for j, bank in enumerate(banks):
                    tiles = slice(b * TB + 2 * j, b * TB + 2 * j + 2)
                    out4 = s[:, parts[j], :].rearrange("p (t h) k -> p t h k", h=2)
                    in4 = bank.rearrange("p (t h) k -> p t h k", h=2)
                    ins = nc.vector.tensor_tensor(out4, in4, wide(mask[0][:, tiles, :], 2, 2), ALU.mult)
                ins.then_inc(sig["s_taken"].sem, sig["s_taken"].step())
                dve.wait_ge(sig["s_taken"].sem, sig["s_taken"].at(u + 1))
                s4 = s.rearrange("p (t h) k -> p t h k", h=2)
                link(dve, nc.vector.tensor_tensor(s4, s4, wide(mask[1][:, b * TB:(b + 1) * TB, :], 2, 2), ALU.add))
                link(dve, nc.vector.tensor_reduce(mx[:, u, :], s, AXX, ALU.max))
                nc.vector.tensor_tensor(s, s, wide(mx[:, u, :], KC, 2), ALU.subtract).then_inc(
                    sig["max_done"].sem, sig["max_done"].step())

            def factors(u):
                dve.wait_ge(sig["exp_done"].sem, sig["exp_done"].at(u + 1))
                link(dve, nc.vector.tensor_reduce(den[:, u, :], e_sb[:, u % 3], AXX, ALU.add))
                nc.vector.reciprocal(rden[:, u, :], den[:, u, :]).then_inc(sig["aux_dve"].sem, sig["aux_dve"].step())

            def add(g):
                b = units[g * per_group][0]
                dve.wait_ge(sig["out_done"].sem, sig["out_done"].at(g + 1))
                if g >= 1:
                    dve.wait_ge(sig["out_added"].sem, sig["out_added"].at(g))
                half = dst[:, b * TB:(b + 1) * TB, :].rearrange("p t c -> p (t c)")
                nc.vector.tensor_tensor(half, half, y_bank[:], ALU.add).then_inc(
                    sig["out_added"].sem, sig["out_added"].step())

            for i in range(U + 6):
                if i < U:
                    front(i)
                if 0 <= i - 1 < U:
                    factors(i - 1)
                if i - 5 in group_end:
                    add(group_end[i - 5])

        @block.gpsimd
        def _(pool):
            nc.gpsimd.memset(e_t[64:P], 0.0).then_inc(sig["aux_pool"].sem, sig["aux_pool"].step())
            pool.wait_ge(sig["aux_pool"].sem, sig["aux_pool"].at(1))
            for u in range(U):
                pool.wait_ge(sig["aux_dve"].sem, sig["aux_dve"].at(u + 1))
                e = e_sb[:, u % 3]
                nc.gpsimd.tensor_tensor(e, e, wide(rden[:, u, :], KC, 2), ALU.mult).then_inc(
                    sig["norm_rows"].sem, sig["norm_rows"].step())

        @block.scalar
        def _(act):
            def exps(u):
                ready = sig["s_taken"] if mask is None else sig["max_done"]
                act.wait_ge(ready.sem, ready.at(u + 1))
                if u >= 3:
                    act.wait_ge(sig["turn_done"].sem, sig["turn_done"].at(2 * (u - 2)))
                nc.scalar.activation(e_sb[:, u % 3], s_sb[:, u % 2], ACT.Exp).then_inc(
                    sig["exp_done"].sem, sig["exp_done"].step())

            def copies(u):
                for head in range(2):
                    act.wait_ge(sig["turn_done"].sem, sig["turn_done"].at(2 * u + head + 1))
                    if u >= 2:
                        act.wait_ge(sig["pv_done"].sem, sig["pv_done"].at(u - 1))
                    nc.scalar.activation(e_t[:KC, u % 2, head, :], t_bank[head][:KC, :], ACT.Copy).then_inc(
                        sig["turn_taken"].sem, sig["turn_taken"].step())

            def take(g):
                act.wait_ge(sig["pv_done"].sem, sig["pv_done"].at((g + 1) * per_group))
                if g >= 2:
                    act.wait_ge(sig["out_done"].sem, sig["out_done"].at(g - 1))
                nc.scalar.activation(o_t[:, g % 2, :], o_bank[:], ACT.Copy).then_inc(
                    sig["o_done"].sem, sig["o_done"].step())

            for i in range(U + 5):
                if i < U and not stable:
                    exps(i)
                if i == 2:
                    act.wait_ge(sig["aux_pool"].sem, sig["aux_pool"].at(1))
                if 0 <= i - 2 < U:
                    copies(i - 2)
                if i - 3 in group_end:
                    take(group_end[i - 3])
    core.end_region()


def spread_keys(core, outs, zeros):
    nc = core.nc
    with nc.Block() as block:
        @block.gpsimd
        def _(pool):
            for z in zeros:
                nc.gpsimd.memset(z, 0.0)

        @block.vector
        def _(dve):
            for dst, keys, masks in outs:
                nc.vector.tensor_tensor(dst, keys, masks, ALU.mult)
    core.end_region()



def route(core, ctx, wr, row, k, tri, tiles=NT):
    nc, sig = core.nc, core.sig
    E = 8

    def sb(name, shape):
        return ctx.enter_context(nc.sbuf_tensor(f"{name}_{nc.next_id()}", shape, F32))

    logits, gates, ex = sb("logits", [P, NT, E]), sb("gates", [P, NT, E]), sb("gate_exp", [P, NT, E])
    larger, equal = sb("larger", [P, NT, E, E]), sb("equal", [P, NT, E, E])
    rank, mx, tot = sb("rank", [P, NT, E]), sb("gate_max", [P, NT]), sb("gate_sum", [P, NT])
    with nc.Block() as block:
        @block.tensor
        def _(pe):
            for t in range(NT):
                out = core.bank[0][:, t * E:(t + 1) * E]
                ins = nc.tensor.matmul(out, core.xn_t[:, t * P:(t + 1) * P], wr, start=True, stop=row is None)
                if row is not None:
                    ins = nc.tensor.matmul(out, core.ones_row[0:1, :], row, start=False, stop=True)
            ins.then_inc(sig["mm_done"].sem, sig["mm_done"].step())

        @block.vector
        def _(dve):
            link = core.dve_chain.link
            dve.wait_ge(sig["mm_done"].sem, sig["mm_done"].at(1))
            link(dve, nc.vector.tensor_copy(logits[:], core.bank[0][:, :NT * E].rearrange("p (t e) -> p t e", e=E)))
            mine = wide(logits[:], E, 3)
            other = wide(logits[:], E, 2)
            nc.vector.tensor_tensor(larger[:], other, mine, ALU.is_gt)
            link(dve, nc.vector.tensor_tensor(equal[:], other, mine, ALU.is_equal))
            link(dve, nc.vector.tensor_tensor(
                equal[:].rearrange("p t e j -> p t (e j)"), equal[:].rearrange("p t e j -> p t (e j)"),
                wide(tri, NT, 1), ALU.mult))
            link(dve, nc.vector.tensor_tensor(larger[:], larger[:], equal[:], ALU.add))
            nc.vector.tensor_reduce(mx[:], logits[:], AXX, ALU.max)
            link(dve, nc.vector.tensor_reduce(rank[:], larger[:], AXX, ALU.add))
            nc.vector.tensor_tensor(ex[:], logits[:], wide(mx[:], E, 2), ALU.subtract).then_inc(
                sig["max_done"].sem, sig["max_done"].step())
            dve.wait_ge(sig["exp_done"].sem, sig["exp_done"].at(1))
            link(dve, nc.vector.tensor_scalar(rank[:], rank[:], float(k), None, ALU.is_lt))
            link(dve, nc.vector.tensor_tensor(gates[:], ex[:], rank[:], ALU.mult))
            link(dve, nc.vector.tensor_reduce(tot[:], gates[:], AXX, ALU.add))
            link(dve, nc.vector.reciprocal(tot[:], tot[:]))
            nc.vector.tensor_tensor(gates[:], gates[:], wide(tot[:], E, 2), ALU.mult)

        @block.scalar
        def _(act):
            act.wait_ge(sig["max_done"].sem, sig["max_done"].at(1))
            nc.scalar.activation(ex[:], ex[:], ACT.Exp).then_inc(sig["exp_done"].sem, sig["exp_done"].step())
    core.end_region()
    return gates



def feed_forward(core, ctx, dst, jobs, gates=None):
    nc, sig = core.nc, core.sig
    hid = ctx.enter_context(nc.sbuf_tensor(f"hid_{nc.next_id()}", [P, 2, 4, BANK], F32))
    silu = ctx.enter_context(nc.sbuf_tensor(f"silu_{nc.next_id()}", [P, 2, BANK], F32))
    runs = [(j, half) for j in jobs for half in range(B)]
    chunks = [(r, c) for r, (j, half) in enumerate(runs) for c in range(j[5])]
    first = {r: sum(j[5] for j, _ in runs[:r]) for r in range(len(runs) + 1)}
    gated = [n for n, (r, c) in enumerate(chunks) if runs[r][0][1] is not None]

    def hidden_ready(eng, n):
        if n in gated:
            eng.wait_ge(sig["prod_done"].sem, sig["prod_done"].at(gated.index(n) + 1))
        else:
            eng.wait_ge(sig["act_done"].sem, sig["act_done"].at(n + 1))

    with nc.Block() as block:
        @block.tensor
        def _(pe):
            def up(n):
                r, c = chunks[n]
                (w, second, down, bias, fn, nch, gate), half = runs[r]
                if n >= 2:
                    hidden_ready(pe, n - 2)
                x = core.xn_t[:, half * T:(half + 1) * T]
                m = w(c).shape[-1]
                ins = nc.tensor.matmul(core.bank[n % 2][:m, :], w(c), x, start=True, stop=True)
                if second is not None:
                    ins = nc.tensor.matmul(core.bank[2 + n % 2][:m, :], second(c), x, start=True, stop=True)
                ins.then_inc(sig["mm_done"].sem, sig["mm_done"].step())

            def down_part(r):
                (w, second, down, bias, fn, nch, gate), half = runs[r]
                hidden_ready(pe, first[r + 1] - 1)
                if r >= 2:
                    pe.wait_ge(sig["y_added"].sem, sig["y_added"].at(r - 1))
                m = w(0).shape[-1]
                for t in range(TB):
                    out = core.bank[4 + r % 2][:, t * P:(t + 1) * P]
                    for c in range(nch):
                        ins = nc.tensor.matmul(out, hid[:m, r % 2, c, t * P:(t + 1) * P], down(c),
                                               start=c == 0, stop=c == nch - 1)
                ins.then_inc(sig["y_done"].sem, sig["y_done"].step())

            for n in range(len(chunks)):
                r, c = chunks[n]
                up(n)
                if r >= 1 and c == runs[r][0][5] - 1:
                    down_part(r - 1)
            down_part(len(runs) - 1)

        @block.scalar
        def _(act):
            for n, (r, c) in enumerate(chunks):
                (w, second, down, bias, fn, nch, gate), half = runs[r]
                act.wait_ge(sig["mm_done"].sem, sig["mm_done"].at(n + 1))
                m = w(c).shape[-1]
                if second is not None:
                    if n >= 2:
                        act.wait_ge(sig["prod_done"].sem, sig["prod_done"].at(gated.index(n) - 1))
                    out = silu[:m, n % 2, :]
                else:
                    if r >= 2:
                        act.wait_ge(sig["y_done"].sem, sig["y_done"].at(r - 1))
                    out = hid[:m, r % 2, c, :]
                nc.scalar.activation(out, core.bank[n % 2][:m, :], fn, bias=0.0 if bias is None else bias(c)).then_inc(
                    sig["act_done"].sem, sig["act_done"].step())

        @block.vector
        def _(dve):
            def add(r):
                (w, second, down, bias, fn, nch, gate), half = runs[r]
                dve.wait_ge(sig["y_done"].sem, sig["y_done"].at(r + 1))
                if r >= 1:
                    dve.wait_ge(sig["y_added"].sem, sig["y_added"].at(r))
                bank = core.bank[4 + r % 2]
                if gate is None:
                    ins = nc.vector.tensor_tensor(dst[:, half * TB:(half + 1) * TB, :].rearrange("p t c -> p (t c)"),
                                                  dst[:, half * TB:(half + 1) * TB, :].rearrange("p t c -> p (t c)"),
                                                  bank[:], ALU.add)
                else:
                    for t in range(TB):
                        tile = half * TB + t
                        ins = nc.vector.scalar_tensor_tensor(
                            out=dst[:, tile, :], in0=bank[:, t * P:(t + 1) * P],
                            scalar=gates[:, tile, gate:gate + 1], in1=dst[:, tile, :], op0=ALU.mult, op1=ALU.add)
                ins.then_inc(sig["y_added"].sem, sig["y_added"].step())

            for n, (r, c) in enumerate(chunks):
                (w, second, down, bias, fn, nch, gate), half = runs[r]
                if second is not None:
                    dve.wait_ge(sig["act_done"].sem, sig["act_done"].at(n + 1))
                    if r >= 2:
                        dve.wait_ge(sig["y_done"].sem, sig["y_done"].at(r - 1))
                    m = w(c).shape[-1]
                    nc.vector.tensor_tensor(hid[:m, r % 2, c, :], silu[:m, n % 2, :], core.bank[2 + n % 2][:m, :],
                                            ALU.mult).then_inc(sig["prod_done"].sem, sig["prod_done"].step())
                if r >= 1 and c == nch - 1:
                    add(r - 1)
            add(len(runs) - 1)
    core.end_region()


def add_rows(core, dst, row):
    nc, sig = core.nc, core.sig
    with nc.Block() as block:
        @block.tensor
        def _(pe):
            for t in range(TB):
                ins = nc.tensor.matmul(core.bank[7][:, t * P:(t + 1) * P], core.ones_row[0:1, :], row,
                                       start=True, stop=True)
            ins.then_inc(sig["mm_done"].sem, sig["mm_done"].step())

        @block.vector
        def _(dve):
            dve.wait_ge(sig["mm_done"].sem, sig["mm_done"].at(1))
            for half in range(B):
                nc.vector.tensor_tensor(dst[:, half * TB:(half + 1) * TB, :].rearrange("p t c -> p (t c)"),
                                        dst[:, half * TB:(half + 1) * TB, :].rearrange("p t c -> p (t c)"),
                                        core.bank[7][:], ALU.add)
    core.end_region()



def gated_recurrence(core, ctx, w_hg, ident):
    nc, sig = core.nc, core.sig

    def sb(name):
        return ctx.enter_context(nc.sbuf_tensor(f"{name}_{nc.next_id()}", [P, B, T], F32))

    decay, update, low, value, state = sb("decay"), sb("update"), sb("low"), sb("value"), sb("state")
    with nc.Block() as block:
        @block.tensor
        def _(pe):
            for b in range(B):
                for j in range(2):
                    ins = nc.tensor.matmul(core.bank[2 * b + j][:], w_hg[:, j * P:(j + 1) * P],
                                           core.xn_t[:, b * T:(b + 1) * T], start=True, stop=True)
                ins.then_inc(sig["mm_done"].sem, sig["mm_done"].step())
            for b in range(B):
                pe.wait_ge(sig["prod_done"].sem, sig["prod_done"].at(b + 1))
                for t in range(TB):
                    ins = nc.tensor.transpose(core.bank[4 + b][:, t * P:(t + 1) * P],
                                              state[:, b, t * P:(t + 1) * P], ident)
                ins.then_inc(sig["turn_done"].sem, sig["turn_done"].step())

        @block.scalar
        def _(act):
            for b in range(B):
                act.wait_ge(sig["mm_done"].sem, sig["mm_done"].at(b + 1))
                nc.scalar.activation(decay[:, b, :], core.bank[2 * b + 1][:], ACT.Sigmoid, scale=-1.0)
                nc.scalar.activation(update[:, b, :], core.bank[2 * b + 1][:], ACT.Sigmoid)
                act.wait_ge(sig["aux_dve"].sem, sig["aux_dve"].at(b + 1))
                nc.scalar.activation(value[:, b, :], low[:, b, :], ACT.Sigmoid).then_inc(
                    sig["act_done"].sem, sig["act_done"].step())

        @block.vector
        def _(dve):
            link = core.dve_chain.link
            for b in range(B):
                dve.wait_ge(sig["mm_done"].sem, sig["mm_done"].at(b + 1))
                nc.vector.tensor_scalar(low[:, b, :], core.bank[2 * b][:], 0.0, None, ALU.min).then_inc(
                    sig["aux_dve"].sem, sig["aux_dve"].step())
            for b in range(B):
                dve.wait_ge(sig["act_done"].sem, sig["act_done"].at(b + 1))
                link(dve, nc.vector.scalar_tensor_tensor(out=value[:, b, :], in0=core.bank[2 * b][:], scalar=0.0,
                                                         in1=value[:, b, :], op0=ALU.max, op1=ALU.add))
                link(dve, nc.vector.tensor_tensor(value[:, b, :], value[:, b, :], update[:, b, :], ALU.mult))
                nc.vector.tensor_tensor_scan(out=state[:, b, :], data0=decay[:, b, :], data1=value[:, b, :],
                                             initial=0.0, op0=ALU.mult, op1=ALU.add).then_inc(
                    sig["prod_done"].sem, sig["prod_done"].step())
            for b in range(B):
                dve.wait_ge(sig["turn_done"].sem, sig["turn_done"].at(b + 1))
                half = core.x_sb[:, b * TB:(b + 1) * TB, :].rearrange("p t c -> p (t c)")
                nc.vector.tensor_tensor(half, half, core.bank[4 + b][:], ALU.add)
    core.end_region()


def state_space(core, ctx, w):
    nc, sig = core.nc, core.sig
    S = 16

    def sb(name, shape):
        return ctx.enter_context(nc.sbuf_tensor(f"{name}_{nc.next_id()}", shape, F32))

    z, low = sb("delta_in", [P, B, T]), sb("delta_low", [P, B, T])
    dbar, decay, bt, ct, hs = (sb(n, [S, B, T]) for n in ("dbar", "ss_decay", "ss_bt", "ss_ct", "ss_h"))
    sa, ysum = sb("ss_a", [S, 1]), sb("ss_y", [P, NT])
    with nc.Block() as block:
        @block.tensor
        def _(pe):
            for b in range(B):
                x = core.xn_t[:, b * T:(b + 1) * T]
                nc.tensor.matmul(core.bank[b][:], w["ss_wd"], x, start=True, stop=True)
                nc.tensor.matmul(core.bank[2 + b][:S, :], w["ss_wb"], x, start=True, stop=True)
                ins = nc.tensor.matmul(core.bank[4 + b][:S, :], w["ss_wc"], x, start=True, stop=True)
                ins.then_inc(sig["mm_done"].sem, sig["mm_done"].step())
            nc.tensor.matmul(core.bank[6][:S, 0:1], w["ss_a"], w["mean_col"][:, 0:1], start=True, stop=True).then_inc(
                sig["aux_pe"].sem, sig["aux_pe"].step())
            for b in range(B):
                pe.wait_ge(sig["prod_done"].sem, sig["prod_done"].at(b + 1))
                nc.tensor.matmul(core.bank[b][:S, :], w["mean_col"], z[:, b, :], start=True, stop=True).then_inc(
                    sig["s_done"].sem, sig["s_done"].step())
            for b in range(B):
                pe.wait_ge(sig["o_done"].sem, sig["o_done"].at(b + 1))
                if b == 0:
                    pe.wait_ge(sig["aux_dve"].sem, sig["aux_dve"].at(1))
                for t in range(TB):
                    ins = nc.tensor.matmul(core.bank[6 + b][:, t:t + 1],
                                           hs[:, b, t * P:(t + 1) * P], w["ones"][:S, 0:1], start=True, stop=True)
                ins.then_inc(sig["pv_done"].sem, sig["pv_done"].step())
            for b in range(B):
                pe.wait_ge(sig["act_done"].sem, sig["act_done"].at(2 * b + 2))
                for t in range(TB):
                    tile = b * TB + t
                    nc.tensor.matmul(core.bank[2 + b][:, t * P:(t + 1) * P], core.xn_t[:, tile * P:(tile + 1) * P],
                                     w["ss_wo"], start=True, stop=True)
                    ins = nc.tensor.matmul(core.bank[4 + b][:, t * P:(t + 1) * P], core.ones_row[0:1, :],
                                           w["ss_bo"], start=True, stop=True)
                ins.then_inc(sig["y_done"].sem, sig["y_done"].step())

        @block.scalar
        def _(act):
            for b in range(B):
                act.wait_ge(sig["mm_done"].sem, sig["mm_done"].at(b + 1))
                nc.scalar.activation(bt[:, b, :], core.bank[2 + b][:S, :], ACT.Identity, bias=w["ss_bb"][:S, :]).then_inc(
                    sig["act_done"].sem, sig["act_done"].step())
                nc.scalar.activation(ct[:, b, :], core.bank[4 + b][:S, :], ACT.Identity, bias=w["ss_bc"][:S, :]).then_inc(
                    sig["act_done"].sem, sig["act_done"].step())
            for b in range(B):
                act.wait_ge(sig["aux_dve"].sem, sig["aux_dve"].at(b + 2))
                nc.scalar.activation(low[:, b, :], low[:, b, :], ACT.Exp, scale=-1.0).then_inc(
                    sig["aux_act"].sem, sig["aux_act"].step())
            for b in range(B):
                act.wait_ge(sig["aux_act"].sem, sig["aux_act"].at(b + 1))
                nc.scalar.activation(low[:, b, :], low[:, b, :], ACT.Ln, bias=1.0).then_inc(
                    sig["exp_done"].sem, sig["exp_done"].step())
            act.wait_ge(sig["aux_dve"].sem, sig["aux_dve"].at(1))
            nc.scalar.activation(sa[:], sa[:], ACT.Sigmoid).then_inc(sig["max_done"].sem, sig["max_done"].step())

        @block.vector
        def _(dve):
            link = core.dve_chain.link
            dve.wait_ge(sig["aux_pe"].sem, sig["aux_pe"].at(1))
            nc.vector.tensor_copy(sa[:], core.bank[6][:S, 0:1]).then_inc(sig["aux_dve"].sem, sig["aux_dve"].step())
            for b in range(B):
                link(dve, nc.vector.tensor_scalar(z[:, b, :], core.bank[b][:], w["ss_bd"], None, ALU.add))
                nc.vector.scalar_tensor_tensor(out=low[:, b, :], in0=z[:, b, :], scalar=-1.0, in1=z[:, b, :],
                                               op0=ALU.mult, op1=ALU.max).then_inc(
                    sig["aux_dve"].sem, sig["aux_dve"].step())
            for b in range(B):
                dve.wait_ge(sig["exp_done"].sem, sig["exp_done"].at(b + 1))
                nc.vector.scalar_tensor_tensor(out=z[:, b, :], in0=z[:, b, :], scalar=0.0, in1=low[:, b, :],
                                               op0=ALU.max, op1=ALU.add).then_inc(
                    sig["prod_done"].sem, sig["prod_done"].step())
            dve.wait_ge(sig["max_done"].sem, sig["max_done"].at(1))
            dve.wait_ge(sig["act_done"].sem, sig["act_done"].at(2 * B))
            for b in range(B):
                dve.wait_ge(sig["s_done"].sem, sig["s_done"].at(b + 1))
                nc.vector.tensor_scalar(decay[:, b, :], core.bank[b][:S, :], -1.0, 1.0, ALU.mult, ALU.add)
                link(dve, nc.vector.tensor_tensor(bt[:, b, :], core.bank[b][:S, :], bt[:, b, :], ALU.mult))
                link(dve, nc.vector.tensor_scalar(bt[:, b, :], bt[:, b, :], sa[:], None, ALU.mult))
                link(dve, nc.vector.tensor_tensor_scan(out=hs[:, b, :], data0=decay[:, b, :], data1=bt[:, b, :],
                                                       initial=0.0, op0=ALU.mult, op1=ALU.add))
                nc.vector.tensor_tensor(hs[:, b, :], hs[:, b, :], ct[:, b, :], ALU.mult).then_inc(
                    sig["o_done"].sem, sig["o_done"].step())
            for b in range(B):
                dve.wait_ge(sig["pv_done"].sem, sig["pv_done"].at(b + 1))
                link(dve, nc.vector.tensor_copy(ysum[:, b * TB:(b + 1) * TB], core.bank[6 + b][:, 0:TB]))
                dve.wait_ge(sig["y_done"].sem, sig["y_done"].at(b + 1))
                for t in range(TB):
                    tile = b * TB + t
                    ins = nc.vector.scalar_tensor_tensor(
                        out=core.x_sb[:, tile, :], in0=core.bank[2 + b][:, t * P:(t + 1) * P],
                        scalar=ysum[:, tile:tile + 1], in1=core.x_sb[:, tile, :], op0=ALU.mult, op1=ALU.add)
                link(dve, ins)
                half = core.x_sb[:, b * TB:(b + 1) * TB, :].rearrange("p t c -> p (t c)")
                nc.vector.tensor_tensor(half, half, core.bank[4 + b][:], ALU.add)
    core.end_region()



def bit_feed_forward(core, ctx, w1_t, w2_t, b1_rows, b2_row, ident, ones):
    nc, sig = core.nc, core.sig
    F = 4 * P

    def sb(name, shape, dt=F32):
        return ctx.enter_context(nc.sbuf_tensor(f"{name}_{nc.next_id()}", shape, dt))

    asum, wmean, wscale = sb("asum", [P, 2]), sb("wmean", [P, 2]), sb("wscale", [P, 2])
    wtmp = sb("wtmp", [P, F])
    w1q, w2q = sb("w1q", [P, F], BF16), sb("w2q", [P, F], BF16)
    sq = sb("sq", [P, NT, C])
    ms, amax, qscale, step1 = (sb(n, [P, NT]) for n in ("ms", "amax", "qscale", "step1"))
    ms2, amax2, qscale2, step2, r2, inv2 = (sb(n, [P, NT]) for n in ("ms2", "amax2", "qscale2", "step2", "r2", "inv2"))
    xq_t = sb("xq_t", [P, NT, P], BF16)
    hid = sb("bhid", [P, 2, F])
    sq2 = sb("sq2", [P, F])
    hq_t = sb("hq_t", [P, 2, 4, P], BF16)

    with nc.Block() as block:
        @block.vector
        def _(dve):
            link = core.dve_chain.link
            nc.vector.tensor_reduce(asum[:, 0:1], w1_t, AXX, ALU.add, apply_absolute_value=True)
            nc.vector.tensor_reduce(asum[:, 1:2], w2_t, AXX, ALU.add, apply_absolute_value=True).then_inc(
                sig["aux_dve"].sem, sig["aux_dve"].step())
            link(dve, nc.vector.tensor_tensor(sq[:], core.xn[:], core.xn[:], ALU.mult))
            link(dve, nc.vector.tensor_reduce(ms[:], sq[:], AXX, ALU.add))
            nc.vector.tensor_scalar(core.spread[:], ms[:], 1.0 / C, 1e-5, ALU.mult, ALU.add).then_inc(
                sig["norm_stats"].sem, sig["norm_stats"].step())
            dve.wait_ge(sig["aux_pe"].sem, sig["aux_pe"].at(1))
            link(dve, nc.vector.tensor_scalar(wmean[:], core.bank[0][:, 0:2], 1.0 / (C * F), 1e-5, ALU.mult, ALU.max))
            link(dve, nc.vector.reciprocal(wscale[:], wmean[:]))
            for j, (w, q) in enumerate(((w1_t, w1q), (w2_t, w2q))):
                link(dve, nc.vector.tensor_scalar(wtmp[:], w, wscale[:, j:j + 1], ROUND, ALU.mult, ALU.add))
                link(dve, nc.vector.tensor_scalar(wtmp[:], wtmp[:], -ROUND, 1.0, ALU.add, ALU.min))
                link(dve, nc.vector.tensor_scalar(q[:], wtmp[:], -1.0, None, ALU.max))
            dve.wait_ge(sig["norm_scale"].sem, sig["norm_scale"].at(1))
            link(dve, nc.vector.tensor_tensor(core.xn[:], core.xn[:], wide(core.rstd[:], C, 2), ALU.mult))
            link(dve, nc.vector.tensor_reduce(amax[:], core.xn[:], AXX, ALU.max, apply_absolute_value=True))
            link(dve, nc.vector.tensor_scalar(amax[:], amax[:], 1e-5, None, ALU.max))
            link(dve, nc.vector.reciprocal(qscale[:], amax[:]))
            link(dve, nc.vector.tensor_scalar(qscale[:], qscale[:], 127.0, None, ALU.mult))
            link(dve, nc.vector.tensor_scalar(step1[:], amax[:], wmean[:, 0:1], 1.0 / 127.0, ALU.mult, ALU.mult))
            link(dve, nc.vector.tensor_tensor(core.xn[:], core.xn[:], wide(qscale[:], C, 2), ALU.mult))
            link(dve, nc.vector.tensor_scalar(core.xn[:], core.xn[:], ROUND, None, ALU.add))
            nc.vector.tensor_scalar(core.xn[:], core.xn[:], -ROUND, None, ALU.add).then_inc(
                sig["norm_rows"].sem, sig["norm_rows"].step())

        @block.gpsimd
        def _(pool):
            pool.wait_ge(sig["norm_stats"].sem, sig["norm_stats"].at(1))
            nc.gpsimd.tensor_tensor(core.rstd[:], core.spread[:], core.minus_half[:], ALU.pow).then_inc(
                sig["norm_scale"].sem, sig["norm_scale"].step())

        @block.tensor
        def _(pe):
            pe.wait_ge(sig["aux_dve"].sem, sig["aux_dve"].at(1))
            nc.tensor.matmul(core.bank[0][:, 0:2], ones, asum[:], start=True, stop=True).then_inc(
                sig["aux_pe"].sem, sig["aux_pe"].step())
            pe.wait_ge(sig["norm_rows"].sem, sig["norm_rows"].at(1))
            for t in range(NT):
                ins = nc.tensor.transpose(core.bank[1 + t // TB][:, (t % TB) * P:(t % TB + 1) * P],
                                          core.xn[:, t, :], ident)
            ins.then_inc(sig["norm_turned"].sem, sig["norm_turned"].step())

        @block.scalar
        def _(act):
            act.wait_ge(sig["norm_turned"].sem, sig["norm_turned"].at(1))
            for b in range(B):
                nc.scalar.activation(xq_t[:, b * TB:(b + 1) * TB, :].rearrange("p t c -> p (t c)"),
                                     core.bank[1 + b][:], ACT.Copy)
    core.end_region()

    with nc.Block() as block:
        @block.tensor
        def _(pe):
            def first(t):
                if t >= 2:
                    pe.wait_ge(sig["s_taken"].sem, sig["s_taken"].at(t - 1))
                nc.tensor.matmul(core.bank[t % 2][:], xq_t[:, t, :], w1q[:], start=True, stop=True).then_inc(
                    sig["mm_done"].sem, sig["mm_done"].step())

            first(0)
            for t in range(NT):
                if t + 1 < NT:
                    first(t + 1)
                pe.wait_ge(sig["prod_done"].sem, sig["prod_done"].at(t + 1))
                if t >= 2:
                    pe.wait_ge(sig["turn_taken"].sem, sig["turn_taken"].at(t - 1))
                for c in range(4):
                    ins = nc.tensor.transpose(core.bank[2 + t % 2][:, c * P:(c + 1) * P],
                                              hid[:, t % 2, c * P:(c + 1) * P], ident)
                ins.then_inc(sig["turn_done"].sem, sig["turn_done"].step())
                pe.wait_ge(sig["turn_taken"].sem, sig["turn_taken"].at(t + 1))
                if t >= 2:
                    pe.wait_ge(sig["y_added"].sem, sig["y_added"].at(t - 1))
                for c in range(4):
                    nc.tensor.matmul(core.bank[4 + t % 2][:, 0:C], hq_t[:, t % 2, c, :], w2q[:, c * P:(c + 1) * P],
                                     start=c == 0, stop=c == 3)
                nc.tensor.matmul(core.bank[6 + t % 2][:, 0:C], core.ones_row[0:1, :], b2_row, start=True,
                                 stop=True).then_inc(sig["y_done"].sem, sig["y_done"].step())

        @block.scalar
        def _(act):
            for t in range(NT):
                act.wait_ge(sig["s_taken"].sem, sig["s_taken"].at(t + 1))
                nc.scalar.activation(hid[:, t % 2, :], hid[:, t % 2, :], ACT.Gelu).then_inc(
                    sig["act_done"].sem, sig["act_done"].step())
                act.wait_ge(sig["turn_done"].sem, sig["turn_done"].at(t + 1))
                if t >= 2:
                    act.wait_ge(sig["y_done"].sem, sig["y_done"].at(t - 1))
                nc.scalar.activation(hq_t[:, t % 2, :, :].rearrange("p c q -> p (c q)"), core.bank[2 + t % 2][:],
                                     ACT.Copy).then_inc(sig["turn_taken"].sem, sig["turn_taken"].step())

        @block.gpsimd
        def _(pool):
            for t in range(NT):
                pool.wait_ge(sig["norm_stats"].sem, sig["norm_stats"].at(t + 1))
                nc.gpsimd.tensor_tensor(r2[:, t:t + 1], ms2[:, t:t + 1], core.minus_half[:, 0:1], ALU.pow).then_inc(
                    sig["norm_scale"].sem, sig["norm_scale"].step())

        @block.vector
        def _(dve):
            link = core.dve_chain.link

            def col(a, t):
                return a[:, t:t + 1]

            def dequant(t):
                dve.wait_ge(sig["mm_done"].sem, sig["mm_done"].at(t + 1))
                if t >= 2:
                    dve.wait_ge(sig["turn_done"].sem, sig["turn_done"].at(t - 1))
                nc.vector.scalar_tensor_tensor(out=hid[:, t % 2, :], in0=core.bank[t % 2][:], scalar=col(step1, t),
                                               in1=b1_rows, op0=ALU.mult, op1=ALU.add).then_inc(
                    sig["s_taken"].sem, sig["s_taken"].step())

            for t in range(NT):
                dequant(t)
                h = hid[:, t % 2, :]
                dve.wait_ge(sig["act_done"].sem, sig["act_done"].at(t + 1))
                nc.vector.tensor_reduce(col(amax2, t), h, AXX, ALU.max, apply_absolute_value=True)
                link(dve, nc.vector.tensor_tensor(sq2[:], h, h, ALU.mult))
                link(dve, nc.vector.tensor_reduce(col(ms2, t), sq2[:], AXX, ALU.add))
                link(dve, nc.vector.tensor_scalar(col(ms2, t), col(ms2, t), 1.0 / F, 1e-5, ALU.mult, ALU.add))
                nc.vector.tensor_copy(col(inv2, t), col(ms2, t)).then_inc(sig["norm_stats"].sem, sig["norm_stats"].step())
                dve.wait_ge(sig["norm_scale"].sem, sig["norm_scale"].at(t + 1))
                link(dve, nc.vector.tensor_scalar(col(amax2, t), col(amax2, t), col(r2, t), 1e-5, ALU.mult, ALU.max))
                link(dve, nc.vector.reciprocal(col(qscale2, t), col(amax2, t)))
                link(dve, nc.vector.tensor_scalar(col(qscale2, t), col(qscale2, t), 127.0, None, ALU.mult))
                nc.vector.tensor_scalar(col(step2, t), col(amax2, t), wmean[:, 1:2], 1.0 / 127.0, ALU.mult, ALU.mult)
                link(dve, nc.vector.tensor_scalar(h, h, col(r2, t), col(qscale2, t), ALU.mult, ALU.mult))
                link(dve, nc.vector.tensor_scalar(h, h, ROUND, None, ALU.add))
                nc.vector.tensor_scalar(h, h, -ROUND, None, ALU.add).then_inc(
                    sig["prod_done"].sem, sig["prod_done"].step())
                dve.wait_ge(sig["y_done"].sem, sig["y_done"].at(t + 1))
                link(dve, nc.vector.scalar_tensor_tensor(out=core.x_sb[:, t, :], in0=core.bank[4 + t % 2][:, 0:C],
                                                         scalar=col(step2, t), in1=core.x_sb[:, t, :],
                                                         op0=ALU.mult, op1=ALU.add))
                nc.vector.tensor_tensor(core.x_sb[:, t, :], core.x_sb[:, t, :], core.bank[6 + t % 2][:, 0:C],
                                        ALU.add).then_inc(sig["y_added"].sem, sig["y_added"].step())
    core.end_region()



def linear_experts(core, ctx, w_in, w_out_t, gates):
    nc, sig = core.nc, core.sig
    E = 8
    both = ctx.enter_context(nc.sbuf_tensor("expert_product", [P, E, C], F32))
    with nc.Block() as block:
        @block.tensor
        def _(pe):
            for e in range(E):
                for c in range(4):
                    k = (e * 4 + c) * P
                    ins = nc.tensor.matmul(core.bank[e // 4][:, (e % 4) * C:(e % 4 + 1) * C], w_in[:, k:k + P],
                                           w_out_t[:, k:k + P], start=c == 0, stop=c == 3)
                if e % 4 == 3:
                    ins.then_inc(sig["mm_done"].sem, sig["mm_done"].step())
            pe.wait_ge(sig["act_done"].sem, sig["act_done"].at(2))
            for n in range(2 * NT):
                t, half = n // 2, n % 2
                if n >= 4:
                    pe.wait_ge(sig["y_added"].sem, sig["y_added"].at(n - 3))
                nc.tensor.matmul(core.bank[2 + n % 4][:], core.xn_t[:, t * P:(t + 1) * P],
                                 both[:, 4 * half:4 * half + 4, :].rearrange("p e c -> p (e c)"),
                                 start=True, stop=True).then_inc(sig["y_done"].sem, sig["y_done"].step())

        @block.scalar
        def _(act):
            for half in range(2):
                act.wait_ge(sig["mm_done"].sem, sig["mm_done"].at(half + 1))
                nc.scalar.activation(both[:, 4 * half:4 * half + 4, :].rearrange("p e c -> p (e c)"),
                                     core.bank[half][:], ACT.Copy).then_inc(
                    sig["act_done"].sem, sig["act_done"].step())

        @block.vector
        def _(dve):
            link = core.dve_chain.link
            for n in range(2 * NT):
                t, half = n // 2, n % 2
                dve.wait_ge(sig["y_done"].sem, sig["y_done"].at(n + 1))
                for e in range(4):
                    g = 4 * half + e
                    ins = nc.vector.scalar_tensor_tensor(
                        out=core.x_sb[:, t, :], in0=core.bank[2 + n % 4][:, e * C:(e + 1) * C],
                        scalar=gates[:, t, g:g + 1], in1=core.x_sb[:, t, :], op0=ALU.mult, op1=ALU.add)
                    if e < 3:
                        link(dve, ins)
                ins.then_inc(sig["y_added"].sem, sig["y_added"].step())
                dve.wait_ge(sig["y_added"].sem, sig["y_added"].at(n + 1))
    core.end_region()



CONSTANTS = [("ident", P), ("diagonal", P), ("ones", P), ("mean_col", 16), ("tri", 64), ("gamma", C), ("beta", C),
             ("head_gates", H), ("ctx_t", B * KC), ("ctx_rows", B * C),
             ("flip", P), ("mask8", H), ("mask64", 2)]
FIRST = [("l0_wq", C), ("l0_wk", C), ("l0_wv", 512), ("l0_wo", 512), ("l0_bq", 1), ("l0_bk", 1)]
CONTEXT = [("wq", C), ("wk", C), ("wv", 512), ("wo", 512), ("bq", 1), ("bk", 1)]
EARLY = [("l1_wq", C), ("l1_wk", C), ("l1_wv", 512), ("l1_wo", 512), ("l1_bq", 1), ("l1_bk", 1)] + [
    (f"l1x_{m}", c) for m, c in CONTEXT] + [("l1f_b1", 32), ("l1f_b2", C), ("l1f_wg", 8), ("w_hg", 256),
                                            ("proj_w", C), ("norm_w", 7), ("ff_b1", 8)]
LATE = [(f"l3x_{m}", c) for m, c in CONTEXT] + [
    ("bit_w1", 512), ("bit_w2", 512), ("bit_b1", 512),
    ("ss_wd", C), ("ss_wb", 16), ("ss_wc", 16), ("ss_wo", C), ("ss_a", 16), ("ss_bd", 1), ("ss_bb", 1), ("ss_bc", 1),
    ("l3f_wg", 8)]
ROPE = [("swap", P), ("cos", T), ("sin", T)]
ROWS = [("l0_bv", 512), ("l1_bv", 512), ("l1_bo", C), ("l1x_bv", 512), ("l1x_bo", C), ("l1f_bg", 8), ("bo0", C),
        ("bo1", C), ("cbo0", C), ("cbo1", C), ("fb0", C), ("fb1", C), ("proj_b", C), ("bit_b2", C), ("ss_bo", C),
        ("l3x_bv", 512), ("l3x_bo", C), ("ones_row", P)]
FFN0 = [("w1", 1024), ("w2", 1024), ("w3", 1024), ("ws1", 32), ("ws2", 32), ("ws3", C), ("wr", 8)]
FFN1 = [("up", 4096), ("down", 4096)]
SELF = [("wq", 1024), ("wk", 1024), ("wv", 1024), ("wo", 1024)]
CROSS = SELF + [("fw1", 512), ("fw2", 512)]
FFN3 = [("w_in", 4096), ("w_out", 4096)]
RELS = 2 * T - 1
TOEPLITZ = T + (TB - 1) * P


def width(pack):
    return sum(c for _, c in pack)


def views(tile, pack, at=0):
    out = {}
    for name, c in pack:
        out[name] = tile[:, at:at + c]
        at += c
    return out


def decoder(nc, d):
    with ExitStack() as ctx:
        core = Core(nc, ctx)
        sig = core.sig

        def sb(name, shape, dt=F32):
            return ctx.enter_context(nc.sbuf_tensor(name, shape, dt))

        const_sb, small_sb = sb("const_sb", [P, width(CONSTANTS)]), sb("small_sb", [P, max(width(EARLY), width(LATE))])
        rows_sb = sb("rows_sb", [1, width(ROWS)])
        arena = sb("arena", [P, H * TOEPLITZ])
        arena2 = sb("arena2", [P, width(FFN1)])
        diag_bf, ident_bf = sb("diag_bf", [P, P], BF16), sb("ident_bf", [P, P], BF16)
        key_row, ones_bf = sb("key_row", [P, B * T], BF16), sb("ones_bf", [P, P], BF16)
        w = {**views(const_sb, CONSTANTS), **views(small_sb, EARLY), **views(small_sb, LATE),
             **views(arena2, FIRST, width(FFN0))}
        row = {n: v[0:1, :] for n, v in views(rows_sb, ROWS).items()}
        w["ss_bo"] = row["ss_bo"]
        core.ones_row = row["ones_row"]
        ident = w["ident"]
        load = {n: ctx.enter_context(nc.semaphore(f"load_{n}")) for n in (
            "x", "const", "small", "mask0", "mask4", "key_mask", "late", "toeplitz", "ffn0", "ffn1", "self0", "cross0", "self1", "cross1", "rope",
            "ffn3", "out")}
        parts = 4

        def fetch(eng, dst, src, name):
            n = dst.shape[-1] // parts
            for i in range(parts):
                eng.dma_start(dst[:, i * n:(i + 1) * n], src[:, i * n:(i + 1) * n]).then_inc(load[name], 16)

        LOADED = 16 * parts
        slot0, slot1, slot2 = 0, width(SELF), width(SELF) + width(CROSS)

        with ExitStack() as scope:
            key_u8 = scope.enter_context(nc.sbuf_tensor("key_u8", [1, B * T], U8))
            key_f = scope.enter_context(nc.sbuf_tensor("key_f", [1, B * T], F32))
            with nc.Block() as block:
                @block.sync
                def _(sp):
                    sp.dma_start(core.x_sb[:], d["x"]).then_inc(load["x"], 16)
                    sp.dma_start(const_sb[:], d["constants"]).then_inc(load["const"], 16)
                    sp.dma_start(rows_sb[:], d["rows"]).then_inc(load["const"], 16)
                    sp.dma_start(arena2[:, width(FFN0):width(FFN0) + width(FIRST)], d["first"]).then_inc(load["const"], 16)
                    sp.dma_start(key_u8[:], d["key_mask"]).then_inc(load["key_mask"], 16)
                    fetch(sp, arena2[:, :width(FFN0)], d["ffn0"], "ffn0")
                    sp.dma_start(small_sb[:, :width(EARLY)], d["early"]).then_inc(load["small"], 16)
                    if 3 in SUBLAYERS:
                        base = d["relative"]
                        for h in range(H):
                            src = bass.AP(base.tensor, h * RELS, [[1, P], [1, TOEPLITZ]])
                            sp.dma_start(arena[:, h * TOEPLITZ:(h + 1) * TOEPLITZ], src).then_inc(
                                load["toeplitz"], 16)

                @block.vector
                def _(dve):
                    link = core.dve_chain.link
                    nc.vector.memset(core.minus_half[:], -0.5)
                    nc.vector.memset(ones_bf[:], 1.0)
                    link(dve, nc.vector.memset(key_row[:], 0.0))
                    dve.wait_ge(load["const"], 48)
                    nc.vector.tensor_copy(diag_bf[:], w["diagonal"])
                    nc.vector.tensor_copy(ident_bf[:], ident)
                    dve.wait_ge(load["key_mask"], 16)
                    link(dve, nc.vector.tensor_copy(key_f[:], key_u8[:]))
                    link(dve, nc.vector.tensor_scalar(key_f[:], key_f[:], 0.0, None, ALU.is_equal))
                    nc.vector.tensor_scalar(key_row[0:1, :], key_f[:], NEG, None, ALU.mult)
                    dve.wait_ge(load["x"], 16)
            core.end_region()

            def context_mask(s, name, low):
                mask_sb, m01, mneg = (s.enter_context(nc.sbuf_tensor(f"{n}_{name}", [P, NT, KC], dt))
                                      for n, dt in (("mask", I32), ("m01", F32), ("mneg", F32)))
                with nc.Block() as block:
                    @block.sync
                    def _(sp):
                        sp.dma_start(mask_sb[:], d[name]).then_inc(load[name], 16)

                    @block.vector
                    def _(dve):
                        dve.wait_ge(load[name], 16)
                        core.dve_chain.link(dve, nc.vector.tensor_scalar(m01[:], mask_sb[:], 0, None, ALU.not_equal))
                        nc.vector.tensor_scalar(mneg[:], m01[:], -1.0, low, ALU.add, ALU.mult)
                core.end_region()
                return m01, mneg

            def small_self(name, top=None, gate=None, causal=None, bo=None):
                for b in range(B):
                    with ExitStack() as s:
                        def tb(n, shape):
                            return s.enter_context(nc.sbuf_tensor(f"{n}_{nc.next_id()}", shape, F32))
                        q, k, v = tb("q8", [P, T]), tb("k8", [P, T]), tb("v8", [P, TB, 512])
                        xt = core.xn_t[:, b * T:(b + 1) * T]
                        jobs = [(q[:], w[f"{name}_wq"], xt, w[f"{name}_bq"], None, False),
                                (k[:], w[f"{name}_wk"], xt, w[f"{name}_bk"], None, False)]
                        for t in range(TB):
                            jobs.append((v[:, t, :], xt[:, t * P:(t + 1) * P], w[f"{name}_wv"], None,
                                         row[f"{name}_bv"], False))
                        project(core, jobs)
                        self_attention(core, s, b, lambda h, qt: q[:, qt * P:(qt + 1) * P], lambda h: k[:],
                                       lambda h: w["mask8"][:, h:h + 1], lambda h, c: v[:, c, h * 32:(h + 1) * 32], 8,
                                       core.x_sb, ident, lambda g: w[f"{name}_wo"][:, g * C:(g + 1) * C], bo,
                                       causal=causal, top=top, gate=gate)

            if 0 in SUBLAYERS:
                normalise(core, core.x_sb, ident)
                small_self("l0", causal=(ident_bf[:], diag_bf[:]))

            if 1 in SUBLAYERS:
                normalise(core, core.x_sb, ident)
                with ExitStack() as s:
                    m01, mneg = context_mask(s, "mask0", 9.0e15)

                    def finish(dve, u, o_sb):
                        link = core.dve_chain.link
                        for g in range(TB):
                            last = nc.vector.bn_stats(core.stats[:, g, :], o_sb[:, g * C:(g + 1) * C])
                        link(dve, last)
                        for g in range(TB):
                            last = nc.vector.bn_aggr(core.mv[:, g, :], core.stats[:, g, :])
                        link(dve, last)
                        nc.vector.tensor_scalar(core.spread[:, 0:TB], core.mv[:, 0:TB, 1], 1e-5, None,
                                                ALU.add).then_inc(sig["norm_stats"].sem, sig["norm_stats"].step())
                        dve.wait_ge(sig["norm_scale"].sem, sig["norm_scale"].at(u + 1))
                        for g in range(TB):
                            last = nc.vector.tensor_scalar(o_sb[:, g * C:(g + 1) * C], o_sb[:, g * C:(g + 1) * C],
                                                           core.mv[:, g, 0:1], core.rstd[:, g:g + 1], ALU.subtract,
                                                           ALU.mult)
                        link(dve, last)
                        o3 = o_sb[:].rearrange("p (g c) -> p g c", c=C)
                        link(dve, nc.vector.tensor_tensor(o3, o3, wide(w["gamma"], TB, 1), ALU.mult))
                        link(dve, nc.vector.tensor_tensor(o3, o3, wide(w["beta"], TB, 1), ALU.add))
                        tiles = core.x_sb[:, u * TB:(u + 1) * TB, :]
                        link(dve, nc.vector.tensor_tensor(tiles, tiles, o3, ALU.add))

                    context_attention(
                        core, s, [0, 1], TB, lambda u, g: core.xn_t[:, (u * TB + g) * P:(u * TB + g + 1) * P],
                        lambda u, g: w["ctx_t"][:, u * KC:(u + 1) * KC],
                        lambda u, g: w["ctx_rows"][:KC, u * C:(u + 1) * C], C, C ** -0.5, ident,
                        mask=(lambda u, g: m01[:, u * TB + g.start:u * TB + g.stop, :],
                              lambda u, g: mneg[:, u * TB + g.start:u * TB + g.stop, :]), finish=finish)

        if 2 in SUBLAYERS:
            normalise(core, core.x_sb, ident, loads=[(load["ffn0"], LOADED)])
            with ExitStack() as s:
                f = views(arena2, FFN0)
                gates = route(core, s, f["wr"], None, 6, w["tri"])
                jobs = [(lambda c: f["ws1"], lambda c: f["ws2"], lambda c: f["ws3"][:32, :], None, ACT.Silu, 1, None)]
                for e in range(8):
                    jobs.append((lambda c, e=e: f["w1"][:, e * P:(e + 1) * P], lambda c, e=e: f["w2"][:, e * P:(e + 1) * P],
                                 lambda c, e=e: f["w3"][:, e * P:(e + 1) * P], None, ACT.Silu, 1, e))
                feed_forward(core, s, core.x_sb, jobs, gates)

        def fetch_region(what, after=()):
            with nc.Block() as block:
                @block.sync
                def _(sp):
                    for name, value in after:
                        sp.wait_ge(load[name], value)
                    for dst, src, name in what:
                        fetch(sp, dst, src, name)
            core.end_region()

        if 5 in SUBLAYERS:
            fetch_region([(arena2[:, :], d["ffn1"], "ffn1")], [("ffn0", LOADED)])

        if 3 in SUBLAYERS:
            normalise(core, core.x_sb, ident, loads=[(load["toeplitz"], 16 * H), (load["small"], 16)])
            def bias(h, qt):
                at = h * TOEPLITZ + (TB - 1 - qt) * P
                return arena[:, at:at + T]
            small_self("l1", top=(w["flip"], bias, 32), gate=w["head_gates"], bo=row["l1_bo"])

        if 7 in SUBLAYERS:
            fetch_region([(arena[:, slot0:slot0 + width(SELF)], d["self0"], "self0"),
                          (arena[:, slot1:slot1 + width(CROSS)], d["cross0"], "cross0"),
                          (arena[:, slot2:slot2 + width(SELF)], d["self1"], "self1")])

        def small_context(name, mask=None, stable=False):
            with ExitStack() as s:
                def tb(n, shape):
                    return s.enter_context(nc.sbuf_tensor(f"{n}_{nc.next_id()}", shape, F32))
                q, k, v = tb("q8", [P, B * T]), tb("k8", [P, B * KC]), tb("v8", [P, B, 512])
                keys = tb("keys8", [P, B, H, KC])
                jobs = [(k[:], w[f"{name}_wk"], w["ctx_t"], w[f"{name}_bk"], None, False)]
                for b in range(B):
                    jobs.append((v[:KC, b, :], w["ctx_t"][:, b * KC:(b + 1) * KC], w[f"{name}_wv"], None,
                                 row[f"{name}_bv"], False))
                    jobs.append((q[:, b * T:(b + 1) * T], w[f"{name}_wq"], core.xn_t[:, b * T:(b + 1) * T],
                                 w[f"{name}_bq"], None, False))
                spread_keys(core, [], [v[64:P]])
                project(core, jobs)
                spread_keys(core, [(keys[:, b], wide(k[:, b * KC:(b + 1) * KC], H, 1), wide(w["mask8"], KC, 2))
                                   for b in range(B)], [])
                paired_context_attention(
                    core, s, range(B), lambda b, p, qt: q[:, (b * TB + qt) * P:(b * TB + qt + 1) * P],
                    lambda b, p: keys[:, b, 2 * p:2 * p + 2, :].rearrange("p h k -> p (h k)"),
                    lambda b, h: v[:, b, h * 32:(h + 1) * 32], 8, core.x_sb, ident,
                    lambda g: w[f"{name}_wo"][:, g * C:(g + 1) * C], row[f"{name}_bo"], mask=mask, stable=stable)

        if 4 in SUBLAYERS:
            with ExitStack() as s:
                m01, mneg = context_mask(s, "mask4", 1.0e11)
                normalise(core, core.x_sb, ident, loads=[(load["small"], 16)])
                small_context("l1x", mask=(m01, mneg))

        if 5 in SUBLAYERS:
            normalise(core, core.x_sb, ident, loads=[(load["ffn1"], LOADED), (load["small"], 16)])
            with ExitStack() as s:
                f = views(arena2, FFN1)
                gates = route(core, s, w["l1f_wg"], row["l1f_bg"], 2, w["tri"])
                gates_t = s.enter_context(nc.sbuf_tensor("gates_t", [8, NT, P], F32))
                with nc.Block() as block:
                    @block.tensor
                    def _(pe):
                        for t in range(NT):
                            ins = nc.tensor.transpose(core.bank[t // TB][:8, (t % TB) * P:(t % TB + 1) * P],
                                                      gates[:, t, :], ident)
                        ins.then_inc(sig["turn_done"].sem, sig["turn_done"].step())
                        pe.wait_ge(sig["turn_taken"].sem, sig["turn_taken"].at(B))
                        for t in range(NT):
                            ins = nc.tensor.matmul(core.bank[2 + t // TB][:, (t % TB) * P:(t % TB + 1) * P],
                                                   gates_t[:, t, :], w["l1f_b2"][:8, :], start=True, stop=True)
                        ins.then_inc(sig["y_done"].sem, sig["y_done"].step())

                    @block.scalar
                    def _(act):
                        act.wait_ge(sig["turn_done"].sem, sig["turn_done"].at(1))
                        for b in range(B):
                            nc.scalar.activation(
                                gates_t[:, b * TB:(b + 1) * TB, :].rearrange("p t c -> p (t c)"),
                                core.bank[b][:8, :], ACT.Copy).then_inc(sig["turn_taken"].sem, sig["turn_taken"].step())

                    @block.vector
                    def _(dve):
                        dve.wait_ge(sig["y_done"].sem, sig["y_done"].at(1))
                        for b in range(B):
                            half = core.x_sb[:, b * TB:(b + 1) * TB, :].rearrange("p t c -> p (t c)")
                            nc.vector.tensor_tensor(half, half, core.bank[2 + b][:], ALU.add)
                core.end_region()
                jobs = []
                for e in list(range(0, 8, 2)) + list(range(1, 8, 2)):
                    jobs.append((lambda c, e=e: f["up"][:, (e * 4 + c) * P:(e * 4 + c + 1) * P], None,
                                 lambda c, e=e: f["down"][:, (e * 4 + c) * P:(e * 4 + c + 1) * P],
                                 lambda c, e=e: w["l1f_b1"][:, e * 4 + c:e * 4 + c + 1],
                                 ACT.Silu if e % 2 else ACT.Gelu, 4, e))
                feed_forward(core, s, core.x_sb, jobs, gates)

        if 6 in SUBLAYERS:
            normalise(core, core.x_sb, ident, loads=[(load["small"], 16)])
            with ExitStack() as s:
                gated_recurrence(core, s, w["w_hg"], ident)

        if 7 in SUBLAYERS:
            with ExitStack() as s7:
                rope_sb = s7.enter_context(nc.sbuf_tensor("rope_sb", [P, width(ROPE)], F32))
                r = views(rope_sb, ROPE)
                with nc.Block() as block:
                    @block.sync
                    def _(sp):
                        sp.dma_start(rope_sb[:], d["rope"]).then_inc(load["rope"], 16)
                core.end_region()
                normalise(core, core.x_sb, ident, keep_rows=core.y_sb,
                          loads=[(load["small"], 16), (load["rope"], 16)])
                for l in range(2):
                    ws = views(arena, SELF, slot0 if l == 0 else slot2)
                    wc = views(arena, CROSS, slot1)
                    normalise(core, core.y_sb, ident, mean_free=False, weight=w["norm_w"][:, l:l + 1],
                              loads=[(load[f"self{l}"], LOADED)])
                    for b in range(B):
                        with ExitStack() as s:
                            def tb(n, shape):
                                return s.enter_context(nc.sbuf_tensor(f"{n}_{nc.next_id()}", shape, F32))
                            q = arena2[:, 0:8 * T].rearrange("p (s t) -> p s t", s=8)
                            k = arena2[:, 8 * T:16 * T].rearrange("p (s t) -> p s t", s=8)
                            v = tb("v64", [P, TB, 1024])
                            xt = core.xn_t[:, b * T:(b + 1) * T]
                            with ExitStack() as s2:
                                bufs = [s2.enter_context(nc.sbuf_tensor(f"rope_{n}_{nc.next_id()}", [P, m, T], F32))
                                        for n, m in (("raw", 3), ("part", 3), ("swapped", 2))]
                                jobs = []
                                for c in range(8):
                                    jobs.append((q[:, c, :], ws["wq"][:, c * P:(c + 1) * P], xt, None, None, True))
                                    jobs.append((v[:, c // 2, (c % 2) * T:(c % 2 + 1) * T],
                                                 xt[:, (c // 2) * P:(c // 2 + 1) * P],
                                                 ws["wv"][:, (c % 2) * T:(c % 2 + 1) * T], None, None, False))
                                    jobs.append((k[:, c, :], ws["wk"][:, c * P:(c + 1) * P], xt, None, None, True))
                                project(core, jobs, rope=(r["swap"], r["cos"], r["sin"], *bufs))
                            self_attention(
                                core, s, b, lambda h, qt: q[:, h // 2, qt * P:(qt + 1) * P],
                                lambda h: k[:, h // 2, :], lambda h: w["mask64"][:, h % 2:h % 2 + 1],
                                lambda h, c: v[:, c, h * 64:(h + 1) * 64], 64, core.y_sb, ident,
                                lambda g: ws["wo"][:, g * C:(g + 1) * C], row[f"bo{l}"],
                                key_mask=(ones_bf[:], key_row[:, b * T:(b + 1) * T]))
                    normalise(core, core.y_sb, ident, mean_free=False, weight=w["norm_w"][:, 2 + l:3 + l],
                              loads=[(load[f"cross{l}"], LOADED)])
                    with ExitStack() as s:
                        def tb(n, shape):
                            return s.enter_context(nc.sbuf_tensor(f"{n}_{nc.next_id()}", shape, F32))
                        q = arena2[:, :8 * B * T].rearrange("p (s t) -> p s t", s=8)
                        k, v, keys = tb("k64", [P, B, 8, KC]), tb("v64", [P, B, 1024]), tb("keys64", [P, B, 8, 2, KC])
                        spread_keys(core, [], [v[64:P]])
                        with ExitStack() as s2:
                            bufs = [s2.enter_context(nc.sbuf_tensor(f"rope_{n}_{nc.next_id()}", [P, m, T], F32))
                                    for n, m in (("raw", 3), ("part", 3), ("swapped", 2))]
                            jobs = []
                            for b in range(B):
                                ct = w["ctx_t"][:, b * KC:(b + 1) * KC]
                                for c in range(8):
                                    jobs.append((k[:, b, c, :], wc["wk"][:, c * P:(c + 1) * P], ct, None, None, True))
                                    jobs.append((q[:, c, b * T:(b + 1) * T], wc["wq"][:, c * P:(c + 1) * P],
                                                 core.xn_t[:, b * T:(b + 1) * T], None, None, True))
                                    if c < 2:
                                        jobs.append((v[:KC, b, c * T:(c + 1) * T], ct, wc["wv"][:, c * T:(c + 1) * T],
                                                     None, None, False))
                            project(core, jobs, rope=(r["swap"], r["cos"], r["sin"], *bufs))
                        spread_keys(core, [(keys[:, b], wide(k[:, b], 2, 2), wide(wide(w["mask64"], 8, 1), KC, 3))
                                           for b in range(B)], [])
                        paired_context_attention(
                            core, s, range(B), lambda b, p, qt: q[:, p, (b * TB + qt) * P:(b * TB + qt + 1) * P],
                            lambda b, p: keys[:, b, p].rearrange("p h k -> p (h k)"),
                            lambda b, h: v[:, b, h * 64:(h + 1) * 64], 64, core.y_sb, ident,
                            lambda g: wc["wo"][:, g * C:(g + 1) * C], row[f"cbo{l}"])
                    normalise(core, core.y_sb, ident, mean_free=False, weight=w["norm_w"][:, 4 + l:5 + l])
                    with ExitStack() as s:
                        feed_forward(core, s, core.y_sb, [(
                            lambda c: wc["fw1"][:, c * P:(c + 1) * P], None, lambda c: wc["fw2"][:, c * P:(c + 1) * P],
                            lambda c: w["ff_b1"][:, 4 * l + c:4 * l + c + 1], ACT.Gelu, 4, None)])
                    add_rows(core, core.y_sb, row[f"fb{l}"])
                    if l == 0:
                        fetch_region([(arena[:, slot1:slot1 + width(CROSS)], d["cross1"], "cross1")])
                normalise(core, core.y_sb, ident, mean_free=False, weight=w["norm_w"][:, 6:7])
                with nc.Block() as block:
                    @block.tensor
                    def _(pe):
                        for t in range(NT):
                            out = core.bank[t // TB][:, (t % TB) * P:(t % TB + 1) * P]
                            nc.tensor.matmul(out, core.xn_t[:, t * P:(t + 1) * P], w["proj_w"], start=True, stop=False)
                            nc.tensor.matmul(out, core.ones_row[0:1, :], row["proj_b"], start=False,
                                             stop=True).then_inc(sig["y_done"].sem, sig["y_done"].step())

                    @block.vector
                    def _(dve):
                        for b in range(B):
                            dve.wait_ge(sig["y_done"].sem, sig["y_done"].at((b + 1) * TB))
                            half = core.x_sb[:, b * TB:(b + 1) * TB, :].rearrange("p t c -> p (t c)")
                            nc.vector.tensor_tensor(half, half, core.bank[b][:], ALU.add)
                core.end_region()

        if 11 in SUBLAYERS:
            fetch_region([(arena2[:, :], d["ffn3"], "ffn3")], [("ffn1" if 5 in SUBLAYERS else "ffn0", LOADED)])
        with nc.Block() as block:
            @block.sync
            def _(sp):
                sp.wait_ge(load["small"], 16)
                sp.dma_start(small_sb[:, :width(LATE)], d["late"]).then_inc(load["late"], 16)
        core.end_region()

        if 8 in SUBLAYERS:
            normalise(core, core.x_sb, ident, loads=[(load["late"], 16)])
            with ExitStack() as s:
                bit_feed_forward(core, s, w["bit_w1"], w["bit_w2"], w["bit_b1"], row["bit_b2"], ident, w["ones"])

        if 9 in SUBLAYERS:
            normalise(core, core.x_sb, ident, loads=[(load["late"], 16)])
            with ExitStack() as s:
                state_space(core, s, w)

        if 10 in SUBLAYERS:
            normalise(core, core.x_sb, ident, loads=[(load["late"], 16)])
            small_context("l3x", stable=True)

        if 11 in SUBLAYERS:
            normalise(core, core.x_sb, ident, loads=[(load["ffn3"], LOADED), (load["late"], 16)])
            with ExitStack() as s:
                gates = route(core, s, w["l3f_wg"], None, 2, w["tri"])
                f = views(arena2, FFN3)
                linear_experts(core, s, f["w_in"], f["w_out"], gates)

        with nc.Block() as block:
            @block.sync
            def _(sp):
                sp.dma_start(d["out"], core.x_sb[:]).then_inc(load["out"], 16)
                sp.wait_ge(load["out"], 16)
        core.end_region()



def pack_arrays(pack, arrays):
    out = np.zeros((P, width(pack)), np.float32)
    at = 0
    for name, c in pack:
        a = arrays[name]
        assert a.shape[1] == c, (name, a.shape, c)
        out[:a.shape[0], at:at + c] = a
        at += c
    return out


def heads_of_8(wt, bias):
    wide_w = np.zeros((C, 4, 4, 32), np.float32)
    wide_w[..., :8] = wt.reshape(C, 4, 4, 8)
    wide_b = np.zeros((4, 4, 32), np.float32)
    wide_b[..., :8] = bias.reshape(4, 4, 8)
    return wide_w.reshape(C, 512), wide_b.reshape(4, P).T


def rows_of_8(w):
    tall = np.zeros((4, 4, 32, C), np.float32)
    tall[:, :, :8] = w.reshape(4, 4, 8, C)
    return tall.reshape(4, P, C).transpose(1, 0, 2).reshape(P, 4 * C)


def chunked(a):
    n = a.shape[0] // P
    return a.reshape(n, P, -1).transpose(1, 0, 2).reshape(P, -1)


def kernel(**inputs):
    import concourse.bacc as bacc
    from concourse.bass_utils import run_bass_kernel_spmd

    v = {k: np.asarray(a) for k, a in inputs.items()}
    a = {}
    a["ident"] = np.eye(P, dtype=np.float32)
    a["diagonal"] = np.where(np.tril(np.ones((P, P), bool)), 0.0, NEG).astype(np.float32)
    a["ones"] = np.ones((P, P), np.float32)
    a["mean_col"] = np.full((P, 16), 1.0 / P, np.float32)
    a["tri"] = np.broadcast_to(np.tril(np.ones((8, 8), np.float32), -1).reshape(1, 64), (P, 64))
    a["gamma"] = np.broadcast_to(v["L0_xattn_gamma"], (P, C))
    a["beta"] = np.broadcast_to(v["L0_xattn_beta"], (P, C))
    a["head_gates"] = np.broadcast_to(v["L1_attn_head_gates"], (P, H))
    a["ctx_t"] = v["ctx_1024"].transpose(2, 0, 1).reshape(C, B * KC)
    a["ctx_rows"] = v["ctx_1024"].transpose(1, 0, 2).reshape(KC, B * C)
    a["bit_b1"] = np.broadcast_to(v["L2_ffn_b1"], (P, 512))
    w0, b0 = v["L0_attn_W"], v["L0_attn_b"]
    a["flip"] = np.eye(P, dtype=np.float32)[::-1]
    a["mask8"] = np.kron(np.eye(H), np.ones((8, 1))).astype(np.float32) * np.float32(8 ** -0.5)
    a["mask64"] = np.kron(np.eye(2), np.ones((64, 1))).astype(np.float32) * np.float32(64 ** -0.5)
    a["l0_wq"], a["l0_bq"] = w0[:C].T, b0[:C, None]
    a["l0_wk"], a["l0_bk"] = w0[C:2 * C].T, b0[C:2 * C, None]
    a["l0_wv"], bv = heads_of_8(w0[2 * C:].T, b0[2 * C:])
    a["l0_bv"] = bv.T.reshape(1, 512)
    a["l0_wo"] = rows_of_8(np.eye(C, dtype=np.float32))
    for n, src, turned in (("l1", "L1_attn", True), ("l1x", "L1_xattn", False), ("l3x", "L3_xattn", True)):
        m = {k: v[f"{src}_W{k}"].T if turned else v[f"{src}_W{k}"] for k in "qkvo"}
        a[f"{n}_wq"], a[f"{n}_wk"] = m["q"], m["k"]
        a[f"{n}_bq"], a[f"{n}_bk"] = v[f"{src}_bq"][:, None], v[f"{src}_bk"][:, None]
        a[f"{n}_wv"], bv = heads_of_8(m["v"], v[f"{src}_bv"])
        a[f"{n}_bv"], a[f"{n}_wo"], a[f"{n}_bo"] = bv.T.reshape(1, 512), rows_of_8(m["o"]), v[f"{src}_bo"][None]
    a["l1f_b1"] = v["L1_ffn_b1"].reshape(32, P).T
    a["l1f_b2"], a["l1f_wg"], a["l1f_bg"] = v["L1_ffn_b2"], v["L1_ffn_Wg"], v["L1_ffn_bg"][None]
    a["w_hg"] = v["L2_attn_W_hg"].T
    a["bit_w1"], a["bit_w2"], a["bit_b2"] = v["L2_ffn_w1"].T, chunked(v["L2_ffn_w2"].T), v["L2_ffn_b2"][None]
    a["ss_wd"], a["ss_wb"], a["ss_wc"], a["ss_wo"] = (v[f"L3_attn_W{k}"] for k in "dbco")
    a["ss_a"], a["ss_bo"] = v["L3_attn_A"], v["L3_attn_bo"][None]
    a["ss_bd"], a["ss_bb"], a["ss_bc"] = (v[f"L3_attn_b{k}"][:, None] for k in "dbc")
    x2 = "L2_xattn_"
    a["proj_w"], a["proj_b"] = v[x2 + "proj_w"], v[x2 + "proj_b"][None]
    a["norm_w"] = np.stack([v[x2 + "attn_norm_w"][0], v[x2 + "attn_norm_w"][1], v[x2 + "cross_norm_w"][0],
                            v[x2 + "cross_norm_w"][1], v[x2 + "ff_norm_w"][0], v[x2 + "ff_norm_w"][1],
                            v[x2 + "norm_out_w"]], 1)
    a["ff_b1"] = v[x2 + "ff_b1"].reshape(8, P).T
    for l in range(2):
        a[f"bo{l}"], a[f"cbo{l}"], a[f"fb{l}"] = v[x2 + "bo"][l:l + 1], v[x2 + "cbo"][l:l + 1], v[x2 + "ff_b2"][l:l + 1]
    a["l3f_wg"] = v["L3_ffn_w_gate"].T
    a["ones_row"] = np.ones((1, P), np.float32)

    inv = (1.0 / 10000.0 ** (np.arange(0, 32, 2, dtype=np.float32) / np.float32(32))).astype(np.float32)
    angle = (np.arange(T, dtype=np.float32)[:, None] * inv[None, :]).astype(np.float32)
    cos, sin, swap = np.ones((P, T), np.float32), np.zeros((P, T), np.float32), np.zeros((P, P), np.float32)
    for base in (0, 64):
        cos[base:base + 16] = cos[base + 16:base + 32] = np.cos(angle).T
        sin[base:base + 16], sin[base + 16:base + 32] = -np.sin(angle).T, np.sin(angle).T
        for i in range(16):
            swap[base + 16 + i, base + i] = swap[base + i, base + 16 + i] = 1.0

    packs = {"constants": pack_arrays(CONSTANTS, a), "early": pack_arrays(EARLY, a), "late": pack_arrays(LATE, a), "first": pack_arrays(FIRST, a),
             "rows": np.concatenate([a[n] for n, _ in ROWS], 1).astype(np.float32),
             "rope": pack_arrays(ROPE, {"swap": swap, "cos": cos, "sin": sin})}

    def experts(m):
        return m.transpose(1, 0, 2).reshape(m.shape[1], -1)

    packs["ffn0"] = pack_arrays(FFN0, {
        "w1": experts(v["L0_ffn_w1"]), "w2": experts(v["L0_ffn_w2"]), "w3": experts(v["L0_ffn_w3"]),
        "ws1": v["L0_ffn_ws1"], "ws2": v["L0_ffn_ws2"], "ws3": v["L0_ffn_ws3"], "wr": v["L0_ffn_wr"]})
    packs["ffn1"] = pack_arrays(FFN1, {"up": experts(v["L1_ffn_W1"]),
                                       "down": chunked(v["L1_ffn_W2"].reshape(8 * 512, C))})
    packs["ffn3"] = pack_arrays(FFN3, {"w_in": chunked(v["L3_ffn_w_in"].reshape(8 * 512, C)),
                                       "w_out": chunked(v["L3_ffn_w_out"].transpose(0, 2, 1).reshape(8 * 512, C))})
    for l in range(2):
        packs[f"self{l}"] = pack_arrays(SELF, {
            "wq": v[x2 + "Wq"][l], "wk": v[x2 + "Wk"][l], "wv": v[x2 + "Wv"][l], "wo": chunked(v[x2 + "Wo"][l])})
        packs[f"cross{l}"] = pack_arrays(CROSS, {
            "wq": v[x2 + "cWq"][l], "wk": v[x2 + "cWk"][l], "wv": v[x2 + "cWv"][l], "wo": chunked(v[x2 + "cWo"][l]),
            "fw1": v[x2 + "ff_w1"][l], "fw2": chunked(v[x2 + "ff_w2"][l])})

    table = v["L1_attn_rel_bias"]
    at = np.arange(-(T - 1), T) + 63
    at = np.clip(np.where(at < 0, at + table.shape[0], at), 0, table.shape[0] - 1)
    packs["relative"] = np.ascontiguousarray(table[at].T)

    def tokens(m):
        return np.ascontiguousarray(m.reshape(NT, P, -1).transpose(1, 0, 2))

    packs["x"] = tokens(v["x"])
    packs["mask0"] = tokens(v["mask_BxSxS2_ik1"].reshape(B * T, KC))
    packs["mask4"] = tokens(v["mask_Bx1xSxS2_ik1"].reshape(B * T, KC))
    packs["key_mask"] = np.ascontiguousarray(v["mask_BxS_bf1"]).view(np.uint8).reshape(1, B * T)

    nc = bacc.Bacc("TRN2", target_bir_lowering=False, num_devices=1)
    d = {n: nc.dram_tensor(f"in_{n}", m.shape, mybir.dt.from_np(m.dtype), kind="ExternalInput").ap()
         for n, m in packs.items()}
    d["out"] = nc.dram_tensor("out_x", (P, NT, C), F32, kind="ExternalOutput").ap()
    decoder(nc, d)
    r = run_bass_kernel_spmd(nc, [{f"in_{n}": m for n, m in packs.items()}], core_ids=[0])
    got = r.results[0]["out_x"]
    return np.ascontiguousarray(got.transpose(1, 0, 2)).reshape(B, T, C)
```

```python
from contextlib import ExitStack

import numpy as np
import concourse.bass as bass
from concourse import mybir

F32 = mybir.dt.float32
BF16 = mybir.dt.bfloat16
I32 = mybir.dt.int32
U8 = mybir.dt.uint8
ALU = mybir.AluOpType
ACT = mybir.ActivationFunctionType
AXX = mybir.AxisListType.X

P = 128
B, T, C = 2, 512, 128
NT = B * T // P
TB = T // P
KC = 77
H = 16
BANK = 512
NEG = -1.0e30
ROUND = 12582912.0
SUBLAYERS = (0, 1, 2, 3, 4, 5, 6, 7, 8, 9, 10, 11)


class Signal:

    def __init__(self, nc, ctx, name):
        self.sem = ctx.enter_context(nc.semaphore(name))
        self.base = 0
        self.count = 0

    def step(self):
        self.count += 1
        return 1

    def at(self, n):
        return self.base + n

    def next_region(self):
        self.base = self.count


class Chain:

    def __init__(self, nc, ctx, name):
        self.sem = ctx.enter_context(nc.semaphore(name))
        self.count = 0

    def link(self, eng, ins):
        self.count += 1
        ins.then_inc(self.sem, 1)
        eng.wait_ge(self.sem, self.count)

    def mark(self, ins):
        self.count += 1
        ins.then_inc(self.sem, 1)
        return self.count


def wide(ap, n, axis):
    return ap.unsqueeze(axis).broadcast_to(list(ap.shape[:axis]) + [n] + list(ap.shape[axis:]))


class Core:

    SIGNALS = ("norm_stats", "norm_scale", "norm_rows", "norm_turned", "mm_done", "raw_ready", "swap_done",
               "cos_done", "rope_done", "s_done", "s_taken", "max_done", "exp_done", "turn_done", "turn_taken",
               "pv_done", "o_done", "out_done", "out_added", "act_done", "prod_done", "y_done", "y_added",
               "aux_pe", "aux_dve", "aux_act", "aux_pool")

    def __init__(self, nc, ctx):
        self.nc = nc
        self.dve_chain = Chain(nc, ctx, "dve_chain")
        self.pool_chain = Chain(nc, ctx, "pool_chain")
        self.sig = {n: Signal(nc, ctx, n) for n in self.SIGNALS}
        self.bank = [ctx.enter_context(nc.psum_tensor(f"bank{i}", [P, BANK], F32)) for i in range(8)]

        def sb(name, shape, dt=F32):
            return ctx.enter_context(nc.sbuf_tensor(name, shape, dt))

        self.x_sb = sb("x_sb", [P, NT, C])
        self.y_sb = sb("y_sb", [P, NT, C])
        self.xn = sb("xn", [P, NT, C])
        self.xn_t = sb("xn_t", [P, B * T])
        self.stats = sb("stats", [P, NT, 6])
        self.mv = sb("mv", [P, NT, 2])
        self.spread = sb("spread", [P, NT])
        self.rstd = sb("rstd", [P, NT])
        self.minus_half = sb("minus_half", [P, NT])

    def end_region(self):
        for s in self.sig.values():
            s.next_region()



def normalise(core, src, ident, mean_free=True, weight=None, keep_rows=None, loads=()):
    nc, sig = core.nc, core.sig
    with nc.Block() as block:
        @block.vector
        def _(dve):
            link = core.dve_chain.link
            for s, v in loads:
                dve.wait_ge(s, v)
            for t in range(NT):
                last = nc.vector.bn_stats(core.stats[:, t, :], src[:, t, :])
            link(dve, last)
            for t in range(NT):
                last = nc.vector.bn_aggr(core.mv[:, t, :], core.stats[:, t, :])
            link(dve, last)
            mean, var = core.mv[:, :, 0], core.mv[:, :, 1]
            if mean_free:
                nc.vector.tensor_scalar(core.spread[:], var, 1e-5, None, ALU.add).then_inc(
                    sig["norm_stats"].sem, sig["norm_stats"].step())
            else:
                link(dve, nc.vector.tensor_tensor(core.spread[:], mean, mean, ALU.mult))
                link(dve, nc.vector.tensor_tensor(core.spread[:], core.spread[:], var, ALU.add))
                nc.vector.tensor_scalar(core.spread[:], core.spread[:], 1e-16, None, ALU.max).then_inc(
                    sig["norm_stats"].sem, sig["norm_stats"].step())
            dve.wait_ge(sig["norm_scale"].sem, sig["norm_scale"].at(1))
            for t in range(NT):
                if mean_free:
                    ins = nc.vector.tensor_scalar(core.xn[:, t, :], src[:, t, :], core.mv[:, t, 0:1],
                                                  core.rstd[:, t:t + 1], ALU.subtract, ALU.mult)
                else:
                    ins = nc.vector.tensor_scalar(core.xn[:, t, :], src[:, t, :], core.rstd[:, t:t + 1],
                                                  None, ALU.mult)
                ins.then_inc(sig["norm_rows"].sem, sig["norm_rows"].step())
            if keep_rows is not None:
                dve.wait_ge(sig["norm_rows"].sem, sig["norm_rows"].at(NT))
                nc.vector.tensor_copy(keep_rows[:], core.xn[:])

        @block.gpsimd
        def _(pool):
            pool.wait_ge(sig["norm_stats"].sem, sig["norm_stats"].at(1))
            nc.gpsimd.tensor_tensor(core.rstd[:], core.spread[:], core.minus_half[:], ALU.pow).then_inc(
                sig["norm_scale"].sem, sig["norm_scale"].step())

        @block.tensor
        def _(pe):
            for t in range(NT):
                pe.wait_ge(sig["norm_rows"].sem, sig["norm_rows"].at(t + 1))
                ins = nc.tensor.transpose(core.bank[t // TB][:, (t % TB) * P:(t % TB + 1) * P],
                                          core.xn[:, t, :], ident)
                if t % TB == TB - 1:
                    ins.then_inc(sig["norm_turned"].sem, sig["norm_turned"].step())

        @block.scalar
        def _(act):
            for b in range(B):
                act.wait_ge(sig["norm_turned"].sem, sig["norm_turned"].at(b + 1))
                nc.scalar.activation(core.xn_t[:, b * T:(b + 1) * T], core.bank[b][:], ACT.Copy if weight is None
                                     else ACT.Identity, scale=1.0 if weight is None else weight)
    core.end_region()



def project(core, jobs, rope=None):
    nc, sig = core.nc, core.sig
    NB = 4
    turned = [i for i, j in enumerate(jobs) if j[5]]
    by_act = [i for i, j in enumerate(jobs) if j[5] or i % 2 == 0]
    by_dve = [i for i in range(len(jobs)) if i not in by_act]

    def wait_taken(eng, i):
        if i in by_act:
            eng.wait_ge(sig["act_done"].sem, sig["act_done"].at(by_act.index(i) + 1))
        else:
            eng.wait_ge(sig["prod_done"].sem, sig["prod_done"].at(by_dve.index(i) + 1))

    with nc.Block() as block:
        @block.tensor
        def _(pe):
            def swap(n):
                i = turned[n]
                pe.wait_ge(sig["act_done"].sem, sig["act_done"].at(by_act.index(i) + 1))
                if n >= 2:
                    pe.wait_ge(sig["swap_done"].sem, sig["swap_done"].at(n - 1))
                nd = jobs[i][0].shape[-1]
                nc.tensor.matmul(core.bank[NB + n % 2][:, :nd], rope[0], rope[3][:, n % 3, :nd],
                                 start=True, stop=True).then_inc(sig["raw_ready"].sem, sig["raw_ready"].step())

            swapped = 0
            for i, (dst, lhs, rhs, col, row, turn) in enumerate(jobs):
                if i >= NB:
                    wait_taken(pe, i - NB)
                m, n = lhs.shape[-1], rhs.shape[-1]
                out = core.bank[i % NB][:m, :n]
                ins = nc.tensor.matmul(out, lhs, rhs, start=True, stop=row is None)
                if row is not None:
                    ins = nc.tensor.matmul(out, core.ones_row[0:1, :m], row, start=False, stop=True)
                ins.then_inc(sig["mm_done"].sem, sig["mm_done"].step())
                while swapped < len(turned) and turned[swapped] <= i - 2:
                    swap(swapped)
                    swapped += 1
            while swapped < len(turned):
                swap(swapped)
                swapped += 1

        @block.scalar
        def _(act):
            for i in by_act:
                dst, lhs, rhs, col, row, turn = jobs[i]
                act.wait_ge(sig["mm_done"].sem, sig["mm_done"].at(i + 1))
                if turn:
                    n = turned.index(i)
                    if n >= 3:
                        act.wait_ge(sig["raw_ready"].sem, sig["raw_ready"].at(n - 2))
                        act.wait_ge(sig["cos_done"].sem, sig["cos_done"].at(n - 2))
                    dst = rope[3][:, n % 3, :dst.shape[-1]]
                src = core.bank[i % NB][:lhs.shape[-1], :rhs.shape[-1]]
                nc.scalar.activation(dst, src, ACT.Identity, bias=0.0 if col is None else col).then_inc(
                    sig["act_done"].sem, sig["act_done"].step())

        @block.gpsimd
        def _(pool):
            for n, i in enumerate(turned):
                nd = jobs[i][0].shape[-1]
                pool.wait_ge(sig["act_done"].sem, sig["act_done"].at(by_act.index(i) + 1))
                if n >= 3:
                    pool.wait_ge(sig["rope_done"].sem, sig["rope_done"].at(n - 2))
                nc.gpsimd.tensor_tensor(rope[4][:, n % 3, :nd], rope[3][:, n % 3, :nd], rope[1][:, :nd],
                                        ALU.mult).then_inc(sig["cos_done"].sem, sig["cos_done"].step())

        @block.vector
        def _(dve):
            def turn_one(n):
                dst = jobs[turned[n]][0]
                nd = dst.shape[-1]
                dve.wait_ge(sig["raw_ready"].sem, sig["raw_ready"].at(n + 1))
                if n >= 2:
                    dve.wait_ge(sig["rope_done"].sem, sig["rope_done"].at(n - 1))
                nc.vector.tensor_tensor(rope[5][:, n % 2, :nd], core.bank[NB + n % 2][:, :nd], rope[2][:, :nd],
                                        ALU.mult).then_inc(sig["swap_done"].sem, sig["swap_done"].step())
                dve.wait_ge(sig["swap_done"].sem, sig["swap_done"].at(n + 1))
                dve.wait_ge(sig["cos_done"].sem, sig["cos_done"].at(n + 1))
                nc.vector.tensor_tensor(dst, rope[4][:, n % 3, :nd], rope[5][:, n % 2, :nd], ALU.add).then_inc(
                    sig["rope_done"].sem, sig["rope_done"].step())

            for i in range(len(jobs)):
                if i in by_dve:
                    dst, lhs, rhs, col, row, _ = jobs[i]
                    dve.wait_ge(sig["mm_done"].sem, sig["mm_done"].at(i + 1))
                    src = core.bank[i % NB][:lhs.shape[-1], :rhs.shape[-1]]
                    if col is None:
                        ins = nc.vector.tensor_copy(dst, src)
                    else:
                        ins = nc.vector.tensor_scalar(dst, src, col, None, ALU.add)
                    ins.then_inc(sig["prod_done"].sem, sig["prod_done"].step())
                if i in turned:
                    turn_one(turned.index(i))
    core.end_region()



def self_attention(core, ctx, b, q_of, k_pair, head_mask, v_of, hd, dst, ident, wo, bo, causal=None, key_mask=None,
                   top=None, gate=None):
    nc, sig = core.nc, core.sig
    units = [(h, qt) for h in range(H) for qt in range(TB)]
    U = len(units)
    NS, NT2, NE, NTS = 4, 2, 6, 3
    LAG = 5 if top else 4
    pairs = H // 2
    per_group = 1 if hd == 64 else 2
    col = 64 if hd == 64 else 32
    groups = pairs // per_group

    def sb(name, shape, dt=F32):
        return ctx.enter_context(nc.sbuf_tensor(f"{name}_{nc.next_id()}", shape, dt))

    k_one = key_mask[3] if key_mask else sb("k_one", [P, 2, T])
    q_one = key_mask[4] if key_mask else None
    e_sb = sb("e_sb", [P, NE, T])
    e_t = sb("e_t", [P, NTS, TB, T])
    o_t = sb("o_t", [P, T])
    work = sb("work", [P, 2, T]) if top else None
    s_sb = sb("s_sb", [P, 4, T]) if top else None
    best = sb("best", [P, 4, 32]) if top else None
    nmax, den, rden = sb("nmax", [P, U]), sb("den", [P, U]), sb("rden", [P, U])
    s_bank, t_bank, o_bank, y_bank = core.bank[0:4], core.bank[4:6], core.bank[6], core.bank[7]

    def chunks(qt):
        return qt + 1 if causal else TB

    def value_step(p):
        return 8 * p + 7 + LAG + 2

    def group_step(g):
        return value_step((g + 1) * per_group - 1) + (2 if top else 5)

    steps = group_step(groups - 1) + 3
    if top:
        value_at = {value_step(p): (p, range(TB)) for p in range(pairs)}
    else:
        value_at = {value_step(p) + k: (p, (k,)) for p in range(pairs) for k in range(TB)}
    group_at = {group_step(g): g for g in range(groups)}

    with nc.Block() as block:
        @block.tensor
        def _(pe):
            def scores(u):
                h, qt = units[u]
                n = chunks(qt) * P
                if qt == 0:
                    pe.wait_ge(sig["aux_pool"].sem, sig["aux_pool"].at(h + 1))
                if u == 0 and key_mask:
                    pe.wait_ge(sig["aux_act"].sem, sig["aux_act"].at(1))
                if u >= NS:
                    freed = sig["s_taken" if top else "exp_done"]
                    pe.wait_ge(freed.sem, freed.at(u - NS + 1))
                out = s_bank[u % NS][:, :n]
                query = q_one[:, h % 2, qt * P:(qt + 1) * P] if key_mask else q_of(h, qt)
                ins = nc.tensor.matmul(out, query, k_one[:, h % 2, :n], start=True, stop=not (causal or top))
                if causal:
                    ins = nc.tensor.matmul(out[:, n - P:n], causal[0], causal[1], start=False, stop=True)
                if top:
                    ins = nc.tensor.matmul(out, top[0], top[1](h, qt), start=False, stop=True)
                ins.then_inc(sig["s_done"].sem, sig["s_done"].step())

            def turn(u):
                h, qt = units[u]
                pe.wait_ge(sig["norm_rows"].sem, sig["norm_rows"].at(u + 1))
                if u >= NT2:
                    pe.wait_ge(sig["turn_taken"].sem, sig["turn_taken"].at(u - NT2 + 1))
                for k in range(chunks(qt)):
                    ins = nc.tensor.transpose(t_bank[u % NT2][:, k * P:(k + 1) * P],
                                              e_sb[:, u % NE, k * P:(k + 1) * P], ident)
                ins.then_inc(sig["turn_done"].sem, sig["turn_done"].step())

            def values(p, tiles):
                g, part = p // per_group, p % per_group
                if tiles[0] == 0:
                    pe.wait_ge(sig["turn_taken"].sem, sig["turn_taken"].at(8 * (p + 1)))
                if tiles[0] == 0 and part == 0 and g >= 1:
                    pe.wait_ge(sig["o_done"].sem, sig["o_done"].at(g))
                for k in tiles:
                    at = k * P if causal else 0
                    for h in (2 * p, 2 * p + 1):
                        row = (h * col) % P
                        ins = nc.tensor.matmul(o_bank[row:row + col, at:], v_of(h, k), e_t[:, h % NTS, k, at:],
                                               start=k == 0, stop=k == TB - 1)
                if tiles[-1] == TB - 1:
                    ins.then_inc(sig["pv_done"].sem, sig["pv_done"].step())

            def out(g):
                pe.wait_ge(sig["o_done"].sem, sig["o_done"].at(g + 1))
                if g >= 1:
                    pe.wait_ge(sig["out_added"].sem, sig["out_added"].at(g))
                last = g == groups - 1 and bo is not None
                for qt in range(TB):
                    y = y_bank[:, qt * C:(qt + 1) * C]
                    ins = nc.tensor.matmul(y, o_t[:, qt * P:(qt + 1) * P], wo(g), start=True, stop=not last)
                    if last:
                        ins = nc.tensor.matmul(y, core.ones_row[0:1, :], bo, start=False, stop=True)
                ins.then_inc(sig["out_done"].sem, sig["out_done"].step())

            for i in range(steps):
                if i < U:
                    scores(i)
                if LAG <= i < U + LAG:
                    turn(i - LAG)
                if i in value_at:
                    values(*value_at[i])
                if i in group_at:
                    out(group_at[i])

        @block.gpsimd
        def _(pool):
            link = core.pool_chain.link
            for h in range(H):
                if h >= 2:
                    pool.wait_ge(sig["s_done"].sem, sig["s_done"].at(TB * (h - 1)))
                if key_mask:
                    own = slice(64 * (h % 2), 64 * (h % 2) + 64)
                    if h >= 1:
                        link(pool, nc.gpsimd.tensor_copy(q_one[own, h % 2, :], key_mask[0](h)[own, :]))
                    nc.gpsimd.tensor_scalar(k_one[own, h % 2, :], k_pair(h)[own, :], key_mask[2], None,
                                            ALU.mult).then_inc(sig["aux_pool"].sem, sig["aux_pool"].step())
                    pool.wait_ge(sig["aux_pool"].sem, sig["aux_pool"].at(h + 1))
                    continue
                nc.gpsimd.tensor_tensor(k_one[:, h % 2, :], k_pair(h), head_mask(h).broadcast_to([P, T]),
                                        ALU.mult).then_inc(sig["aux_pool"].sem, sig["aux_pool"].step())

        @block.vector
        def _(dve):
            link = core.dve_chain.link

            def maxima(u):
                h, qt = units[u]
                bank = s_bank[u % NS]
                dve.wait_ge(sig["s_done"].sem, sig["s_done"].at(u + 1))
                nc.vector.tensor_reduce(nmax[:, u:u + 1], bank[:, :chunks(qt) * P], AXX, ALU.max,
                                        negate=True).then_inc(sig["max_done"].sem, sig["max_done"].step())

            def largest(pair, before):
                chain, mark, found = core.dve_chain, core.dve_chain.mark, {}
                dve.wait_ge(sig["s_taken"].sem, sig["s_taken"].at(pair[-1] + 1))
                for u in pair:
                    found[u] = mark(nc.vector.max(best[:, u % 4, 0:8], s_sb[:, u % 4, :]))
                turned = reciprocals(before)
                dve.wait_ge(chain.sem, found[pair[-1]])
                nc.vector.tensor_scalar(nmax[:, pair[0]:pair[0] + 2], best[:, pair[0] % 4:pair[0] % 4 + 2, 0], -1.0,
                                        None, ALU.mult).then_inc(sig["max_done"].sem, sig["max_done"].step())
                gated(turned)
                for r in range(1, top[2] // 8):
                    for u in pair:
                        dve.wait_ge(chain.sem, found[u])
                        found[u] = mark(nc.vector.match_replace(
                            work[:, u % 2, :], best[:, u % 4, 8 * (r - 1):8 * r],
                            s_sb[:, u % 4, :] if r == 1 else work[:, u % 2, :], -3.0e38))
                    for u in pair:
                        dve.wait_ge(chain.sem, found[u])
                        found[u] = mark(nc.vector.max(best[:, u % 4, 8 * r:8 * r + 8], work[:, u % 2, :]))
                return found

            def keep(pair, found):
                for u in pair:
                    dve.wait_ge(sig["exp_done"].sem, sig["exp_done"].at(u + 1))
                    dve.wait_ge(core.dve_chain.sem, found[u])
                    e = e_sb[:, u % NE, :]
                    nc.vector.scalar_tensor_tensor(
                        out=e, in0=s_sb[:, u % 4, :], scalar=best[:, u % 4, top[2] - 1:top[2]], in1=e, op0=ALU.is_ge,
                        op1=ALU.mult, accum_out=den[:, u:u + 1]).then_inc(sig["prod_done"].sem, sig["prod_done"].step())

            def reciprocals(which):
                if not which:
                    return None
                own = sig["prod_done" if top else "exp_done"]
                dve.wait_ge(own.sem, own.at(which[-1] + 1))
                r = rden[:, which[0]:which[-1] + 1]
                ins = nc.vector.reciprocal(r, den[:, which[0]:which[-1] + 1])
                if gate is None:
                    ins.then_inc(sig["aux_dve"].sem, sig["aux_dve"].step())
                    return None
                return r, units[which[0]][0], core.dve_chain.mark(ins)

            def gated(turned):
                if turned:
                    r, h, at = turned
                    dve.wait_ge(core.dve_chain.sem, at)
                    nc.vector.tensor_scalar(r, r, gate[:, h:h + 1], None, ALU.mult).then_inc(
                        sig["aux_dve"].sem, sig["aux_dve"].step())

            def divide(u):
                h, qt = units[u]
                e = e_sb[:, u % NE, :chunks(qt) * P]
                dve.wait_ge(sig["aux_dve"].sem, sig["aux_dve"].at(u + 1))
                nc.vector.tensor_scalar(e, e, rden[:, u:u + 1], None, ALU.mult).then_inc(
                    sig["norm_rows"].sem, sig["norm_rows"].step())

            def add(g):
                dve.wait_ge(sig["out_done"].sem, sig["out_done"].at(g + 1))
                if g >= 1:
                    dve.wait_ge(sig["out_added"].sem, sig["out_added"].at(g))
                half = dst[:, b * TB:(b + 1) * TB, :].rearrange("p t c -> p (t c)")
                nc.vector.tensor_tensor(half, half, y_bank[:], ALU.add).then_inc(
                    sig["out_added"].sem, sig["out_added"].step())

            for i in range(0, steps, 2) if top else ():
                if i < U:
                    pair = (i, i + 1)
                    keep(pair, largest(pair, (i - 2, i - 1) if i else ()))
                if i == U:
                    gated(reciprocals((U - 2, U - 1)))
                if i - 2 in group_at:
                    add(group_at[i - 2])
            for i in () if top else range(steps):
                if i < U:
                    maxima(i)
                if 1 <= i < U + 1:
                    gated(reciprocals((i - 1,)))
                    divide(i - 1)
                if i - 1 in group_at:
                    add(group_at[i - 1])

        @block.scalar
        def _(act):
            def exps(u):
                h, qt = units[u]
                n = chunks(qt) * P
                act.wait_ge(sig["max_done"].sem, sig["max_done"].at(u // 2 + 1 if top else u + 1))
                if u >= NE:
                    act.wait_ge(sig["turn_done"].sem, sig["turn_done"].at(u - NE + 1))
                e, s = e_sb[:, u % NE, :n], s_bank[u % NS][:, :n]
                if top:
                    ins = nc.scalar.activation(e, s_sb[:, u % 4, :], ACT.Exp, bias=nmax[:, u:u + 1])
                else:
                    ins = nc.scalar.activation(e, s, ACT.Exp, bias=nmax[:, u:u + 1], accum_out=den[:, u:u + 1])
                ins.then_inc(sig["exp_done"].sem, sig["exp_done"].step())

            def take_scores(u):
                act.wait_ge(sig["s_done"].sem, sig["s_done"].at(u + 1))
                if u >= 4:
                    act.wait_ge(sig["prod_done"].sem, sig["prod_done"].at(u - 3))
                nc.scalar.activation(s_sb[:, u % 4, :], s_bank[u % NS][:], ACT.Copy).then_inc(
                    sig["s_taken"].sem, sig["s_taken"].step())

            def divide(u):
                act.wait_ge(sig["aux_dve"].sem, sig["aux_dve"].at(u // 2 + 1))
                e = e_sb[:, u % NE, :]
                nc.scalar.activation(e, e, ACT.Copy, scale=rden[:, u:u + 1]).then_inc(
                    sig["norm_rows"].sem, sig["norm_rows"].step())

            def copy(u):
                h, qt = units[u]
                n = chunks(qt)
                act.wait_ge(sig["turn_done"].sem, sig["turn_done"].at(u + 1))
                if h >= NTS:
                    act.wait_ge(sig["pv_done"].sem, sig["pv_done"].at((h - NTS) // 2 + 1))
                nc.scalar.activation(e_t[:, h % NTS, 0:n, qt * P:(qt + 1) * P],
                                     t_bank[u % NT2][:, :n * P].rearrange("p (k q) -> p k q", q=P), ACT.Copy).then_inc(
                    sig["turn_taken"].sem, sig["turn_taken"].step())

            def take(g):
                act.wait_ge(sig["pv_done"].sem, sig["pv_done"].at((g + 1) * per_group))
                if g >= 1:
                    act.wait_ge(sig["out_done"].sem, sig["out_done"].at(g))
                nc.scalar.activation(o_t[:], o_bank[:], ACT.Copy).then_inc(
                    sig["o_done"].sem, sig["o_done"].step())

            if key_mask:
                for slot in range(2):
                    first = slice(P - 64 - 64 * slot, P - 64 * slot - 63)
                    nc.scalar.activation(k_one[first, slot, :], key_mask[1][first, :], ACT.Copy)
                nc.scalar.activation(q_one[:64, 0, :], key_mask[0](0)[:64, :], ACT.Copy).then_inc(
                    sig["aux_act"].sem, sig["aux_act"].step())
            if top:
                take_scores(0)
                take_scores(1)
            for i in range(0, steps, 2) if top else ():
                for u in (i - 2, i - 1):
                    if 0 <= u < U:
                        divide(u)
                for u in (i, i + 1):
                    if u < U:
                        exps(u)
                for u in (i - 4, i - 3):
                    if 0 <= u < U:
                        copy(u)
                if i + 2 in group_at:
                    take(group_at[i + 2])
                for u in (i + 2, i + 3):
                    if u < U:
                        take_scores(u)
            for i in () if top else range(steps):
                if LAG <= i < U + LAG:
                    copy(i - LAG)
                if i < U:
                    exps(i)
                if i + 1 in group_at:
                    take(group_at[i + 1])
    core.end_region()



def single_heads(core, ctx):
    nc = core.nc
    k_one, q_one = (ctx.enter_context(nc.sbuf_tensor(n, [P, 2, T], F32)) for n in ("k_single", "q_single"))
    with nc.Block() as block:
        @block.gpsimd
        def _(pool):
            link = core.pool_chain.link
            for slot in range(2):
                other = slice(P - 64 - 64 * slot, P - 64 * slot)
                link(pool, nc.gpsimd.memset(k_one[other, slot, :], 0.0))
                link(pool, nc.gpsimd.memset(q_one[other, slot, :], 0.0))
                link(pool, nc.gpsimd.memset(q_one[other.start:other.start + 1, slot, :], 1.0))
    core.end_region()
    return k_one, q_one


def context_attention(core, ctx, units, G, q_of, k_of, v_of, scale, ident, mask, finish):
    nc, sig = core.nc, core.sig

    def sb(name, shape, dt=F32):
        return ctx.enter_context(nc.sbuf_tensor(f"{name}_{nc.next_id()}", shape, dt))

    s_bank = core.bank[0]
    t_bank = (core.bank[4], core.bank[7])
    o_bank = core.bank[5]
    e_sb = sb("ce_sb", [P, G, KC])
    s_sb = sb("cs_sb", [P, G, KC])
    e_t = sb("ce_t", [P, G, P])
    mx = sb("cmx", [P, G])
    den = sb("cden", [P, G])
    rden = sb("crden", [P, G])
    o_sb = sb("co_sb", [P, G * C])
    NQ = G // 4
    NU = len(units)

    with nc.Block() as block:
        @block.tensor
        def _(pe):
            def scores(u):
                if u >= 1:
                    pe.wait_ge(sig["s_taken"].sem, sig["s_taken"].at(u))
                for g in range(G):
                    ins = nc.tensor.matmul(s_bank[:, g * KC:(g + 1) * KC],
                                           q_of(units[u], g), k_of(units[u], g), start=True, stop=True)
                ins.then_inc(sig["s_done"].sem, sig["s_done"].step())

            def turns(u):
                pe.wait_ge(sig["exp_done"].sem, sig["exp_done"].at(u + 1))
                for j in range(NQ):
                    n = NQ * u + j
                    if n >= 2:
                        pe.wait_ge(sig["turn_taken"].sem, sig["turn_taken"].at(n - 1))
                    for g in range(4 * j, 4 * j + 4):
                        ins = nc.tensor.transpose(t_bank[n % 2][:KC, (g % 4) * P:(g % 4 + 1) * P],
                                                  e_sb[:, g, :], ident)
                    ins.then_inc(sig["turn_done"].sem, sig["turn_done"].step())

            def values(u):
                if u >= 1:
                    pe.wait_ge(sig["o_done"].sem, sig["o_done"].at(u))
                pe.wait_ge(sig["turn_taken"].sem, sig["turn_taken"].at(NQ * (u + 1)))
                for g in range(G):
                    ins = nc.tensor.matmul(o_bank[:, g * C:(g + 1) * C], e_t[:KC, g, :],
                                           v_of(units[u], g), start=True, stop=True)
                ins.then_inc(sig["pv_done"].sem, sig["pv_done"].step())

            scores(0)
            for u in range(NU):
                if u + 1 < NU:
                    scores(u + 1)
                turns(u)
                values(u)

        @block.vector
        def _(dve):
            link = core.dve_chain.link

            def front(u):
                dve.wait_ge(sig["s_done"].sem, sig["s_done"].at(u + 1))
                scores = s_bank[:, :G * KC].rearrange("p (g k) -> p g k", k=KC)
                ins = nc.vector.scalar_tensor_tensor(out=s_sb[:], in0=scores, scalar=scale,
                                                     in1=mask[0](units[u], slice(0, G)), op0=ALU.mult, op1=ALU.mult)
                ins.then_inc(sig["s_taken"].sem, sig["s_taken"].step())
                dve.wait_ge(sig["s_taken"].sem, sig["s_taken"].at(u + 1))
                link(dve, nc.vector.tensor_tensor(s_sb[:], s_sb[:], mask[1](units[u], slice(0, G)), ALU.add))
                link(dve, nc.vector.tensor_reduce(mx[:], s_sb[:], AXX, ALU.max))
                nc.vector.tensor_tensor(s_sb[:], s_sb[:], wide(mx[:], KC, 2), ALU.subtract).then_inc(
                    sig["max_done"].sem, sig["max_done"].step())

            def back(u):
                dve.wait_ge(sig["exp_done"].sem, sig["exp_done"].at(u + 1))
                link(dve, nc.vector.tensor_reduce(den[:], e_sb[:], AXX, ALU.add))
                link(dve, nc.vector.reciprocal(rden[:], den[:]))
                dve.wait_ge(sig["pv_done"].sem, sig["pv_done"].at(u + 1))
                nc.vector.tensor_tensor(
                    o_sb[:].rearrange("p (g d) -> p g d", d=C), o_bank[:].rearrange("p (g d) -> p g d", d=C),
                    wide(rden[:], C, 2), ALU.mult).then_inc(sig["o_done"].sem, sig["o_done"].step())
                dve.wait_ge(sig["o_done"].sem, sig["o_done"].at(u + 1))
                finish(dve, u, o_sb)

            for u in range(NU):
                front(u)
                back(u)

        @block.scalar
        def _(act):
            for u in range(NU):
                act.wait_ge(sig["max_done"].sem, sig["max_done"].at(u + 1))
                if u >= 1:
                    act.wait_ge(sig["turn_done"].sem, sig["turn_done"].at(NQ * u))
                nc.scalar.activation(e_sb[:], s_sb[:], ACT.Exp).then_inc(
                    sig["exp_done"].sem, sig["exp_done"].step())
                for j in range(NQ):
                    n = NQ * u + j
                    act.wait_ge(sig["turn_done"].sem, sig["turn_done"].at(n + 1))
                    if u >= 1:
                        act.wait_ge(sig["pv_done"].sem, sig["pv_done"].at(u))
                    nc.scalar.activation(e_t[:KC, 4 * j:4 * j + 4, :],
                                         t_bank[n % 2][:KC, :].rearrange("p (g q) -> p g q", q=P),
                                         ACT.Copy).then_inc(sig["turn_taken"].sem, sig["turn_taken"].step())

        @block.gpsimd
        def _(pool):
            for u in range(NU):
                pool.wait_ge(sig["norm_stats"].sem, sig["norm_stats"].at(u + 1))
                nc.gpsimd.tensor_tensor(core.rstd[:, 0:G], core.spread[:, 0:G], core.minus_half[:, 0:G],
                                        ALU.pow).then_inc(sig["norm_scale"].sem, sig["norm_scale"].step())
    core.end_region()


def paired_context_attention(core, ctx, batches, q_of, k_pair, v_of, hd, dst, ident, wo, bo, mask=None,
                             stable=False):
    nc, sig = core.nc, core.sig
    units = [(b, p) for b in batches for p in range(H // 2)]
    U = len(units)
    per_group = 1 if hd == 64 else 2
    col = 64 if hd == 64 else 32
    BL = 2 * TB
    HALF = BL // 2 * KC

    def sb(name, shape, dt=F32):
        return ctx.enter_context(nc.sbuf_tensor(f"{name}_{nc.next_id()}", shape, dt))

    s_sb = sb("p_s", [P, 2, BL, KC])
    low = sb("p_low", [P, BL, KC]) if stable else None
    LAG, NE = 3, 4
    e_sb = sb("p_e", [P, NE, BL, KC])
    e_t = sb("p_et", [P, 2, 2, T])
    o_t = sb("p_ot", [P, 2, T])
    mx, den, rden = sb("p_mx", [P, U, BL]), sb("p_den", [P, U, BL]), sb("p_rden", [P, U, BL])
    t_bank, o_bank, y_bank = core.bank[4:6], core.bank[6], core.bank[7]
    group_end = {u: u // per_group for u in range(U) if u % per_group == per_group - 1}

    def s_bank(u, j):
        return core.bank[2 * (u % 2) + j]

    with nc.Block() as block:
        @block.tensor
        def _(pe):
            def scores(u):
                b, p = units[u]
                if u >= 2:
                    pe.wait_ge(sig["s_taken"].sem, sig["s_taken"].at(u - 1))
                for qt in range(TB):
                    ins = nc.tensor.matmul(s_bank(u, qt // 2)[:, qt % 2 * 2 * KC:(qt % 2 + 1) * 2 * KC],
                                           q_of(b, p, qt), k_pair(b, p), start=True, stop=True)
                ins.then_inc(sig["s_done"].sem, sig["s_done"].step())

            def turns(u):
                pe.wait_ge(sig["norm_rows"].sem, sig["norm_rows"].at(u + 1))
                for head in range(2):
                    if u >= 1:
                        pe.wait_ge(sig["turn_taken"].sem, sig["turn_taken"].at(2 * u + head - 1))
                    for qt in range(TB):
                        ins = nc.tensor.transpose(t_bank[head][:KC, qt * P:(qt + 1) * P],
                                                  e_sb[:, u % NE, 2 * qt + head, :], ident)
                    ins.then_inc(sig["turn_done"].sem, sig["turn_done"].step())

            def values(u):
                b, p = units[u]
                g = u // per_group
                pe.wait_ge(sig["turn_taken"].sem, sig["turn_taken"].at(2 * (u + 1)))
                if g >= 1 and u % per_group == 0:
                    pe.wait_ge(sig["o_done"].sem, sig["o_done"].at(g))
                for h in (2 * p, 2 * p + 1):
                    at = h * col % P
                    ins = nc.tensor.matmul(o_bank[at:at + col, :], v_of(b, h), e_t[:, u % 2, h % 2, :],
                                           start=True, stop=True)
                ins.then_inc(sig["pv_done"].sem, sig["pv_done"].step())

            def out(g):
                pe.wait_ge(sig["o_done"].sem, sig["o_done"].at(g + 1))
                if g >= 1:
                    pe.wait_ge(sig["out_added"].sem, sig["out_added"].at(g))
                slot = g % (H // 2 // per_group)
                for qt in range(TB):
                    y = y_bank[:, qt * C:(qt + 1) * C]
                    ins = nc.tensor.matmul(y, o_t[:, g % 2, qt * P:(qt + 1) * P], wo(slot), start=True, stop=slot > 0)
                    if slot == 0:
                        ins = nc.tensor.matmul(y, core.ones_row[0:1, :], bo, start=False, stop=True)
                ins.then_inc(sig["out_done"].sem, sig["out_done"].step())

            for i in range(U + LAG + 3):
                if i < U:
                    scores(i)
                if 0 <= i - LAG < U:
                    turns(i - LAG)
                if 0 <= i - LAG - 1 < U:
                    values(i - LAG - 1)
                if i - LAG - 2 in group_end:
                    out(group_end[i - LAG - 2])

        @block.vector
        def _(dve):
            link, mark = core.dve_chain.link, core.dve_chain.mark

            def then(at):
                dve.wait_ge(core.dve_chain.sem, at)

            def front(u):
                b, p = units[u]
                dve.wait_ge(sig["s_done"].sem, sig["s_done"].at(u + 1))
                if u >= 2:
                    dve.wait_ge(sig["exp_done"].sem, sig["exp_done"].at(u - 1))
                s = s_sb[:, u % 2]
                banks = [s_bank(u, j)[:, :HALF].rearrange("p (g k) -> p g k", k=KC) for j in range(2)]
                parts = [slice(0, TB), slice(TB, BL)]
                if stable:
                    if u >= 1:
                        dve.wait_ge(sig["exp_done"].sem, sig["exp_done"].at(u))
                    for bank, g in zip(banks, parts):
                        nc.vector.tensor_scalar(s[:, g, :], bank, 0.0, None, ALU.max)
                        ins = nc.vector.tensor_scalar(low[:, g, :], bank, 0.0, -1.0, ALU.min, ALU.add)
                    ins.then_inc(sig["s_taken"].sem, sig["s_taken"].step())
                    dve.wait_ge(sig["s_taken"].sem, sig["s_taken"].at(u + 1))
                    link(dve, nc.vector.reciprocal(low[:], low[:]))
                    if u >= NE:
                        dve.wait_ge(sig["turn_done"].sem, sig["turn_done"].at(2 * (u - NE + 1)))
                    nc.vector.tensor_tensor(e_sb[:, u % NE], s, low[:], ALU.subtract).then_inc(
                        sig["exp_done"].sem, sig["exp_done"].step())
                    return
                if mask is None:
                    for bank, g in zip(banks, parts):
                        ins = nc.vector.tensor_reduce(mx[:, u, g], bank, AXX, ALU.max)
                    found = mark(ins)
                    total = sums(u - 1)
                    then(found)
                    for bank, g in zip(banks, parts):
                        ins = nc.vector.tensor_tensor(s[:, g, :], bank, wide(mx[:, u, g], KC, 2), ALU.subtract)
                    ins.then_inc(sig["s_taken"].sem, sig["s_taken"].step())
                    factors(u - 1, total)
                    return
                for j, bank in enumerate(banks):
                    tiles = slice(b * TB + 2 * j, b * TB + 2 * j + 2)
                    out4 = s[:, parts[j], :].rearrange("p (t h) k -> p t h k", h=2)
                    in4 = bank.rearrange("p (t h) k -> p t h k", h=2)
                    ins = nc.vector.tensor_tensor(out4, in4, wide(mask[0][:, tiles, :], 2, 2), ALU.mult)
                ins.then_inc(sig["s_taken"].sem, sig["s_taken"].step())
                dve.wait_ge(sig["s_taken"].sem, sig["s_taken"].at(u + 1))
                s4 = s.rearrange("p (t h) k -> p t h k", h=2)
                link(dve, nc.vector.tensor_tensor(s4, s4, wide(mask[1][:, b * TB:(b + 1) * TB, :], 2, 2), ALU.add))
                link(dve, nc.vector.tensor_reduce(mx[:, u, :], s, AXX, ALU.max))
                nc.vector.tensor_tensor(s, s, wide(mx[:, u, :], KC, 2), ALU.subtract).then_inc(
                    sig["max_done"].sem, sig["max_done"].step())

            def sums(u):
                if u >= 0:
                    dve.wait_ge(sig["exp_done"].sem, sig["exp_done"].at(u + 1))
                    return mark(nc.vector.tensor_reduce(den[:, u, :], e_sb[:, u % NE], AXX, ALU.add))

            def factors(u, total):
                if u < 0:
                    return
                then(total)
                nc.vector.reciprocal(rden[:, u, :], den[:, u, :]).then_inc(sig["aux_dve"].sem, sig["aux_dve"].step())

            def add(g):
                b = units[g * per_group][0]
                dve.wait_ge(sig["out_done"].sem, sig["out_done"].at(g + 1))
                if g >= 1:
                    dve.wait_ge(sig["out_added"].sem, sig["out_added"].at(g))
                half = dst[:, b * TB:(b + 1) * TB, :].rearrange("p t c -> p (t c)")
                nc.vector.tensor_tensor(half, half, y_bank[:], ALU.add).then_inc(
                    sig["out_added"].sem, sig["out_added"].step())

            for i in range(U + LAG + 4):
                if i < U:
                    front(i)
                if 0 <= i - 1 < U and (stable or mask is not None or i == U):
                    factors(i - 1, sums(i - 1))
                if i - LAG - 3 in group_end:
                    add(group_end[i - LAG - 3])

        @block.gpsimd
        def _(pool):
            nc.gpsimd.memset(e_t[64:P], 0.0).then_inc(sig["aux_pool"].sem, sig["aux_pool"].step())
            pool.wait_ge(sig["aux_pool"].sem, sig["aux_pool"].at(1))
            for u in range(U):
                pool.wait_ge(sig["aux_dve"].sem, sig["aux_dve"].at(u + 1))
                e = e_sb[:, u % NE]
                nc.gpsimd.tensor_tensor(e, e, wide(rden[:, u, :], KC, 2), ALU.mult).then_inc(
                    sig["norm_rows"].sem, sig["norm_rows"].step())

        @block.scalar
        def _(act):
            def exps(u):
                ready = sig["s_taken"] if mask is None else sig["max_done"]
                act.wait_ge(ready.sem, ready.at(u + 1))
                if u >= NE:
                    act.wait_ge(sig["turn_done"].sem, sig["turn_done"].at(2 * (u - NE + 1)))
                nc.scalar.activation(e_sb[:, u % NE], s_sb[:, u % 2], ACT.Exp).then_inc(
                    sig["exp_done"].sem, sig["exp_done"].step())

            def copies(u):
                for head in range(2):
                    act.wait_ge(sig["turn_done"].sem, sig["turn_done"].at(2 * u + head + 1))
                    if u >= 2:
                        act.wait_ge(sig["pv_done"].sem, sig["pv_done"].at(u - 1))
                    nc.scalar.activation(e_t[:KC, u % 2, head, :], t_bank[head][:KC, :], ACT.Copy).then_inc(
                        sig["turn_taken"].sem, sig["turn_taken"].step())

            def take(g):
                act.wait_ge(sig["pv_done"].sem, sig["pv_done"].at((g + 1) * per_group))
                if g >= 2:
                    act.wait_ge(sig["out_done"].sem, sig["out_done"].at(g - 1))
                nc.scalar.activation(o_t[:, g % 2, :], o_bank[:], ACT.Copy).then_inc(
                    sig["o_done"].sem, sig["o_done"].step())

            for i in range(U + LAG + 3):
                if i == LAG:
                    act.wait_ge(sig["aux_pool"].sem, sig["aux_pool"].at(1))
                if 0 <= i - LAG < U:
                    copies(i - LAG)
                if i < U and not stable:
                    exps(i)
                if i - LAG - 1 in group_end:
                    take(group_end[i - LAG - 1])
    core.end_region()


def spread_keys(core, outs, zeros):
    nc = core.nc
    with nc.Block() as block:
        @block.gpsimd
        def _(pool):
            for z in zeros:
                nc.gpsimd.memset(z, 0.0)

        @block.vector
        def _(dve):
            for dst, keys, masks in outs:
                nc.vector.tensor_tensor(dst, keys, masks, ALU.mult)
    core.end_region()



def route(core, ctx, wr, row, k, tri, tiles=NT):
    nc, sig = core.nc, core.sig
    E = 8

    def sb(name, shape):
        return ctx.enter_context(nc.sbuf_tensor(f"{name}_{nc.next_id()}", shape, F32))

    logits, gates, ex = sb("logits", [P, NT, E]), sb("gates", [P, NT, E]), sb("gate_exp", [P, NT, E])
    larger, equal = sb("larger", [P, NT, E, E]), sb("equal", [P, NT, E, E])
    rank, mx, tot = sb("rank", [P, NT, E]), sb("gate_max", [P, NT]), sb("gate_sum", [P, NT])
    with nc.Block() as block:
        @block.tensor
        def _(pe):
            for t in range(NT):
                out = core.bank[0][:, t * E:(t + 1) * E]
                ins = nc.tensor.matmul(out, core.xn_t[:, t * P:(t + 1) * P], wr, start=True, stop=row is None)
                if row is not None:
                    ins = nc.tensor.matmul(out, core.ones_row[0:1, :], row, start=False, stop=True)
            ins.then_inc(sig["mm_done"].sem, sig["mm_done"].step())

        @block.vector
        def _(dve):
            link = core.dve_chain.link
            dve.wait_ge(sig["mm_done"].sem, sig["mm_done"].at(1))
            link(dve, nc.vector.tensor_copy(logits[:], core.bank[0][:, :NT * E].rearrange("p (t e) -> p t e", e=E)))
            mine = wide(logits[:], E, 3)
            other = wide(logits[:], E, 2)
            nc.vector.tensor_tensor(larger[:], other, mine, ALU.is_gt)
            link(dve, nc.vector.tensor_tensor(equal[:], other, mine, ALU.is_equal))
            link(dve, nc.vector.tensor_tensor(
                equal[:].rearrange("p t e j -> p t (e j)"), equal[:].rearrange("p t e j -> p t (e j)"),
                wide(tri, NT, 1), ALU.mult))
            link(dve, nc.vector.tensor_tensor(larger[:], larger[:], equal[:], ALU.add))
            nc.vector.tensor_reduce(mx[:], logits[:], AXX, ALU.max)
            link(dve, nc.vector.tensor_reduce(rank[:], larger[:], AXX, ALU.add))
            nc.vector.tensor_tensor(ex[:], logits[:], wide(mx[:], E, 2), ALU.subtract).then_inc(
                sig["max_done"].sem, sig["max_done"].step())
            dve.wait_ge(sig["exp_done"].sem, sig["exp_done"].at(1))
            link(dve, nc.vector.tensor_scalar(rank[:], rank[:], float(k), None, ALU.is_lt))
            link(dve, nc.vector.tensor_tensor(gates[:], ex[:], rank[:], ALU.mult))
            link(dve, nc.vector.tensor_reduce(tot[:], gates[:], AXX, ALU.add))
            link(dve, nc.vector.reciprocal(tot[:], tot[:]))
            nc.vector.tensor_tensor(gates[:], gates[:], wide(tot[:], E, 2), ALU.mult)

        @block.scalar
        def _(act):
            act.wait_ge(sig["max_done"].sem, sig["max_done"].at(1))
            nc.scalar.activation(ex[:], ex[:], ACT.Exp).then_inc(sig["exp_done"].sem, sig["exp_done"].step())
    core.end_region()
    return gates



def feed_forward(core, ctx, dst, jobs, gates=None):
    nc, sig = core.nc, core.sig
    hid = ctx.enter_context(nc.sbuf_tensor(f"hid_{nc.next_id()}", [P, 2, 4, BANK], F32))
    silu = ctx.enter_context(nc.sbuf_tensor(f"silu_{nc.next_id()}", [P, 2, BANK], F32))
    runs = [(j, half) for j in jobs for half in range(B)]
    chunks = [(r, c) for r, (j, half) in enumerate(runs) for c in range(j[5])]
    first = {r: sum(j[5] for j, _ in runs[:r]) for r in range(len(runs) + 1)}
    gated = [n for n, (r, c) in enumerate(chunks) if runs[r][0][1] is not None]

    def hidden_ready(eng, n):
        if n in gated:
            eng.wait_ge(sig["prod_done"].sem, sig["prod_done"].at(gated.index(n) + 1))
        else:
            eng.wait_ge(sig["act_done"].sem, sig["act_done"].at(n + 1))

    with nc.Block() as block:
        @block.tensor
        def _(pe):
            def up(n):
                r, c = chunks[n]
                (w, second, down, bias, fn, nch, gate), half = runs[r]
                if n >= 2:
                    hidden_ready(pe, n - 2)
                x = core.xn_t[:, half * T:(half + 1) * T]
                m = w(c).shape[-1]
                ins = nc.tensor.matmul(core.bank[n % 2][:m, :], w(c), x, start=True, stop=True)
                if second is not None:
                    ins = nc.tensor.matmul(core.bank[2 + n % 2][:m, :], second(c), x, start=True, stop=True)
                ins.then_inc(sig["mm_done"].sem, sig["mm_done"].step())

            def down_part(r):
                (w, second, down, bias, fn, nch, gate), half = runs[r]
                hidden_ready(pe, first[r + 1] - 1)
                if r >= 2:
                    pe.wait_ge(sig["y_added"].sem, sig["y_added"].at(r - 1))
                m = w(0).shape[-1]
                for t in range(TB):
                    out = core.bank[4 + r % 2][:, t * P:(t + 1) * P]
                    for c in range(nch):
                        ins = nc.tensor.matmul(out, hid[:m, r % 2, c, t * P:(t + 1) * P], down(c),
                                               start=c == 0, stop=c == nch - 1)
                ins.then_inc(sig["y_done"].sem, sig["y_done"].step())

            for n in range(len(chunks)):
                r, c = chunks[n]
                up(n)
                if r >= 1 and c == runs[r][0][5] - 1:
                    down_part(r - 1)
            down_part(len(runs) - 1)

        @block.scalar
        def _(act):
            for n, (r, c) in enumerate(chunks):
                (w, second, down, bias, fn, nch, gate), half = runs[r]
                act.wait_ge(sig["mm_done"].sem, sig["mm_done"].at(n + 1))
                m = w(c).shape[-1]
                if second is not None:
                    if n >= 2:
                        act.wait_ge(sig["prod_done"].sem, sig["prod_done"].at(gated.index(n) - 1))
                    out = silu[:m, n % 2, :]
                else:
                    if r >= 2:
                        act.wait_ge(sig["y_done"].sem, sig["y_done"].at(r - 1))
                    out = hid[:m, r % 2, c, :]
                nc.scalar.activation(out, core.bank[n % 2][:m, :], fn, bias=0.0 if bias is None else bias(c)).then_inc(
                    sig["act_done"].sem, sig["act_done"].step())

        @block.vector
        def _(dve):
            def add(r):
                (w, second, down, bias, fn, nch, gate), half = runs[r]
                dve.wait_ge(sig["y_done"].sem, sig["y_done"].at(r + 1))
                if r >= 1:
                    dve.wait_ge(sig["y_added"].sem, sig["y_added"].at(r))
                bank = core.bank[4 + r % 2]
                if gate is None:
                    ins = nc.vector.tensor_tensor(dst[:, half * TB:(half + 1) * TB, :].rearrange("p t c -> p (t c)"),
                                                  dst[:, half * TB:(half + 1) * TB, :].rearrange("p t c -> p (t c)"),
                                                  bank[:], ALU.add)
                else:
                    for t in range(TB):
                        tile = half * TB + t
                        ins = nc.vector.scalar_tensor_tensor(
                            out=dst[:, tile, :], in0=bank[:, t * P:(t + 1) * P],
                            scalar=gates[:, tile, gate:gate + 1], in1=dst[:, tile, :], op0=ALU.mult, op1=ALU.add)
                ins.then_inc(sig["y_added"].sem, sig["y_added"].step())

            for n, (r, c) in enumerate(chunks):
                (w, second, down, bias, fn, nch, gate), half = runs[r]
                if second is not None:
                    dve.wait_ge(sig["act_done"].sem, sig["act_done"].at(n + 1))
                    if r >= 2:
                        dve.wait_ge(sig["y_done"].sem, sig["y_done"].at(r - 1))
                    m = w(c).shape[-1]
                    nc.vector.tensor_tensor(hid[:m, r % 2, c, :], silu[:m, n % 2, :], core.bank[2 + n % 2][:m, :],
                                            ALU.mult).then_inc(sig["prod_done"].sem, sig["prod_done"].step())
                if r >= 1 and c == nch - 1:
                    add(r - 1)
            add(len(runs) - 1)
    core.end_region()


def add_rows(core, dst, row):
    nc, sig = core.nc, core.sig
    with nc.Block() as block:
        @block.tensor
        def _(pe):
            for t in range(TB):
                ins = nc.tensor.matmul(core.bank[7][:, t * P:(t + 1) * P], core.ones_row[0:1, :], row,
                                       start=True, stop=True)
            ins.then_inc(sig["mm_done"].sem, sig["mm_done"].step())

        @block.vector
        def _(dve):
            dve.wait_ge(sig["mm_done"].sem, sig["mm_done"].at(1))
            for half in range(B):
                nc.vector.tensor_tensor(dst[:, half * TB:(half + 1) * TB, :].rearrange("p t c -> p (t c)"),
                                        dst[:, half * TB:(half + 1) * TB, :].rearrange("p t c -> p (t c)"),
                                        core.bank[7][:], ALU.add)
    core.end_region()



def gated_recurrence(core, ctx, w_hg, ident):
    nc, sig = core.nc, core.sig

    def sb(name):
        return ctx.enter_context(nc.sbuf_tensor(f"{name}_{nc.next_id()}", [P, B, T], F32))

    decay, update, low, value, state = sb("decay"), sb("update"), sb("low"), sb("value"), sb("state")
    with nc.Block() as block:
        @block.tensor
        def _(pe):
            for b in range(B):
                for j in range(2):
                    ins = nc.tensor.matmul(core.bank[2 * b + j][:], w_hg[:, j * P:(j + 1) * P],
                                           core.xn_t[:, b * T:(b + 1) * T], start=True, stop=True)
                ins.then_inc(sig["mm_done"].sem, sig["mm_done"].step())
            for b in range(B):
                pe.wait_ge(sig["prod_done"].sem, sig["prod_done"].at(b + 1))
                for t in range(TB):
                    ins = nc.tensor.transpose(core.bank[4 + b][:, t * P:(t + 1) * P],
                                              state[:, b, t * P:(t + 1) * P], ident)
                ins.then_inc(sig["turn_done"].sem, sig["turn_done"].step())

        @block.scalar
        def _(act):
            for b in range(B):
                act.wait_ge(sig["mm_done"].sem, sig["mm_done"].at(b + 1))
                nc.scalar.activation(decay[:, b, :], core.bank[2 * b + 1][:], ACT.Sigmoid, scale=-1.0)
                nc.scalar.activation(update[:, b, :], core.bank[2 * b + 1][:], ACT.Sigmoid)
                act.wait_ge(sig["aux_dve"].sem, sig["aux_dve"].at(b + 1))
                nc.scalar.activation(value[:, b, :], low[:, b, :], ACT.Sigmoid).then_inc(
                    sig["act_done"].sem, sig["act_done"].step())

        @block.vector
        def _(dve):
            link = core.dve_chain.link
            for b in range(B):
                dve.wait_ge(sig["mm_done"].sem, sig["mm_done"].at(b + 1))
                nc.vector.tensor_scalar(low[:, b, :], core.bank[2 * b][:], 0.0, None, ALU.min).then_inc(
                    sig["aux_dve"].sem, sig["aux_dve"].step())
            for b in range(B):
                dve.wait_ge(sig["act_done"].sem, sig["act_done"].at(b + 1))
                link(dve, nc.vector.scalar_tensor_tensor(out=value[:, b, :], in0=core.bank[2 * b][:], scalar=0.0,
                                                         in1=value[:, b, :], op0=ALU.max, op1=ALU.add))
                link(dve, nc.vector.tensor_tensor(value[:, b, :], value[:, b, :], update[:, b, :], ALU.mult))
                nc.vector.tensor_tensor_scan(out=state[:, b, :], data0=decay[:, b, :], data1=value[:, b, :],
                                             initial=0.0, op0=ALU.mult, op1=ALU.add).then_inc(
                    sig["prod_done"].sem, sig["prod_done"].step())
            for b in range(B):
                dve.wait_ge(sig["turn_done"].sem, sig["turn_done"].at(b + 1))
                half = core.x_sb[:, b * TB:(b + 1) * TB, :].rearrange("p t c -> p (t c)")
                nc.vector.tensor_tensor(half, half, core.bank[4 + b][:], ALU.add)
    core.end_region()


def state_space(core, ctx, w):
    nc, sig = core.nc, core.sig
    S = 16

    def sb(name, shape):
        return ctx.enter_context(nc.sbuf_tensor(f"{name}_{nc.next_id()}", shape, F32))

    z, low = sb("delta_in", [P, B, T]), sb("delta_low", [P, B, T])
    dbar, decay, bt, ct, hs = (sb(n, [S, B, T]) for n in ("dbar", "ss_decay", "ss_bt", "ss_ct", "ss_h"))
    sa, ysum = sb("ss_a", [S, 1]), sb("ss_y", [P, NT])
    with nc.Block() as block:
        @block.tensor
        def _(pe):
            for b in range(B):
                x = core.xn_t[:, b * T:(b + 1) * T]
                nc.tensor.matmul(core.bank[b][:], w["ss_wd"], x, start=True, stop=True)
                nc.tensor.matmul(core.bank[2 + b][:S, :], w["ss_wb"], x, start=True, stop=True)
                ins = nc.tensor.matmul(core.bank[4 + b][:S, :], w["ss_wc"], x, start=True, stop=True)
                ins.then_inc(sig["mm_done"].sem, sig["mm_done"].step())
            nc.tensor.matmul(core.bank[6][:S, 0:1], w["ss_a"], w["mean_col"][:, 0:1], start=True, stop=True).then_inc(
                sig["aux_pe"].sem, sig["aux_pe"].step())
            for b in range(B):
                pe.wait_ge(sig["prod_done"].sem, sig["prod_done"].at(b + 1))
                nc.tensor.matmul(core.bank[b][:S, :], w["mean_col"], z[:, b, :], start=True, stop=True).then_inc(
                    sig["s_done"].sem, sig["s_done"].step())
            for b in range(B):
                pe.wait_ge(sig["o_done"].sem, sig["o_done"].at(b + 1))
                if b == 0:
                    pe.wait_ge(sig["aux_dve"].sem, sig["aux_dve"].at(1))
                for t in range(TB):
                    ins = nc.tensor.matmul(core.bank[6 + b][:, t:t + 1],
                                           hs[:, b, t * P:(t + 1) * P], w["ones"][:S, 0:1], start=True, stop=True)
                ins.then_inc(sig["pv_done"].sem, sig["pv_done"].step())
            for b in range(B):
                pe.wait_ge(sig["act_done"].sem, sig["act_done"].at(2 * b + 2))
                for t in range(TB):
                    tile = b * TB + t
                    nc.tensor.matmul(core.bank[2 + b][:, t * P:(t + 1) * P], core.xn_t[:, tile * P:(tile + 1) * P],
                                     w["ss_wo"], start=True, stop=True)
                    ins = nc.tensor.matmul(core.bank[4 + b][:, t * P:(t + 1) * P], core.ones_row[0:1, :],
                                           w["ss_bo"], start=True, stop=True)
                ins.then_inc(sig["y_done"].sem, sig["y_done"].step())

        @block.scalar
        def _(act):
            for b in range(B):
                act.wait_ge(sig["mm_done"].sem, sig["mm_done"].at(b + 1))
                nc.scalar.activation(bt[:, b, :], core.bank[2 + b][:S, :], ACT.Identity, bias=w["ss_bb"][:S, :]).then_inc(
                    sig["act_done"].sem, sig["act_done"].step())
                nc.scalar.activation(ct[:, b, :], core.bank[4 + b][:S, :], ACT.Identity, bias=w["ss_bc"][:S, :]).then_inc(
                    sig["act_done"].sem, sig["act_done"].step())
            for b in range(B):
                act.wait_ge(sig["aux_dve"].sem, sig["aux_dve"].at(b + 2))
                nc.scalar.activation(low[:, b, :], low[:, b, :], ACT.Exp, scale=-1.0).then_inc(
                    sig["aux_act"].sem, sig["aux_act"].step())
            for b in range(B):
                act.wait_ge(sig["aux_act"].sem, sig["aux_act"].at(b + 1))
                nc.scalar.activation(low[:, b, :], low[:, b, :], ACT.Ln, bias=1.0).then_inc(
                    sig["exp_done"].sem, sig["exp_done"].step())
            act.wait_ge(sig["aux_dve"].sem, sig["aux_dve"].at(1))
            nc.scalar.activation(sa[:], sa[:], ACT.Sigmoid).then_inc(sig["max_done"].sem, sig["max_done"].step())

        @block.vector
        def _(dve):
            link = core.dve_chain.link
            dve.wait_ge(sig["aux_pe"].sem, sig["aux_pe"].at(1))
            nc.vector.tensor_copy(sa[:], core.bank[6][:S, 0:1]).then_inc(sig["aux_dve"].sem, sig["aux_dve"].step())
            for b in range(B):
                link(dve, nc.vector.tensor_scalar(z[:, b, :], core.bank[b][:], w["ss_bd"], None, ALU.add))
                nc.vector.scalar_tensor_tensor(out=low[:, b, :], in0=z[:, b, :], scalar=-1.0, in1=z[:, b, :],
                                               op0=ALU.mult, op1=ALU.max).then_inc(
                    sig["aux_dve"].sem, sig["aux_dve"].step())
            for b in range(B):
                dve.wait_ge(sig["exp_done"].sem, sig["exp_done"].at(b + 1))
                nc.vector.scalar_tensor_tensor(out=z[:, b, :], in0=z[:, b, :], scalar=0.0, in1=low[:, b, :],
                                               op0=ALU.max, op1=ALU.add).then_inc(
                    sig["prod_done"].sem, sig["prod_done"].step())
            dve.wait_ge(sig["max_done"].sem, sig["max_done"].at(1))
            dve.wait_ge(sig["act_done"].sem, sig["act_done"].at(2 * B))
            for b in range(B):
                dve.wait_ge(sig["s_done"].sem, sig["s_done"].at(b + 1))
                nc.vector.tensor_scalar(decay[:, b, :], core.bank[b][:S, :], -1.0, 1.0, ALU.mult, ALU.add)
                link(dve, nc.vector.tensor_tensor(bt[:, b, :], core.bank[b][:S, :], bt[:, b, :], ALU.mult))
                link(dve, nc.vector.tensor_scalar(bt[:, b, :], bt[:, b, :], sa[:], None, ALU.mult))
                link(dve, nc.vector.tensor_tensor_scan(out=hs[:, b, :], data0=decay[:, b, :], data1=bt[:, b, :],
                                                       initial=0.0, op0=ALU.mult, op1=ALU.add))
                nc.vector.tensor_tensor(hs[:, b, :], hs[:, b, :], ct[:, b, :], ALU.mult).then_inc(
                    sig["o_done"].sem, sig["o_done"].step())
            for b in range(B):
                dve.wait_ge(sig["pv_done"].sem, sig["pv_done"].at(b + 1))
                link(dve, nc.vector.tensor_copy(ysum[:, b * TB:(b + 1) * TB], core.bank[6 + b][:, 0:TB]))
                dve.wait_ge(sig["y_done"].sem, sig["y_done"].at(b + 1))
                for t in range(TB):
                    tile = b * TB + t
                    ins = nc.vector.scalar_tensor_tensor(
                        out=core.x_sb[:, tile, :], in0=core.bank[2 + b][:, t * P:(t + 1) * P],
                        scalar=ysum[:, tile:tile + 1], in1=core.x_sb[:, tile, :], op0=ALU.mult, op1=ALU.add)
                link(dve, ins)
                half = core.x_sb[:, b * TB:(b + 1) * TB, :].rearrange("p t c -> p (t c)")
                nc.vector.tensor_tensor(half, half, core.bank[4 + b][:], ALU.add)
    core.end_region()



def bit_feed_forward(core, ctx, w1_t, w2_t, b1_rows, b2_row, ident, ones):
    nc, sig = core.nc, core.sig
    F = 4 * P

    def sb(name, shape, dt=F32):
        return ctx.enter_context(nc.sbuf_tensor(f"{name}_{nc.next_id()}", shape, dt))

    asum, wmean, wscale = sb("asum", [P, 2]), sb("wmean", [P, 2]), sb("wscale", [P, 2])
    wtmp = sb("wtmp", [P, F])
    w1q, w2q = sb("w1q", [P, F], BF16), sb("w2q", [P, F], BF16)
    sq = sb("sq", [P, NT, C])
    ms, amax, qscale, step1 = (sb(n, [P, NT]) for n in ("ms", "amax", "qscale", "step1"))
    ms2, amax2, qscale2, step2, r2 = (sb(n, [P, NT]) for n in ("ms2", "amax2", "qscale2", "step2", "r2"))
    xq_t = sb("xq_t", [P, NT, P], BF16)
    hid = sb("bhid", [P, NT, F])
    sq2 = sb("sq2", [P, 2, F])
    hq_t = sb("hq_t", [P, 2, 4, P], BF16)

    with nc.Block() as block:
        @block.vector
        def _(dve):
            link = core.dve_chain.link
            nc.vector.tensor_reduce(asum[:, 0:1], w1_t, AXX, ALU.add, apply_absolute_value=True)
            nc.vector.tensor_reduce(asum[:, 1:2], w2_t, AXX, ALU.add, apply_absolute_value=True).then_inc(
                sig["aux_dve"].sem, sig["aux_dve"].step())
            link(dve, nc.vector.tensor_tensor(sq[:], core.xn[:], core.xn[:], ALU.mult))
            link(dve, nc.vector.tensor_reduce(ms[:], sq[:], AXX, ALU.add))
            nc.vector.tensor_scalar(core.spread[:], ms[:], 1.0 / C, 1e-5, ALU.mult, ALU.add).then_inc(
                sig["norm_stats"].sem, sig["norm_stats"].step())
            dve.wait_ge(sig["aux_pe"].sem, sig["aux_pe"].at(1))
            link(dve, nc.vector.tensor_scalar(wmean[:], core.bank[0][:, 0:2], 1.0 / (C * F), 1e-5, ALU.mult, ALU.max))
            link(dve, nc.vector.reciprocal(wscale[:], wmean[:]))
            for j, (w, q) in enumerate(((w1_t, w1q), (w2_t, w2q))):
                link(dve, nc.vector.tensor_scalar(wtmp[:], w, wscale[:, j:j + 1], ROUND, ALU.mult, ALU.add))
                link(dve, nc.vector.tensor_scalar(wtmp[:], wtmp[:], -ROUND, 1.0, ALU.add, ALU.min))
                link(dve, nc.vector.tensor_scalar(q[:], wtmp[:], -1.0, None, ALU.max))
            dve.wait_ge(sig["norm_scale"].sem, sig["norm_scale"].at(1))
            link(dve, nc.vector.tensor_tensor(core.xn[:], core.xn[:], wide(core.rstd[:], C, 2), ALU.mult))
            link(dve, nc.vector.tensor_reduce(amax[:], core.xn[:], AXX, ALU.max, apply_absolute_value=True))
            link(dve, nc.vector.tensor_scalar(amax[:], amax[:], 1e-5, None, ALU.max))
            link(dve, nc.vector.reciprocal(qscale[:], amax[:]))
            link(dve, nc.vector.tensor_scalar(qscale[:], qscale[:], 127.0, None, ALU.mult))
            link(dve, nc.vector.tensor_scalar(step1[:], amax[:], wmean[:, 0:1], 1.0 / 127.0, ALU.mult, ALU.mult))
            link(dve, nc.vector.tensor_tensor(core.xn[:], core.xn[:], wide(qscale[:], C, 2), ALU.mult))
            link(dve, nc.vector.tensor_scalar(core.xn[:], core.xn[:], ROUND, None, ALU.add))
            nc.vector.tensor_scalar(core.xn[:], core.xn[:], -ROUND, None, ALU.add).then_inc(
                sig["norm_rows"].sem, sig["norm_rows"].step())

        @block.gpsimd
        def _(pool):
            pool.wait_ge(sig["norm_stats"].sem, sig["norm_stats"].at(1))
            nc.gpsimd.tensor_tensor(core.rstd[:], core.spread[:], core.minus_half[:], ALU.pow).then_inc(
                sig["norm_scale"].sem, sig["norm_scale"].step())

        @block.tensor
        def _(pe):
            pe.wait_ge(sig["aux_dve"].sem, sig["aux_dve"].at(1))
            nc.tensor.matmul(core.bank[0][:, 0:2], ones, asum[:], start=True, stop=True).then_inc(
                sig["aux_pe"].sem, sig["aux_pe"].step())
            pe.wait_ge(sig["norm_rows"].sem, sig["norm_rows"].at(1))
            for t in range(NT):
                ins = nc.tensor.transpose(core.bank[1 + t // TB][:, (t % TB) * P:(t % TB + 1) * P],
                                          core.xn[:, t, :], ident)
            ins.then_inc(sig["norm_turned"].sem, sig["norm_turned"].step())

        @block.scalar
        def _(act):
            act.wait_ge(sig["norm_turned"].sem, sig["norm_turned"].at(1))
            for b in range(B):
                nc.scalar.activation(xq_t[:, b * TB:(b + 1) * TB, :].rearrange("p t c -> p (t c)"),
                                     core.bank[1 + b][:], ACT.Copy)
    core.end_region()

    with nc.Block() as block:
        @block.tensor
        def _(pe):
            def turn(t):
                pe.wait_ge(sig["prod_done"].sem, sig["prod_done"].at(t + 1))
                if t >= 2:
                    pe.wait_ge(sig["turn_taken"].sem, sig["turn_taken"].at(t - 1))
                for c in range(4):
                    ins = nc.tensor.transpose(core.bank[2 + t % 2][:, c * P:(c + 1) * P],
                                              hid[:, t, c * P:(c + 1) * P], ident)
                ins.then_inc(sig["turn_done"].sem, sig["turn_done"].step())

            def second(t):
                pe.wait_ge(sig["turn_taken"].sem, sig["turn_taken"].at(t + 1))
                if t >= 2:
                    pe.wait_ge(sig["y_added"].sem, sig["y_added"].at(t - 1))
                for c in range(4):
                    nc.tensor.matmul(core.bank[4 + t % 2][:, 0:C], hq_t[:, t % 2, c, :], w2q[:, c * P:(c + 1) * P],
                                     start=c == 0, stop=c == 3)
                nc.tensor.matmul(core.bank[6 + t % 2][:, 0:C], core.ones_row[0:1, :], b2_row, start=True,
                                 stop=True).then_inc(sig["y_done"].sem, sig["y_done"].step())

            for t in range(NT):
                if t >= 2:
                    pe.wait_ge(sig["s_taken"].sem, sig["s_taken"].at(t - 1))
                nc.tensor.matmul(core.bank[t % 2][:], xq_t[:, t, :], w1q[:], start=True, stop=True).then_inc(
                    sig["mm_done"].sem, sig["mm_done"].step())
            for t in range(NT + 1):
                if t < NT:
                    turn(t)
                if t >= 1:
                    second(t - 1)

        @block.scalar
        def _(act):
            for t in range(NT):
                act.wait_ge(sig["s_taken"].sem, sig["s_taken"].at(t + 1))
                nc.scalar.activation(hid[:, t, :], hid[:, t, :], ACT.Gelu).then_inc(
                    sig["act_done"].sem, sig["act_done"].step())
                act.wait_ge(sig["act_done"].sem, sig["act_done"].at(t + 1))
                if t >= 2:
                    act.wait_ge(sig["aux_act"].sem, sig["aux_act"].at(t - 1))
                nc.scalar.activation(sq2[:, t % 2, :], hid[:, t, :], ACT.Square, accum_out=ms2[:, t:t + 1]).then_inc(
                    sig["aux_act"].sem, sig["aux_act"].step())
            for t in range(NT):
                act.wait_ge(sig["turn_done"].sem, sig["turn_done"].at(t + 1))
                if t >= 2:
                    act.wait_ge(sig["y_done"].sem, sig["y_done"].at(t - 1))
                nc.scalar.activation(hq_t[:, t % 2, :, :].rearrange("p c q -> p (c q)"), core.bank[2 + t % 2][:],
                                     ACT.Copy).then_inc(sig["turn_taken"].sem, sig["turn_taken"].step())

        @block.gpsimd
        def _(pool):
            pool.wait_ge(sig["norm_stats"].sem, sig["norm_stats"].at(1))
            nc.gpsimd.tensor_tensor(r2[:], ms2[:], core.minus_half[:], ALU.pow).then_inc(
                sig["norm_scale"].sem, sig["norm_scale"].step())

        @block.vector
        def _(dve):
            link, mark = core.dve_chain.link, core.dve_chain.mark

            def dequant(t):
                dve.wait_ge(sig["mm_done"].sem, sig["mm_done"].at(t + 1))
                nc.vector.scalar_tensor_tensor(out=hid[:, t, :], in0=core.bank[t % 2][:], scalar=step1[:, t:t + 1],
                                               in1=b1_rows, op0=ALU.mult, op1=ALU.add).then_inc(
                    sig["s_taken"].sem, sig["s_taken"].step())

            def quantise(pair):
                done = {}
                for t in pair:
                    done[t] = mark(nc.vector.tensor_scalar(hid[:, t, :], hid[:, t, :], r2[:, t:t + 1],
                                                           qscale2[:, t:t + 1], ALU.mult, ALU.mult))
                for t in pair:
                    dve.wait_ge(core.dve_chain.sem, done[t])
                    done[t] = mark(nc.vector.tensor_scalar(hid[:, t, :], hid[:, t, :], ROUND, None, ALU.add))
                for t in pair:
                    dve.wait_ge(core.dve_chain.sem, done[t])
                    nc.vector.tensor_scalar(hid[:, t, :], hid[:, t, :], -ROUND, None, ALU.add).then_inc(
                        sig["prod_done"].sem, sig["prod_done"].step())

            def finish(pair):
                done = {}
                for t in pair:
                    dve.wait_ge(sig["y_done"].sem, sig["y_done"].at(t + 1))
                    done[t] = mark(nc.vector.scalar_tensor_tensor(
                        out=core.x_sb[:, t, :], in0=core.bank[4 + t % 2][:, 0:C], scalar=step2[:, t:t + 1],
                        in1=core.x_sb[:, t, :], op0=ALU.mult, op1=ALU.add))
                for t in pair:
                    dve.wait_ge(core.dve_chain.sem, done[t])
                    nc.vector.tensor_tensor(core.x_sb[:, t, :], core.x_sb[:, t, :], core.bank[6 + t % 2][:, 0:C],
                                            ALU.add).then_inc(sig["y_added"].sem, sig["y_added"].step())

            for t in range(NT + 1):
                if t < NT:
                    dequant(t)
                if t >= 1:
                    dve.wait_ge(sig["act_done"].sem, sig["act_done"].at(t))
                    ins = nc.vector.tensor_reduce(amax2[:, t - 1:t], hid[:, t - 1, :], AXX, ALU.max,
                                                  apply_absolute_value=True)
            link(dve, ins)
            dve.wait_ge(sig["aux_act"].sem, sig["aux_act"].at(NT))
            nc.vector.tensor_scalar(ms2[:], ms2[:], 1.0 / F, 1e-5, ALU.mult, ALU.add).then_inc(
                sig["norm_stats"].sem, sig["norm_stats"].step())
            dve.wait_ge(sig["norm_scale"].sem, sig["norm_scale"].at(1))
            link(dve, nc.vector.tensor_tensor(amax2[:], amax2[:], r2[:], ALU.mult))
            link(dve, nc.vector.tensor_scalar(amax2[:], amax2[:], 1e-5, None, ALU.max))
            link(dve, nc.vector.reciprocal(qscale2[:], amax2[:]))
            link(dve, nc.vector.tensor_scalar(qscale2[:], qscale2[:], 127.0, None, ALU.mult))
            link(dve, nc.vector.tensor_scalar(step2[:], amax2[:], wmean[:, 1:2], 1.0 / 127.0, ALU.mult, ALU.mult))
            for t in range(0, NT + 2, 2):
                if t < NT:
                    quantise((t, t + 1))
                if t >= 2:
                    finish((t - 2, t - 1))
    core.end_region()



def linear_experts(core, ctx, w_in, w_out_t, gates):
    nc, sig = core.nc, core.sig
    E = 8
    both = ctx.enter_context(nc.sbuf_tensor("expert_product", [P, E, C], F32))
    with nc.Block() as block:
        @block.tensor
        def _(pe):
            for e in range(E):
                for c in range(4):
                    k = (e * 4 + c) * P
                    ins = nc.tensor.matmul(core.bank[e // 4][:, (e % 4) * C:(e % 4 + 1) * C], w_in[:, k:k + P],
                                           w_out_t[:, k:k + P], start=c == 0, stop=c == 3)
                if e % 4 == 3:
                    ins.then_inc(sig["mm_done"].sem, sig["mm_done"].step())
            pe.wait_ge(sig["act_done"].sem, sig["act_done"].at(2))
            for n in range(2 * NT):
                t, half = n // 2, n % 2
                if n >= 4:
                    pe.wait_ge(sig["y_added"].sem, sig["y_added"].at(n - 3))
                nc.tensor.matmul(core.bank[2 + n % 4][:], core.xn_t[:, t * P:(t + 1) * P],
                                 both[:, 4 * half:4 * half + 4, :].rearrange("p e c -> p (e c)"),
                                 start=True, stop=True).then_inc(sig["y_done"].sem, sig["y_done"].step())

        @block.scalar
        def _(act):
            for half in range(2):
                act.wait_ge(sig["mm_done"].sem, sig["mm_done"].at(half + 1))
                nc.scalar.activation(both[:, 4 * half:4 * half + 4, :].rearrange("p e c -> p (e c)"),
                                     core.bank[half][:], ACT.Copy).then_inc(
                    sig["act_done"].sem, sig["act_done"].step())

        @block.vector
        def _(dve):
            link = core.dve_chain.link
            for n in range(2 * NT):
                t, half = n // 2, n % 2
                dve.wait_ge(sig["y_done"].sem, sig["y_done"].at(n + 1))
                for e in range(4):
                    g = 4 * half + e
                    ins = nc.vector.scalar_tensor_tensor(
                        out=core.x_sb[:, t, :], in0=core.bank[2 + n % 4][:, e * C:(e + 1) * C],
                        scalar=gates[:, t, g:g + 1], in1=core.x_sb[:, t, :], op0=ALU.mult, op1=ALU.add)
                    if e < 3:
                        link(dve, ins)
                ins.then_inc(sig["y_added"].sem, sig["y_added"].step())
                dve.wait_ge(sig["y_added"].sem, sig["y_added"].at(n + 1))
    core.end_region()



CONSTANTS = [("ident", P), ("diagonal", P), ("ones", P), ("mean_col", 16), ("tri", 64), ("gamma", C), ("beta", C),
             ("head_gates", H), ("ctx_t", B * KC), ("ctx_rows", B * C),
             ("flip", P), ("mask8", H), ("mask64", 2), ("proj_w", C), ("norm_w", 7), ("ff_b1", 8)]
FIRST = [("l0_wq", C), ("l0_wk", C), ("l0_wv", 512), ("l0_wo", 512), ("l0_bq", 1), ("l0_bk", 1)]
CONTEXT = [("wq", C), ("wk", C), ("wv", 512), ("wo", 512), ("bq", 1), ("bk", 1)]
EARLY = [("l1_wq", C), ("l1_wk", C), ("l1_wv", 512), ("l1_wo", 512), ("l1_bq", 1), ("l1_bk", 1)] + [
    (f"l1x_{m}", c) for m, c in CONTEXT] + [("l1f_b1", 32), ("l1f_b2", C), ("l1f_wg", 8), ("w_hg", 256)]
LATE = [(f"l3x_{m}", c) for m, c in CONTEXT] + [
    ("bit_w1", 512), ("bit_w2", 512), ("bit_b1", 512),
    ("ss_wd", C), ("ss_wb", 16), ("ss_wc", 16), ("ss_wo", C), ("ss_a", 16), ("ss_bd", 1), ("ss_bb", 1), ("ss_bc", 1),
    ("l3f_wg", 8)]
ROPE = [("swap", P), ("cos", T), ("sin", T)]
ROWS = [("l0_bv", 512), ("l1_bv", 512), ("l1_bo", C), ("l1x_bv", 512), ("l1x_bo", C), ("l1f_bg", 8), ("bo0", C),
        ("bo1", C), ("cbo0", C), ("cbo1", C), ("fb0", C), ("fb1", C), ("proj_b", C), ("bit_b2", C), ("ss_bo", C),
        ("l3x_bv", 512), ("l3x_bo", C), ("ones_row", P)]
FFN0 = [("w1", 1024), ("w2", 1024), ("w3", 1024), ("ws1", 32), ("ws2", 32), ("ws3", C), ("wr", 8)]
FFN1 = [("up", 4096), ("down", 4096)]
SELF = [("wq", 1024), ("wk", 1024), ("wv", 1024), ("wo", 1024)]
CROSS = SELF + [("fw1", 512), ("fw2", 512)]
FFN3 = [("w_in", 4096), ("w_out", 4096)]
RELS = 2 * T - 1
TOEPLITZ = T + (TB - 1) * P


def width(pack):
    return sum(c for _, c in pack)


def views(tile, pack, at=0):
    out = {}
    for name, c in pack:
        out[name] = tile[:, at:at + c]
        at += c
    return out


def decoder(nc, d):
    with ExitStack() as ctx:
        core = Core(nc, ctx)
        sig = core.sig

        def sb(name, shape, dt=F32):
            return ctx.enter_context(nc.sbuf_tensor(name, shape, dt))

        const_sb, small_sb = sb("const_sb", [P, width(CONSTANTS)]), sb("small_sb", [P, max(width(EARLY), width(LATE))])
        rows_sb = sb("rows_sb", [1, width(ROWS)])
        arena = sb("arena", [P, H * TOEPLITZ])
        arena2 = sb("arena2", [P, width(FFN1)])
        diag_bf, ident_bf = sb("diag_bf", [P, P], BF16), sb("ident_bf", [P, P], BF16)
        key_row = sb("key_row", [P, B * T], BF16)
        w = {**views(const_sb, CONSTANTS), **views(small_sb, EARLY), **views(small_sb, LATE),
             **views(arena2, FIRST, width(FFN0))}
        row = {n: v[0:1, :] for n, v in views(rows_sb, ROWS).items()}
        w["ss_bo"] = row["ss_bo"]
        core.ones_row = row["ones_row"]
        ident = w["ident"]
        load = {n: ctx.enter_context(nc.semaphore(f"load_{n}")) for n in (
            "x", "const", "small", "mask0", "mask4", "key_mask", "late", "toeplitz", "ffn0", "ffn1", "self0", "cross0", "self1", "cross1", "rope",
            "ffn3", "out")}
        parts = 4

        def fetch(eng, dst, src, name):
            n = dst.shape[-1] // parts
            for i in range(parts):
                eng.dma_start(dst[:, i * n:(i + 1) * n], src[:, i * n:(i + 1) * n]).then_inc(load[name], 16)

        LOADED = 16 * parts
        slot0, slot1, slot2 = 0, width(SELF), width(SELF) + width(CROSS)

        with ExitStack() as scope:
            key_u8 = scope.enter_context(nc.sbuf_tensor("key_u8", [1, B * T], U8))
            key_f = scope.enter_context(nc.sbuf_tensor("key_f", [1, B * T], F32))
            with nc.Block() as block:
                @block.sync
                def _(sp):
                    sp.dma_start(core.x_sb[:], d["x"]).then_inc(load["x"], 16)
                    sp.dma_start(const_sb[:], d["constants"]).then_inc(load["const"], 16)
                    sp.dma_start(rows_sb[:], d["rows"]).then_inc(load["const"], 16)
                    sp.dma_start(arena2[:, width(FFN0):width(FFN0) + width(FIRST)], d["first"]).then_inc(load["const"], 16)
                    sp.dma_start(key_u8[:], d["key_mask"]).then_inc(load["key_mask"], 16)
                    fetch(sp, arena2[:, :width(FFN0)], d["ffn0"], "ffn0")
                    sp.dma_start(small_sb[:, :width(EARLY)], d["early"]).then_inc(load["small"], 16)
                    if 3 in SUBLAYERS:
                        base = d["relative"]
                        for h in range(H):
                            src = bass.AP(base.tensor, h * RELS, [[1, P], [1, TOEPLITZ]])
                            sp.dma_start(arena[:, h * TOEPLITZ:(h + 1) * TOEPLITZ], src).then_inc(
                                load["toeplitz"], 16)

                @block.vector
                def _(dve):
                    link = core.dve_chain.link
                    nc.vector.memset(core.minus_half[:], -0.5)
                    dve.wait_ge(load["const"], 48)
                    nc.vector.tensor_copy(diag_bf[:], w["diagonal"])
                    nc.vector.tensor_copy(ident_bf[:], ident)
                    dve.wait_ge(load["key_mask"], 16)
                    link(dve, nc.vector.tensor_copy(key_f[:], key_u8[:]))
                    link(dve, nc.vector.tensor_scalar(key_f[:], key_f[:], 0.0, None, ALU.is_equal))
                    nc.vector.tensor_scalar(key_row[0:1, :], key_f[:], NEG, None, ALU.mult)
                    nc.vector.tensor_scalar(key_row[64:65, :], key_f[:], NEG, None, ALU.mult)
                    dve.wait_ge(load["x"], 16)
            core.end_region()

            def context_mask(s, name, low):
                mask_sb, m01, mneg = (s.enter_context(nc.sbuf_tensor(f"{n}_{name}", [P, NT, KC], dt))
                                      for n, dt in (("mask", I32), ("m01", F32), ("mneg", F32)))
                with nc.Block() as block:
                    @block.sync
                    def _(sp):
                        sp.dma_start(mask_sb[:], d[name]).then_inc(load[name], 16)

                    @block.vector
                    def _(dve):
                        dve.wait_ge(load[name], 16)
                        core.dve_chain.link(dve, nc.vector.tensor_scalar(m01[:], mask_sb[:], 0, None, ALU.not_equal))
                        nc.vector.tensor_scalar(mneg[:], m01[:], -1.0, low, ALU.add, ALU.mult)
                core.end_region()
                return m01, mneg

            def small_self(name, top=None, gate=None, causal=None, bo=None):
                for b in range(B):
                    with ExitStack() as s:
                        def tb(n, shape):
                            return s.enter_context(nc.sbuf_tensor(f"{n}_{nc.next_id()}", shape, F32))
                        q, k, v = tb("q8", [P, T]), tb("k8", [P, T]), tb("v8", [P, TB, 512])
                        xt = core.xn_t[:, b * T:(b + 1) * T]
                        jobs = [(q[:], w[f"{name}_wq"], xt, w[f"{name}_bq"], None, False),
                                (k[:], w[f"{name}_wk"], xt, w[f"{name}_bk"], None, False)]
                        for t in range(TB):
                            jobs.append((v[:, t, :], xt[:, t * P:(t + 1) * P], w[f"{name}_wv"], None,
                                         row[f"{name}_bv"], False))
                        project(core, jobs)
                        self_attention(core, s, b, lambda h, qt: q[:, qt * P:(qt + 1) * P], lambda h: k[:],
                                       lambda h: w["mask8"][:, h:h + 1], lambda h, c: v[:, c, h * 32:(h + 1) * 32], 8,
                                       core.x_sb, ident, lambda g: w[f"{name}_wo"][:, g * C:(g + 1) * C], bo,
                                       causal=causal, top=top, gate=gate)

            if 0 in SUBLAYERS:
                normalise(core, core.x_sb, ident)
                small_self("l0", causal=(ident_bf[:], diag_bf[:]))

            if 1 in SUBLAYERS:
                normalise(core, core.x_sb, ident)
                with ExitStack() as s:
                    m01, mneg = context_mask(s, "mask0", 9.0e15)

                    def finish(dve, u, o_sb):
                        link = core.dve_chain.link
                        for g in range(TB):
                            last = nc.vector.bn_stats(core.stats[:, g, :], o_sb[:, g * C:(g + 1) * C])
                        link(dve, last)
                        for g in range(TB):
                            last = nc.vector.bn_aggr(core.mv[:, g, :], core.stats[:, g, :])
                        link(dve, last)
                        nc.vector.tensor_scalar(core.spread[:, 0:TB], core.mv[:, 0:TB, 1], 1e-5, None,
                                                ALU.add).then_inc(sig["norm_stats"].sem, sig["norm_stats"].step())
                        dve.wait_ge(sig["norm_scale"].sem, sig["norm_scale"].at(u + 1))
                        for g in range(TB):
                            last = nc.vector.tensor_scalar(o_sb[:, g * C:(g + 1) * C], o_sb[:, g * C:(g + 1) * C],
                                                           core.mv[:, g, 0:1], core.rstd[:, g:g + 1], ALU.subtract,
                                                           ALU.mult)
                        link(dve, last)
                        o3 = o_sb[:].rearrange("p (g c) -> p g c", c=C)
                        link(dve, nc.vector.tensor_tensor(o3, o3, wide(w["gamma"], TB, 1), ALU.mult))
                        link(dve, nc.vector.tensor_tensor(o3, o3, wide(w["beta"], TB, 1), ALU.add))
                        tiles = core.x_sb[:, u * TB:(u + 1) * TB, :]
                        link(dve, nc.vector.tensor_tensor(tiles, tiles, o3, ALU.add))

                    context_attention(
                        core, s, [0, 1], TB, lambda u, g: core.xn_t[:, (u * TB + g) * P:(u * TB + g + 1) * P],
                        lambda u, g: w["ctx_t"][:, u * KC:(u + 1) * KC],
                        lambda u, g: w["ctx_rows"][:KC, u * C:(u + 1) * C], C ** -0.5, ident,
                        mask=(lambda u, g: m01[:, u * TB + g.start:u * TB + g.stop, :],
                              lambda u, g: mneg[:, u * TB + g.start:u * TB + g.stop, :]), finish=finish)

        if 2 in SUBLAYERS:
            normalise(core, core.x_sb, ident, loads=[(load["ffn0"], LOADED)])
            with ExitStack() as s:
                f = views(arena2, FFN0)
                gates = route(core, s, f["wr"], None, 6, w["tri"])
                jobs = [(lambda c: f["ws1"], lambda c: f["ws2"], lambda c: f["ws3"][:32, :], None, ACT.Silu, 1, None)]
                for e in range(8):
                    jobs.append((lambda c, e=e: f["w1"][:, e * P:(e + 1) * P], lambda c, e=e: f["w2"][:, e * P:(e + 1) * P],
                                 lambda c, e=e: f["w3"][:, e * P:(e + 1) * P], None, ACT.Silu, 1, e))
                feed_forward(core, s, core.x_sb, jobs, gates)

        def fetch_region(what, after=()):
            with nc.Block() as block:
                @block.sync
                def _(sp):
                    for name, value in after:
                        sp.wait_ge(load[name], value)
                    for dst, src, name in what:
                        fetch(sp, dst, src, name)
            core.end_region()

        if 5 in SUBLAYERS:
            fetch_region([(arena2[:, :], d["ffn1"], "ffn1")], [("ffn0", LOADED)])

        if 3 in SUBLAYERS:
            normalise(core, core.x_sb, ident, loads=[(load["toeplitz"], 16 * H), (load["small"], 16)])
            def bias(h, qt):
                at = h * TOEPLITZ + (TB - 1 - qt) * P
                return arena[:, at:at + T]
            small_self("l1", top=(w["flip"], bias, 32), gate=w["head_gates"], bo=row["l1_bo"])


        def fetch_inner():
            fetch_region([(rope_sb[:], d["rope"], "rope"),
                          (arena[:, slot0:slot0 + width(SELF)], d["self0"], "self0"),
                          (arena[:, slot1:slot1 + width(CROSS)], d["cross0"], "cross0"),
                          (arena[:, slot2:slot2 + width(SELF)], d["self1"], "self1")])

        inner = ctx.enter_context(ExitStack())
        rope_sb = inner.enter_context(nc.sbuf_tensor("rope_sb", [P, width(ROPE)], F32))

        def small_context(name, mask=None, stable=False):
            with ExitStack() as s:
                def tb(n, shape):
                    return s.enter_context(nc.sbuf_tensor(f"{n}_{nc.next_id()}", shape, F32))
                q, k, v = tb("q8", [P, B * T]), tb("k8", [P, B * KC]), tb("v8", [P, B, 512])
                keys = tb("keys8", [P, B, H, KC])
                jobs = [(k[:], w[f"{name}_wk"], w["ctx_t"], w[f"{name}_bk"], None, False)]
                for b in range(B):
                    jobs.append((v[:KC, b, :], w["ctx_t"][:, b * KC:(b + 1) * KC], w[f"{name}_wv"], None,
                                 row[f"{name}_bv"], False))
                    jobs.append((q[:, b * T:(b + 1) * T], w[f"{name}_wq"], core.xn_t[:, b * T:(b + 1) * T],
                                 w[f"{name}_bq"], None, False))
                spread_keys(core, [], [v[64:P]])
                project(core, jobs)
                spread_keys(core, [(keys[:, b], wide(k[:, b * KC:(b + 1) * KC], H, 1), wide(w["mask8"], KC, 2))
                                   for b in range(B)], [])
                paired_context_attention(
                    core, s, range(B), lambda b, p, qt: q[:, (b * TB + qt) * P:(b * TB + qt + 1) * P],
                    lambda b, p: keys[:, b, 2 * p:2 * p + 2, :].rearrange("p h k -> p (h k)"),
                    lambda b, h: v[:, b, h * 32:(h + 1) * 32], 8, core.x_sb, ident,
                    lambda g: w[f"{name}_wo"][:, g * C:(g + 1) * C], row[f"{name}_bo"], mask=mask, stable=stable)

        if 7 in SUBLAYERS and 4 not in SUBLAYERS:
            fetch_inner()
        if 4 in SUBLAYERS:
            with ExitStack() as s:
                m01, mneg = context_mask(s, "mask4", 1.0e11)
                if 7 in SUBLAYERS:
                    fetch_inner()
                normalise(core, core.x_sb, ident, loads=[(load["small"], 16)])
                small_context("l1x", mask=(m01, mneg))

        if 5 in SUBLAYERS:
            normalise(core, core.x_sb, ident, loads=[(load["ffn1"], LOADED), (load["small"], 16)])
            with ExitStack() as s:
                f = views(arena2, FFN1)
                gates = route(core, s, w["l1f_wg"], row["l1f_bg"], 2, w["tri"])
                gates_t = s.enter_context(nc.sbuf_tensor("gates_t", [8, NT, P], F32))
                with nc.Block() as block:
                    @block.tensor
                    def _(pe):
                        for t in range(NT):
                            ins = nc.tensor.transpose(core.bank[t // TB][:8, (t % TB) * P:(t % TB + 1) * P],
                                                      gates[:, t, :], ident)
                        ins.then_inc(sig["turn_done"].sem, sig["turn_done"].step())
                        pe.wait_ge(sig["turn_taken"].sem, sig["turn_taken"].at(B))
                        for t in range(NT):
                            ins = nc.tensor.matmul(core.bank[2 + t // TB][:, (t % TB) * P:(t % TB + 1) * P],
                                                   gates_t[:, t, :], w["l1f_b2"][:8, :], start=True, stop=True)
                        ins.then_inc(sig["y_done"].sem, sig["y_done"].step())

                    @block.scalar
                    def _(act):
                        act.wait_ge(sig["turn_done"].sem, sig["turn_done"].at(1))
                        for b in range(B):
                            nc.scalar.activation(
                                gates_t[:, b * TB:(b + 1) * TB, :].rearrange("p t c -> p (t c)"),
                                core.bank[b][:8, :], ACT.Copy).then_inc(sig["turn_taken"].sem, sig["turn_taken"].step())

                    @block.vector
                    def _(dve):
                        dve.wait_ge(sig["y_done"].sem, sig["y_done"].at(1))
                        for b in range(B):
                            half = core.x_sb[:, b * TB:(b + 1) * TB, :].rearrange("p t c -> p (t c)")
                            nc.vector.tensor_tensor(half, half, core.bank[2 + b][:], ALU.add)
                core.end_region()
                jobs = []
                for e in list(range(0, 8, 2)) + list(range(1, 8, 2)):
                    jobs.append((lambda c, e=e: f["up"][:, (e * 4 + c) * P:(e * 4 + c + 1) * P], None,
                                 lambda c, e=e: f["down"][:, (e * 4 + c) * P:(e * 4 + c + 1) * P],
                                 lambda c, e=e: w["l1f_b1"][:, e * 4 + c:e * 4 + c + 1],
                                 ACT.Silu if e % 2 else ACT.Gelu, 4, e))
                feed_forward(core, s, core.x_sb, jobs, gates)

        if 6 in SUBLAYERS:
            normalise(core, core.x_sb, ident, loads=[(load["small"], 16)])
            with ExitStack() as s:
                gated_recurrence(core, s, w["w_hg"], ident)

        with nc.Block() as block:
            @block.sync
            def _(sp):
                sp.wait_ge(load["small"], 16)
                sp.dma_start(small_sb[:, :width(LATE)], d["late"]).then_inc(load["late"], 16)
        core.end_region()

        if 7 in SUBLAYERS:
            with inner:
                r = views(rope_sb, ROPE)
                k_one, q_one = single_heads(core, inner)
                normalise(core, core.x_sb, ident, keep_rows=core.y_sb,
                          loads=[(load["rope"], LOADED)])
                for l in range(2):
                    ws = views(arena, SELF, slot0 if l == 0 else slot2)
                    wc = views(arena, CROSS, slot1)
                    normalise(core, core.y_sb, ident, mean_free=False, weight=w["norm_w"][:, l:l + 1],
                              loads=[(load[f"self{l}"], LOADED)])
                    for b in range(B):
                        with ExitStack() as s:
                            def tb(n, shape):
                                return s.enter_context(nc.sbuf_tensor(f"{n}_{nc.next_id()}", shape, F32))
                            q = arena2[:, 0:8 * T].rearrange("p (s t) -> p s t", s=8)
                            k = arena2[:, 8 * T:16 * T].rearrange("p (s t) -> p s t", s=8)
                            v = tb("v64", [P, TB, 1024])
                            xt = core.xn_t[:, b * T:(b + 1) * T]
                            with ExitStack() as s2:
                                bufs = [s2.enter_context(nc.sbuf_tensor(f"rope_{n}_{nc.next_id()}", [P, m, T], F32))
                                        for n, m in (("raw", 3), ("part", 3), ("swapped", 2))]
                                jobs = []
                                for c in range(8):
                                    jobs.append((q[:, c, :], ws["wq"][:, c * P:(c + 1) * P], xt, None, None, True))
                                    jobs.append((v[:, c // 2, (c % 2) * T:(c % 2 + 1) * T],
                                                 xt[:, (c // 2) * P:(c // 2 + 1) * P],
                                                 ws["wv"][:, (c % 2) * T:(c % 2 + 1) * T], None, None, False))
                                    jobs.append((k[:, c, :], ws["wk"][:, c * P:(c + 1) * P], xt, None, None, True))
                                project(core, jobs, rope=(r["swap"], r["cos"], r["sin"], *bufs))
                            self_attention(
                                core, s, b, lambda h, qt: q[:, h // 2, qt * P:(qt + 1) * P],
                                lambda h: k[:, h // 2, :], lambda h: w["mask64"][:, h % 2:h % 2 + 1],
                                lambda h, c: v[:, c, h * 64:(h + 1) * 64], 64, core.y_sb, ident,
                                lambda g: ws["wo"][:, g * C:(g + 1) * C], row[f"bo{l}"],
                                key_mask=(lambda h: q[:, h // 2, :], key_row[:, b * T:(b + 1) * T], 64 ** -0.5,
                                          k_one, q_one))
                    normalise(core, core.y_sb, ident, mean_free=False, weight=w["norm_w"][:, 2 + l:3 + l],
                              loads=[(load[f"cross{l}"], LOADED)])
                    with ExitStack() as s:
                        def tb(n, shape):
                            return s.enter_context(nc.sbuf_tensor(f"{n}_{nc.next_id()}", shape, F32))
                        q = arena2[:, :8 * B * T].rearrange("p (s t) -> p s t", s=8)
                        k, v, keys = tb("k64", [P, B, 8, KC]), tb("v64", [P, B, 1024]), tb("keys64", [P, B, 8, 2, KC])
                        spread_keys(core, [], [v[64:P]])
                        with ExitStack() as s2:
                            bufs = [s2.enter_context(nc.sbuf_tensor(f"rope_{n}_{nc.next_id()}", [P, m, T], F32))
                                    for n, m in (("raw", 3), ("part", 3), ("swapped", 2))]
                            jobs = []
                            for b in range(B):
                                ct = w["ctx_t"][:, b * KC:(b + 1) * KC]
                                for c in range(8):
                                    jobs.append((k[:, b, c, :], wc["wk"][:, c * P:(c + 1) * P], ct, None, None, True))
                                    jobs.append((q[:, c, b * T:(b + 1) * T], wc["wq"][:, c * P:(c + 1) * P],
                                                 core.xn_t[:, b * T:(b + 1) * T], None, None, True))
                                    if c < 2:
                                        jobs.append((v[:KC, b, c * T:(c + 1) * T], ct, wc["wv"][:, c * T:(c + 1) * T],
                                                     None, None, False))
                            project(core, jobs, rope=(r["swap"], r["cos"], r["sin"], *bufs))
                        spread_keys(core, [(keys[:, b], wide(k[:, b], 2, 2), wide(wide(w["mask64"], 8, 1), KC, 3))
                                           for b in range(B)], [])
                        paired_context_attention(
                            core, s, range(B), lambda b, p, qt: q[:, p, (b * TB + qt) * P:(b * TB + qt + 1) * P],
                            lambda b, p: keys[:, b, p].rearrange("p h k -> p (h k)"),
                            lambda b, h: v[:, b, h * 64:(h + 1) * 64], 64, core.y_sb, ident,
                            lambda g: wc["wo"][:, g * C:(g + 1) * C], row[f"cbo{l}"])
                    normalise(core, core.y_sb, ident, mean_free=False, weight=w["norm_w"][:, 4 + l:5 + l])
                    with ExitStack() as s:
                        feed_forward(core, s, core.y_sb, [(
                            lambda c: wc["fw1"][:, c * P:(c + 1) * P], None, lambda c: wc["fw2"][:, c * P:(c + 1) * P],
                            lambda c: w["ff_b1"][:, 4 * l + c:4 * l + c + 1], ACT.Gelu, 4, None)])
                    add_rows(core, core.y_sb, row[f"fb{l}"])
                    if l == 0:
                        fetch_region([(arena[:, slot1:slot1 + width(CROSS)], d["cross1"], "cross1")])
                normalise(core, core.y_sb, ident, mean_free=False, weight=w["norm_w"][:, 6:7])
                with nc.Block() as block:
                    @block.tensor
                    def _(pe):
                        for t in range(NT):
                            out = core.bank[t // TB][:, (t % TB) * P:(t % TB + 1) * P]
                            nc.tensor.matmul(out, core.xn_t[:, t * P:(t + 1) * P], w["proj_w"], start=True, stop=False)
                            nc.tensor.matmul(out, core.ones_row[0:1, :], row["proj_b"], start=False,
                                             stop=True).then_inc(sig["y_done"].sem, sig["y_done"].step())

                    @block.vector
                    def _(dve):
                        for b in range(B):
                            dve.wait_ge(sig["y_done"].sem, sig["y_done"].at((b + 1) * TB))
                            half = core.x_sb[:, b * TB:(b + 1) * TB, :].rearrange("p t c -> p (t c)")
                            nc.vector.tensor_tensor(half, half, core.bank[b][:], ALU.add)
                core.end_region()

        if 11 in SUBLAYERS:
            fetch_region([(arena2[:, :], d["ffn3"], "ffn3")], [("ffn1" if 5 in SUBLAYERS else "ffn0", LOADED)])
        inner.close()

        if 8 in SUBLAYERS:
            normalise(core, core.x_sb, ident, loads=[(load["late"], 16)])
            with ExitStack() as s:
                bit_feed_forward(core, s, w["bit_w1"], w["bit_w2"], w["bit_b1"], row["bit_b2"], ident, w["ones"])

        if 9 in SUBLAYERS:
            normalise(core, core.x_sb, ident, loads=[(load["late"], 16)])
            with ExitStack() as s:
                state_space(core, s, w)

        if 10 in SUBLAYERS:
            normalise(core, core.x_sb, ident, loads=[(load["late"], 16)])
            small_context("l3x", stable=True)

        if 11 in SUBLAYERS:
            normalise(core, core.x_sb, ident, loads=[(load["ffn3"], LOADED), (load["late"], 16)])
            with ExitStack() as s:
                gates = route(core, s, w["l3f_wg"], None, 2, w["tri"])
                f = views(arena2, FFN3)
                linear_experts(core, s, f["w_in"], f["w_out"], gates)

        with nc.Block() as block:
            @block.sync
            def _(sp):
                sp.dma_start(d["out"], core.x_sb[:]).then_inc(load["out"], 16)
                sp.wait_ge(load["out"], 16)
        core.end_region()



def pack_arrays(pack, arrays):
    out = np.zeros((P, width(pack)), np.float32)
    at = 0
    for name, c in pack:
        a = arrays[name]
        assert a.shape[1] == c, (name, a.shape, c)
        out[:a.shape[0], at:at + c] = a
        at += c
    return out


def heads_of_8(wt, bias):
    wide_w = np.zeros((C, 4, 4, 32), np.float32)
    wide_w[..., :8] = wt.reshape(C, 4, 4, 8)
    wide_b = np.zeros((4, 4, 32), np.float32)
    wide_b[..., :8] = bias.reshape(4, 4, 8)
    return wide_w.reshape(C, 512), wide_b.reshape(4, P).T


def rows_of_8(w):
    tall = np.zeros((4, 4, 32, C), np.float32)
    tall[:, :, :8] = w.reshape(4, 4, 8, C)
    return tall.reshape(4, P, C).transpose(1, 0, 2).reshape(P, 4 * C)


def chunked(a):
    n = a.shape[0] // P
    return a.reshape(n, P, -1).transpose(1, 0, 2).reshape(P, -1)


def kernel(**inputs):
    import concourse.bacc as bacc
    from concourse.bass_utils import run_bass_kernel_spmd

    v = {k: np.asarray(a) for k, a in inputs.items()}
    a = {}
    a["ident"] = np.eye(P, dtype=np.float32)
    a["diagonal"] = np.where(np.tril(np.ones((P, P), bool)), 0.0, NEG).astype(np.float32)
    a["ones"] = np.ones((P, P), np.float32)
    a["mean_col"] = np.full((P, 16), 1.0 / P, np.float32)
    a["tri"] = np.broadcast_to(np.tril(np.ones((8, 8), np.float32), -1).reshape(1, 64), (P, 64))
    a["gamma"] = np.broadcast_to(v["L0_xattn_gamma"], (P, C))
    a["beta"] = np.broadcast_to(v["L0_xattn_beta"], (P, C))
    a["head_gates"] = np.broadcast_to(v["L1_attn_head_gates"], (P, H))
    a["ctx_t"] = v["ctx_1024"].transpose(2, 0, 1).reshape(C, B * KC)
    a["ctx_rows"] = v["ctx_1024"].transpose(1, 0, 2).reshape(KC, B * C)
    a["bit_b1"] = np.broadcast_to(v["L2_ffn_b1"], (P, 512))
    w0, b0 = v["L0_attn_W"], v["L0_attn_b"]
    a["flip"] = np.eye(P, dtype=np.float32)[::-1]
    a["mask8"] = np.kron(np.eye(H), np.ones((8, 1))).astype(np.float32) * np.float32(8 ** -0.5)
    a["mask64"] = np.kron(np.eye(2), np.ones((64, 1))).astype(np.float32) * np.float32(64 ** -0.5)
    a["l0_wq"], a["l0_bq"] = w0[:C].T, b0[:C, None]
    a["l0_wk"], a["l0_bk"] = w0[C:2 * C].T, b0[C:2 * C, None]
    a["l0_wv"], bv = heads_of_8(w0[2 * C:].T, b0[2 * C:])
    a["l0_bv"] = bv.T.reshape(1, 512)
    a["l0_wo"] = rows_of_8(np.eye(C, dtype=np.float32))
    for n, src, turned in (("l1", "L1_attn", True), ("l1x", "L1_xattn", False), ("l3x", "L3_xattn", True)):
        m = {k: v[f"{src}_W{k}"].T if turned else v[f"{src}_W{k}"] for k in "qkvo"}
        a[f"{n}_wq"], a[f"{n}_wk"] = m["q"], m["k"]
        a[f"{n}_bq"], a[f"{n}_bk"] = v[f"{src}_bq"][:, None], v[f"{src}_bk"][:, None]
        a[f"{n}_wv"], bv = heads_of_8(m["v"], v[f"{src}_bv"])
        a[f"{n}_bv"], a[f"{n}_wo"], a[f"{n}_bo"] = bv.T.reshape(1, 512), rows_of_8(m["o"]), v[f"{src}_bo"][None]
    a["l1f_b1"] = v["L1_ffn_b1"].reshape(32, P).T
    a["l1f_b2"], a["l1f_wg"], a["l1f_bg"] = v["L1_ffn_b2"], v["L1_ffn_Wg"], v["L1_ffn_bg"][None]
    a["w_hg"] = v["L2_attn_W_hg"].T
    a["bit_w1"], a["bit_w2"], a["bit_b2"] = v["L2_ffn_w1"].T, chunked(v["L2_ffn_w2"].T), v["L2_ffn_b2"][None]
    a["ss_wd"], a["ss_wb"], a["ss_wc"], a["ss_wo"] = (v[f"L3_attn_W{k}"] for k in "dbco")
    a["ss_a"], a["ss_bo"] = v["L3_attn_A"], v["L3_attn_bo"][None]
    a["ss_bd"], a["ss_bb"], a["ss_bc"] = (v[f"L3_attn_b{k}"][:, None] for k in "dbc")
    x2 = "L2_xattn_"
    a["proj_w"], a["proj_b"] = v[x2 + "proj_w"], v[x2 + "proj_b"][None]
    a["norm_w"] = np.stack([v[x2 + "attn_norm_w"][0], v[x2 + "attn_norm_w"][1], v[x2 + "cross_norm_w"][0],
                            v[x2 + "cross_norm_w"][1], v[x2 + "ff_norm_w"][0], v[x2 + "ff_norm_w"][1],
                            v[x2 + "norm_out_w"]], 1)
    a["ff_b1"] = v[x2 + "ff_b1"].reshape(8, P).T
    for l in range(2):
        a[f"bo{l}"], a[f"cbo{l}"], a[f"fb{l}"] = v[x2 + "bo"][l:l + 1], v[x2 + "cbo"][l:l + 1], v[x2 + "ff_b2"][l:l + 1]
    a["l3f_wg"] = v["L3_ffn_w_gate"].T
    a["ones_row"] = np.ones((1, P), np.float32)

    inv = (1.0 / 10000.0 ** (np.arange(0, 32, 2, dtype=np.float32) / np.float32(32))).astype(np.float32)
    angle = (np.arange(T, dtype=np.float32)[:, None] * inv[None, :]).astype(np.float32)
    cos, sin, swap = np.ones((P, T), np.float32), np.zeros((P, T), np.float32), np.zeros((P, P), np.float32)
    for base in (0, 64):
        cos[base:base + 16] = cos[base + 16:base + 32] = np.cos(angle).T
        sin[base:base + 16], sin[base + 16:base + 32] = -np.sin(angle).T, np.sin(angle).T
        for i in range(16):
            swap[base + 16 + i, base + i] = swap[base + i, base + 16 + i] = 1.0

    packs = {"constants": pack_arrays(CONSTANTS, a), "early": pack_arrays(EARLY, a), "late": pack_arrays(LATE, a),
             "first": pack_arrays(FIRST, a),
             "rows": np.concatenate([a[n] for n, _ in ROWS], 1).astype(np.float32),
             "rope": pack_arrays(ROPE, {"swap": swap, "cos": cos, "sin": sin})}

    def experts(m):
        return m.transpose(1, 0, 2).reshape(m.shape[1], -1)

    packs["ffn0"] = pack_arrays(FFN0, {
        "w1": experts(v["L0_ffn_w1"]), "w2": experts(v["L0_ffn_w2"]), "w3": experts(v["L0_ffn_w3"]),
        "ws1": v["L0_ffn_ws1"], "ws2": v["L0_ffn_ws2"], "ws3": v["L0_ffn_ws3"], "wr": v["L0_ffn_wr"]})
    packs["ffn1"] = pack_arrays(FFN1, {"up": experts(v["L1_ffn_W1"]),
                                       "down": chunked(v["L1_ffn_W2"].reshape(8 * 512, C))})
    packs["ffn3"] = pack_arrays(FFN3, {"w_in": chunked(v["L3_ffn_w_in"].reshape(8 * 512, C)),
                                       "w_out": chunked(v["L3_ffn_w_out"].transpose(0, 2, 1).reshape(8 * 512, C))})
    for l in range(2):
        packs[f"self{l}"] = pack_arrays(SELF, {
            "wq": v[x2 + "Wq"][l], "wk": v[x2 + "Wk"][l], "wv": v[x2 + "Wv"][l], "wo": chunked(v[x2 + "Wo"][l])})
        packs[f"cross{l}"] = pack_arrays(CROSS, {
            "wq": v[x2 + "cWq"][l], "wk": v[x2 + "cWk"][l], "wv": v[x2 + "cWv"][l], "wo": chunked(v[x2 + "cWo"][l]),
            "fw1": v[x2 + "ff_w1"][l], "fw2": chunked(v[x2 + "ff_w2"][l])})

    table = v["L1_attn_rel_bias"]
    at = np.arange(-(T - 1), T) + 63
    at = np.clip(np.where(at < 0, at + table.shape[0], at), 0, table.shape[0] - 1)
    packs["relative"] = np.ascontiguousarray(table[at].T)

    def tokens(m):
        return np.ascontiguousarray(m.reshape(NT, P, -1).transpose(1, 0, 2))

    packs["x"] = tokens(v["x"])
    packs["mask0"] = tokens(v["mask_BxSxS2_ik1"].reshape(B * T, KC))
    packs["mask4"] = tokens(v["mask_Bx1xSxS2_ik1"].reshape(B * T, KC))
    packs["key_mask"] = np.ascontiguousarray(v["mask_BxS_bf1"]).view(np.uint8).reshape(1, B * T)

    nc = bacc.Bacc("TRN2", target_bir_lowering=False, num_devices=1)
    d = {n: nc.dram_tensor(f"in_{n}", m.shape, mybir.dt.from_np(m.dtype), kind="ExternalInput").ap()
         for n, m in packs.items()}
    d["out"] = nc.dram_tensor("out_x", (P, NT, C), F32, kind="ExternalOutput").ap()
    decoder(nc, d)
    r = run_bass_kernel_spmd(nc, [{f"in_{n}": m for n, m in packs.items()}], core_ids=[0])
    got = r.results[0]["out_x"]
    return np.ascontiguousarray(got.transpose(1, 0, 2)).reshape(B, T, C)
```
